# Optimizing a Trainium2 kernel written in Bass

```python
import numpy as np
import jax
import jax.numpy as jnp

def _softmax(x, axis=-1):
    return jax.nn.softmax(x, axis=axis)

def _gelu(x):
    return jax.nn.gelu(x, approximate=True)

def _silu(x):
    return jax.nn.silu(x)

def _sigmoid(x):
    return jax.nn.sigmoid(x)

def _layernorm(x, axis=-1, eps=1e-05):
    m = jnp.mean(x, axis=axis, keepdims=True)
    v = jnp.var(x, axis=axis, keepdims=True)
    return (x - m) / jnp.sqrt(v + eps)

def _scatter_add(tgt, idx, src, axis=0):
    return tgt.at[idx].add(src)

def _segment_sum(src, seg, n):
    return jax.ops.segment_sum(src, seg, n)
kernel_name = 'mk_audio_tower_d2_tok_audfeat256_r4_0ecc2e'

def setup_inputs(seed: int=0):
    np.random.seed(seed)
    _w = jnp.asarray

    def _rec_inputs():
        import jax
        import jax.numpy as jnp
        _rk = jax.random.key(seed)
        x = -9.80646e-05 + 1.00041 * jax.random.normal(jax.random.fold_in(_rk, 1), (8, 4, 750), jnp.float32)
        return x
    x = _rec_inputs()

    def _L0_tok_setup():
        import jax, jax.numpy as jnp
        from jax import lax
        import numpy as np
        NUM_BLOCKS = 9
        KERNEL = 3
        BN_EPS = 1e-05

        def _conv1d(x, w, padding, dilation):
            return lax.conv_general_dilated(x, w, window_strides=(1,), padding=[(padding, padding)], rhs_dilation=(dilation,), dimension_numbers=('NCH', 'OIH', 'NCH'))
        key = jax.random.key(seed)
        ks = jax.random.split(key, 8)
        B, C, L, V = (32, 4, 1024, 64)
        x = jax.random.normal(ks[0], (B, C, L), dtype=jnp.float32)
        conv_w = jax.random.normal(ks[1], (NUM_BLOCKS, C, C, KERNEL), dtype=jnp.float32) * 0.3
        conv_b = jax.random.normal(ks[2], (NUM_BLOCKS, C), dtype=jnp.float32) * 0.1
        bn_gamma = jnp.ones((NUM_BLOCKS, C), dtype=jnp.float32)
        bn_beta = jnp.zeros((NUM_BLOCKS, C), dtype=jnp.float32)
        bn_mean = jax.random.normal(ks[3], (NUM_BLOCKS, C), dtype=jnp.float32) * 0.1
        bn_var = jax.random.uniform(ks[4], (NUM_BLOCKS, C), dtype=jnp.float32, minval=0.5, maxval=1.5)
        out_w = jax.random.normal(ks[5], (V, C, 1), dtype=jnp.float32) * 0.3
        out_b = jax.random.normal(ks[6], (V,), dtype=jnp.float32) * 0.1
        return {'x': x, 'conv_w': conv_w, 'conv_b': conv_b, 'bn_gamma': bn_gamma, 'bn_beta': bn_beta, 'bn_mean': bn_mean, 'bn_var': bn_var, 'out_w': out_w, 'out_b': out_b}
    _L0_tok_all = _L0_tok_setup()
    _L0_tok_in = {k: v for k, v in _L0_tok_all.items() if k in ('conv_w', 'conv_b', 'bn_gamma', 'bn_beta', 'bn_mean', 'bn_var', 'out_w', 'out_b')}
    del _L0_tok_all

    def _L0_attn_setup():
        import jax, jax.numpy as jnp
        import numpy as np
        from math import sqrt
        DIM = 64
        key = jax.random.key(seed)
        k1, k2, k3, k4 = jax.random.split(key, 4)
        B, T, D, H, R = (2, 1024, DIM, 8, 32)

        def xavier(k, shape, fan_in, fan_out):
            a = sqrt(6.0 / (fan_in + fan_out))
            return jax.random.uniform(k, shape, jnp.float32, -a, a)
        x = jax.random.normal(k1, (B, T, D), jnp.float32)
        Q = xavier(k2, (H, R, D), D, R)
        K = xavier(k3, (H, R, D), D, R)
        VO = xavier(k4, (H, D, D), D, D)
        return {'x': x, 'Q': Q, 'K': K, 'VO': VO}
    _L0_attn_all = _L0_attn_setup()
    _L0_attn_in = {k: v for k, v in _L0_attn_all.items() if k in ('Q', 'K', 'VO')}
    del _L0_attn_all

    def _L0_ffn_setup():
        import math
        import jax, jax.numpy as jnp
        import numpy as np
        CAPACITY_FACTOR = 1.25
        key = jax.random.key(seed)
        ks = jax.random.split(key, 5)
        B, L, D, F, E = (8, 2048, 64, 256, 8)
        h = jax.random.normal(ks[0], (B, L, D), dtype=jnp.float32)
        gate_w = jax.random.normal(ks[1], (D, E), dtype=jnp.float32) * 0.02
        gate_b = jnp.zeros((E,), dtype=jnp.float32)
        w1 = jax.random.normal(ks[2], (E, D, F), dtype=jnp.float32) * (1.0 / math.sqrt(D))
        b1 = jnp.zeros((E, F), dtype=jnp.float32)
        w2 = jax.random.normal(ks[3], (E, F, D), dtype=jnp.float32) * (1.0 / math.sqrt(F))
        b2 = jnp.zeros((E, D), dtype=jnp.float32)
        return {'h': h, 'gate_w': gate_w, 'gate_b': gate_b, 'w1': w1, 'b1': b1, 'w2': w2, 'b2': b2}
    _L0_ffn_all = _L0_ffn_setup()
    _L0_ffn_in = {k: v for k, v in _L0_ffn_all.items() if k in ('gate_w', 'gate_b', 'w1', 'b1', 'w2', 'b2')}
    del _L0_ffn_all

    def _L1_attn_setup():
        import jax, jax.numpy as jnp
        import numpy as np
        PI = np.pi
        key = jax.random.key(seed)
        ks = jax.random.split(key, 24)
        B, L, D, P, H, MAXL = (1, 512, 64, 32, 4, 4096)
        Dh = D // 2
        n = lambda k, s, sc=0.02: (jax.random.normal(k, s) * sc).astype(jnp.float32)
        z = lambda s: jnp.zeros(s, jnp.float32)
        return {'x': n(ks[0], (B, L, D), 1.0), 'pos_phases': n(ks[1], (MAXL, P), PI), 'window_deltas': jnp.arange(-2, 3, dtype=jnp.float32), 'mc_w': n(ks[2], (D, D)), 'mc_b': z((D,)), 'hop_w1': n(ks[3], (D + P, D)), 'hop_b1': z((D,)), 'hop_w2': n(ks[4], (D, H * (P + 1))), 'hop_b2': z((H * (P + 1),)), 'cpe_w': n(ks[5], (D, P)), 'cpe_b': z((P,)), 've_w': n(ks[6], (D, D)), 've_b': z((D,)), 'kce_w': n(ks[7], (D, D)), 'kce_b': z((D,)), 'ksk_w1': n(ks[8], (2 * D, D)), 'ksk_b1': z((D,)), 'ksk_w2': n(ks[9], (D, P)), 'ksk_b2': z((P,)), 'sg_w1': n(ks[10], (D, Dh)), 'sg_b1': z((Dh,)), 'sg_w2': n(ks[11], (Dh, 1)), 'sg_b2': z((1,)), 'ln_g': jnp.ones((D,), jnp.float32), 'ln_b': z((D,)), 'out_w': n(ks[12], (D, D)), 'out_b': z((D,))}
    _L1_attn_all = _L1_attn_setup()
    _L1_attn_in = {k: v for k, v in _L1_attn_all.items() if k in ('pos_phases', 'window_deltas', 'mc_w', 'mc_b', 'hop_w1', 'hop_b1', 'hop_w2', 'hop_b2', 'cpe_w', 'cpe_b', 've_w', 've_b', 'kce_w', 'kce_b', 'ksk_w1', 'ksk_b1', 'ksk_w2', 'ksk_b2', 'sg_w1', 'sg_b1', 'sg_w2', 'sg_b2', 'ln_g', 'ln_b', 'out_w', 'out_b')}
    del _L1_attn_all

    def _L1_ffn_setup():
        import jax, jax.numpy as jnp
        import numpy as np
        E, D, H, TOP_K = (6, 64, 64, 2)
        ROUTER_H = D // 2
        key = jax.random.key(seed)
        ks = jax.random.split(key, 12)
        s = 1.0 / np.sqrt(D)
        sh = 1.0 / np.sqrt(H)
        sr = 1.0 / np.sqrt(ROUTER_H)
        return {'features': jax.random.normal(ks[0], (8, 1024, D), dtype=jnp.float32), 'router_w1': jax.random.uniform(ks[1], (D, ROUTER_H), jnp.float32, -s, s), 'router_b1': jnp.zeros((ROUTER_H,), jnp.float32), 'router_w2': jax.random.uniform(ks[2], (ROUTER_H, E), jnp.float32, -sr, sr), 'router_b2': jnp.zeros((E,), jnp.float32), 'expert_w1': jax.random.uniform(ks[3], (E, D, H), jnp.float32, -s, s), 'expert_b1': jnp.zeros((E, H), jnp.float32), 'expert_w2': jax.random.uniform(ks[4], (E, H, H), jnp.float32, -sh, sh), 'expert_b2': jnp.zeros((E, H), jnp.float32), 'expert_w3': jax.random.uniform(ks[5], (E, H, D), jnp.float32, -sh, sh), 'expert_b3': jnp.zeros((E, D), jnp.float32)}
    _L1_ffn_all = _L1_ffn_setup()
    _L1_ffn_in = {k: v for k, v in _L1_ffn_all.items() if k in ('router_w1', 'router_b1', 'router_w2', 'router_b2', 'expert_w1', 'expert_b1', 'expert_w2', 'expert_b2', 'expert_w3', 'expert_b3')}
    del _L1_ffn_all
    return {'x': x, 'L0_tok_conv_w': _L0_tok_in['conv_w'], 'L0_tok_conv_b': _L0_tok_in['conv_b'], 'L0_tok_bn_gamma': _L0_tok_in['bn_gamma'], 'L0_tok_bn_beta': _L0_tok_in['bn_beta'], 'L0_tok_bn_mean': _L0_tok_in['bn_mean'], 'L0_tok_bn_var': _L0_tok_in['bn_var'], 'L0_tok_out_w': _L0_tok_in['out_w'], 'L0_tok_out_b': _L0_tok_in['out_b'], 'L0_attn_Q': _L0_attn_in['Q'], 'L0_attn_K': _L0_attn_in['K'], 'L0_attn_VO': _L0_attn_in['VO'], 'L0_ffn_gate_w': _L0_ffn_in['gate_w'], 'L0_ffn_gate_b': _L0_ffn_in['gate_b'], 'L0_ffn_w1': _L0_ffn_in['w1'], 'L0_ffn_b1': _L0_ffn_in['b1'], 'L0_ffn_w2': _L0_ffn_in['w2'], 'L0_ffn_b2': _L0_ffn_in['b2'], 'L1_attn_pos_phases': _L1_attn_in['pos_phases'], 'L1_attn_window_deltas': _L1_attn_in['window_deltas'], 'L1_attn_mc_w': _L1_attn_in['mc_w'], 'L1_attn_mc_b': _L1_attn_in['mc_b'], 'L1_attn_hop_w1': _L1_attn_in['hop_w1'], 'L1_attn_hop_b1': _L1_attn_in['hop_b1'], 'L1_attn_hop_w2': _L1_attn_in['hop_w2'], 'L1_attn_hop_b2': _L1_attn_in['hop_b2'], 'L1_attn_cpe_w': _L1_attn_in['cpe_w'], 'L1_attn_cpe_b': _L1_attn_in['cpe_b'], 'L1_attn_ve_w': _L1_attn_in['ve_w'], 'L1_attn_ve_b': _L1_attn_in['ve_b'], 'L1_attn_kce_w': _L1_attn_in['kce_w'], 'L1_attn_kce_b': _L1_attn_in['kce_b'], 'L1_attn_ksk_w1': _L1_attn_in['ksk_w1'], 'L1_attn_ksk_b1': _L1_attn_in['ksk_b1'], 'L1_attn_ksk_w2': _L1_attn_in['ksk_w2'], 'L1_attn_ksk_b2': _L1_attn_in['ksk_b2'], 'L1_attn_sg_w1': _L1_attn_in['sg_w1'], 'L1_attn_sg_b1': _L1_attn_in['sg_b1'], 'L1_attn_sg_w2': _L1_attn_in['sg_w2'], 'L1_attn_sg_b2': _L1_attn_in['sg_b2'], 'L1_attn_ln_g': _L1_attn_in['ln_g'], 'L1_attn_ln_b': _L1_attn_in['ln_b'], 'L1_attn_out_w': _L1_attn_in['out_w'], 'L1_attn_out_b': _L1_attn_in['out_b'], 'L1_ffn_router_w1': _L1_ffn_in['router_w1'], 'L1_ffn_router_b1': _L1_ffn_in['router_b1'], 'L1_ffn_router_w2': _L1_ffn_in['router_w2'], 'L1_ffn_router_b2': _L1_ffn_in['router_b2'], 'L1_ffn_expert_w1': _L1_ffn_in['expert_w1'], 'L1_ffn_expert_b1': _L1_ffn_in['expert_b1'], 'L1_ffn_expert_w2': _L1_ffn_in['expert_w2'], 'L1_ffn_expert_b2': _L1_ffn_in['expert_b2'], 'L1_ffn_expert_w3': _L1_ffn_in['expert_w3'], 'L1_ffn_expert_b3': _L1_ffn_in['expert_b3']}

def reference(x, L0_tok_conv_w, L0_tok_conv_b, L0_tok_bn_gamma, L0_tok_bn_beta, L0_tok_bn_mean, L0_tok_bn_var, L0_tok_out_w, L0_tok_out_b, L0_attn_Q, L0_attn_K, L0_attn_VO, L0_ffn_gate_w, L0_ffn_gate_b, L0_ffn_w1, L0_ffn_b1, L0_ffn_w2, L0_ffn_b2, L1_attn_pos_phases, L1_attn_window_deltas, L1_attn_mc_w, L1_attn_mc_b, L1_attn_hop_w1, L1_attn_hop_b1, L1_attn_hop_w2, L1_attn_hop_b2, L1_attn_cpe_w, L1_attn_cpe_b, L1_attn_ve_w, L1_attn_ve_b, L1_attn_kce_w, L1_attn_kce_b, L1_attn_ksk_w1, L1_attn_ksk_b1, L1_attn_ksk_w2, L1_attn_ksk_b2, L1_attn_sg_w1, L1_attn_sg_b1, L1_attn_sg_w2, L1_attn_sg_b2, L1_attn_ln_g, L1_attn_ln_b, L1_attn_out_w, L1_attn_out_b, L1_ffn_router_w1, L1_ffn_router_b1, L1_ffn_router_w2, L1_ffn_router_b2, L1_ffn_expert_w1, L1_ffn_expert_b1, L1_ffn_expert_w2, L1_ffn_expert_b2, L1_ffn_expert_w3, L1_ffn_expert_b3):
    import jax
    import jax.numpy as jnp

    def _L0_tok_ref(x, conv_w, conv_b, bn_gamma, bn_beta, bn_mean, bn_var, out_w, out_b):
        import jax, jax.numpy as jnp
        from jax import lax
        import numpy as np
        NUM_BLOCKS = 9
        KERNEL = 3
        BN_EPS = 1e-05

        def _conv1d(x, w, padding, dilation):
            return lax.conv_general_dilated(x, w, window_strides=(1,), padding=[(padding, padding)], rhs_dilation=(dilation,), dimension_numbers=('NCH', 'OIH', 'NCH'))
        L = x.shape[-1]
        for i in range(NUM_BLOCKS):
            dilation = 2 ** i
            pad = (KERNEL - 1) * dilation
            residual = x
            h = _conv1d(x, conv_w[i], pad, dilation) + conv_b[i][None, :, None]
            h = jax.nn.relu(h)
            scale = bn_gamma[i] * lax.rsqrt(bn_var[i] + BN_EPS)
            h = h * scale[None, :, None] + (bn_beta[i] - bn_mean[i] * scale)[None, :, None]
            h = h[:, :, :L]
            x = residual + h
        y = _conv1d(x, out_w, 0, 1) + out_b[None, :, None]
        return jnp.transpose(y, (0, 2, 1))

    def _L0_attn_ref(x, Q, K, VO):
        import jax, jax.numpy as jnp
        import numpy as np
        from math import sqrt
        DIM = 64
        d = x.shape[-1]
        q = jnp.einsum('btd,hrd->bhtr', x, Q)
        k = jnp.einsum('bud,hrd->bhur', x, K)
        scores = jnp.einsum('bhtr,bhur->bhtu', q, k) / sqrt(d)
        attn = jax.nn.softmax(scores, axis=-1)
        ctx = jnp.einsum('bhtu,bud->bhtd', attn, x)
        out = jnp.einsum('bhtd,hde->bte', ctx, VO)
        return out

    def _L0_ffn_ref(h, gate_w, gate_b, w1, b1, w2, b2):
        import math
        import jax, jax.numpy as jnp
        import numpy as np
        CAPACITY_FACTOR = 1.25
        B, L, D = h.shape
        E = gate_w.shape[1]
        T = B * L
        C = max(1, math.ceil(CAPACITY_FACTOR * T / E))
        x = h.reshape(T, D)
        logits = x @ gate_w + gate_b
        probs = jax.nn.softmax(logits, axis=-1)
        idx = jnp.argmax(probs, axis=-1)
        prb = jnp.take_along_axis(probs, idx[:, None], axis=1)[:, 0]
        one_hot = jax.nn.one_hot(idx, E, dtype=jnp.float32)
        pos = (jnp.cumsum(one_hot, axis=0) * one_hot).sum(-1).astype(jnp.int32) - 1
        kept = pos < C
        pos_safe = jnp.where(kept, pos, C)
        buf = jnp.zeros((E, C, D), dtype=h.dtype).at[idx, pos_safe].set(x, mode='drop')
        hmid = jax.nn.relu(jnp.einsum('ecd,edf->ecf', buf, w1) + b1[:, None, :])
        ybuf = jnp.einsum('ecf,efd->ecd', hmid, w2) + b2[:, None, :]
        pos_g = jnp.minimum(pos, C - 1)
        y_tok = ybuf[idx, pos_g] * (prb * kept)[:, None]
        y = y_tok.reshape(B, L, D)
        y = jnp.nan_to_num(y, nan=0.0, posinf=10000.0, neginf=-10000.0)
        return y

    def _L1_attn_ref(x, pos_phases, window_deltas, mc_w, mc_b, hop_w1, hop_b1, hop_w2, hop_b2, cpe_w, cpe_b, ve_w, ve_b, kce_w, kce_b, ksk_w1, ksk_b1, ksk_w2, ksk_b2, sg_w1, sg_b1, sg_w2, sg_b2, ln_g, ln_b, out_w, out_b):
        import jax, jax.numpy as jnp
        import numpy as np
        PI = np.pi
        B, L, D = x.shape
        P = cpe_w.shape[1]
        H = hop_b2.shape[0] // (P + 1)
        gelu = lambda t: jax.nn.gelu(t, approximate=False)
        sqrtP = jnp.sqrt(jnp.float32(P))
        pp = pos_phases[:L]
        pos_cos, pos_sin = (jnp.cos(pp), jnp.sin(pp))
        content = x @ mc_w + mc_b
        mem1_cos = jnp.cumsum(pos_cos[None, :, :, None] * content[:, :, None, :], axis=1)
        mem1_sin = jnp.cumsum(pos_sin[None, :, :, None] * content[:, :, None, :], axis=1)
        off_in = jnp.concatenate([x, jnp.broadcast_to(pp[None], (B, L, P))], axis=-1)
        ao = (gelu(off_in @ hop_w1 + hop_b1) @ hop_w2 + hop_b2).reshape(B, L, H, P + 1)
        center = jnp.tanh(ao[..., :P]) * PI
        width = jax.nn.sigmoid(ao[..., -1:]) * 2 + 0.1
        Wn = window_deltas.shape[0]
        deltas = window_deltas.reshape(1, 1, 1, Wn)
        weights = jnp.exp(-0.5 * deltas ** 2 / (width ** 2 + 1e-06))
        off_ph = center[:, :, :, None, :] + deltas[..., None] * 0.1
        oc, os_ = (jnp.cos(off_ph), jnp.sin(off_ph))
        pce = pos_cos.reshape(1, L, 1, 1, P)
        pse = pos_sin.reshape(1, L, 1, 1, P)
        qc = (pce * oc - pse * os_).reshape(B, L, H * Wn, P)
        qs = (pse * oc + pce * os_).reshape(B, L, H * Wn, P)
        retrieved = (jnp.einsum('blpd,blhp->blhd', mem1_cos, qc) + jnp.einsum('blpd,blhp->blhd', mem1_sin, qs)) / sqrtP
        retrieved = retrieved.reshape(B, L, H, Wn, D)
        ws = (retrieved * weights[..., None]).sum(axis=3)
        head_out = ws / (weights.sum(axis=3, keepdims=True) + 1e-06)
        mh_out = head_out.mean(axis=2)
        key_ph = jnp.tanh(x @ cpe_w + cpe_b) * PI
        key_cos, key_sin = (jnp.cos(key_ph), jnp.sin(key_ph))
        values = x @ ve_w + ve_b
        gate = jax.nn.sigmoid(gelu(x @ sg_w1 + sg_b1) @ sg_w2 + sg_b2)
        ctx = jnp.cumsum(x @ kce_w + kce_b, axis=1)
        pos = jnp.arange(1, L + 1, dtype=x.dtype).reshape(1, L, 1)
        storage_in = jnp.concatenate([x, ctx / pos], axis=-1)
        st_ph = jnp.tanh(gelu(storage_in @ ksk_w1 + ksk_b1) @ ksk_w2 + ksk_b2) * PI
        sc, ss = (jnp.cos(st_ph), jnp.sin(st_ph))
        gv = values[:, :, None, :] * gate[..., None]
        kv_cos = jnp.cumsum(sc[..., None] * gv, axis=1)
        kv_sin = jnp.cumsum(ss[..., None] * gv, axis=1)
        gate_cum = jnp.clip(jnp.cumsum(gate, axis=1), 1.0, None)
        kv_ret = (kv_cos * key_cos[..., None] + kv_sin * key_sin[..., None]).sum(axis=2)
        kv_ret = kv_ret / (jnp.sqrt(gate_cum) * sqrtP)
        combined = mh_out + kv_ret
        mu = combined.mean(-1, keepdims=True)
        var = combined.var(-1, keepdims=True)
        lnx = (combined - mu) / jnp.sqrt(var + 1e-05) * ln_g + ln_b
        return x + (lnx @ out_w + out_b)

    def _L1_ffn_ref(features, router_w1, router_b1, router_w2, router_b2, expert_w1, expert_b1, expert_w2, expert_b2, expert_w3, expert_b3):
        import jax, jax.numpy as jnp
        import numpy as np
        E, D, H, TOP_K = (6, 64, 64, 2)
        ROUTER_H = D // 2
        rh = jax.nn.relu(features @ router_w1 + router_b1)
        expert_logits = jax.nn.softmax(rh @ router_w2 + router_b2, axis=-1)
        top_w, top_i = jax.lax.top_k(expert_logits, TOP_K)
        routing_weights = jax.nn.softmax(top_w, axis=-1)
        h1 = jax.nn.relu(jnp.einsum('bsd,edh->bseh', features, expert_w1) + expert_b1)
        h2 = jax.nn.relu(jnp.einsum('bseh,ehf->bsef', h1, expert_w2) + expert_b2)
        expert_out = jnp.einsum('bsef,efo->bseo', h2, expert_w3) + expert_b3
        sel = jnp.take_along_axis(expert_out, top_i[:, :, :, None], axis=2)
        combined = jnp.sum(sel * routing_weights[..., None], axis=2)
        return combined
    h = _L0_tok_ref(x, L0_tok_conv_w, L0_tok_conv_b, L0_tok_bn_gamma, L0_tok_bn_beta, L0_tok_bn_mean, L0_tok_bn_var, L0_tok_out_w, L0_tok_out_b)
    h = h + _L0_attn_ref(_layernorm(h, axis=-1), L0_attn_Q, L0_attn_K, L0_attn_VO)
    h = h + _L0_ffn_ref(_layernorm(h, axis=-1), L0_ffn_gate_w, L0_ffn_gate_b, L0_ffn_w1, L0_ffn_b1, L0_ffn_w2, L0_ffn_b2)
    h = h + _L1_attn_ref(_layernorm(h, axis=-1), L1_attn_pos_phases, L1_attn_window_deltas, L1_attn_mc_w, L1_attn_mc_b, L1_attn_hop_w1, L1_attn_hop_b1, L1_attn_hop_w2, L1_attn_hop_b2, L1_attn_cpe_w, L1_attn_cpe_b, L1_attn_ve_w, L1_attn_ve_b, L1_attn_kce_w, L1_attn_kce_b, L1_attn_ksk_w1, L1_attn_ksk_b1, L1_attn_ksk_w2, L1_attn_ksk_b2, L1_attn_sg_w1, L1_attn_sg_b1, L1_attn_sg_w2, L1_attn_sg_b2, L1_attn_ln_g, L1_attn_ln_b, L1_attn_out_w, L1_attn_out_b)
    h = h + _L1_ffn_ref(_layernorm(h, axis=-1), L1_ffn_router_w1, L1_ffn_router_b1, L1_ffn_router_w2, L1_ffn_router_b2, L1_ffn_expert_w1, L1_ffn_expert_b1, L1_ffn_expert_w2, L1_ffn_expert_b2, L1_ffn_expert_w3, L1_ffn_expert_b3)
    return h

_drawn_inputs = setup_inputs


def setup_inputs(seed=0):
    import zlib

    import numpy as np

    out = dict(_drawn_inputs(seed))
    spreads = {'L0_tok_bn_gamma': (1.0, 0.2),
     'L0_tok_bn_beta': (0.0, 0.1),
     'L0_ffn_gate_b': (0.0, 0.8),
     'L0_ffn_b1': (0.0, 0.8),
     'L0_ffn_b2': (0.0, 0.8),
     'L1_attn_mc_b': (0.0, 0.8),
     'L1_attn_hop_b1': (0.0, 0.8),
     'L1_attn_hop_b2': (0.0, 0.8),
     'L1_attn_cpe_b': (0.0, 0.8),
     'L1_attn_ve_b': (0.0, 0.8),
     'L1_attn_kce_b': (0.0, 0.8),
     'L1_attn_ksk_b1': (0.0, 0.8),
     'L1_attn_ksk_b2': (0.0, 0.8),
     'L1_attn_sg_b1': (0.0, 0.8),
     'L1_attn_ln_g': (1.0, 0.6),
     'L1_attn_ln_b': (0.0, 0.8),
     'L1_attn_out_b': (0.0, 0.8),
     'L1_ffn_router_b1': (0.0, 0.8),
     'L1_ffn_router_b2': (0.0, 0.8),
     'L1_ffn_expert_b1': (0.0, 0.8),
     'L1_ffn_expert_b2': (0.0, 0.8),
     'L1_ffn_expert_b3': (0.0, 2.0)}
    factors = {'L0_tok_conv_b': 2.815,
     'L0_tok_out_b': 8.0,
     'L0_attn_Q': 7.071,
     'L0_attn_K': 5.571,
     'L0_ffn_gate_w': 8.0,
     'L0_ffn_w1': 8.0,
     'L0_ffn_w2': 8.0,
     'L1_attn_pos_phases': 8.0,
     'L1_attn_window_deltas': 64.0,
     'L1_attn_mc_w': 8.0,
     'L1_attn_hop_w1': 8.0,
     'L1_attn_hop_w2': 8.0,
     'L1_attn_cpe_w': 8.0,
     'L1_attn_ve_w': 7.881,
     'L1_attn_kce_w': 8.0,
     'L1_attn_ksk_w1': 8.0,
     'L1_attn_ksk_w2': 8.0,
     'L1_attn_sg_w1': 24.65,
     'L1_attn_sg_w2': 33.17,
     'L1_attn_out_w': 6.161,
     'L1_ffn_router_w1': 8.0,
     'L1_ffn_router_w2': 8.0,
     'L1_ffn_expert_w1': 8.0,
     'L1_ffn_expert_w2': 8.0,
     'L1_ffn_expert_w3': 8.0}
    for name, (base, spread) in spreads.items():
        noise = np.random.default_rng([zlib.crc32(name.encode()), seed]).standard_normal(out[name].shape)
        drawn = base * np.exp(spread * noise) if base else spread * noise
        out[name] = jnp.asarray(drawn.astype(out[name].dtype))
    for name, factor in factors.items():
        out[name] = (out[name] * factor).astype(out[name].dtype)
    return out
```

```python
from contextlib import ExitStack

import concourse.bass as bass
import numpy as np
from concourse import mybir

F32 = mybir.dt.float32
BF16 = mybir.dt.bfloat16
U32 = mybir.dt.uint32
ALU = mybir.AluOpType
ACT = mybir.ActivationFunctionType
AX = mybir.AxisListType.X

B, CIN, L, D = 8, 4, 750, 64
NP, NJ, R = 4, 6, 125
NT, NG = NP * NJ, NP * NJ * 2
HALF = L // 2
NB, KT = 9, 3
NS, SEG = 3, 250
HEADS, QR = 8, 32
E0, F0 = 8, 256
CAP = -(-(5 * B * L) // (4 * E0))
CH = CAP // 2
ROWS = 1000
PH, PP, WN = 4, 32, 5
E1 = 6
EPS = 1e-5
PI_IN = 3.1415925
PI = float(np.float32(np.pi))
MAGIC = 12582912.0
C1 = 6.28125
C2 = 0.0019350051879882812
C3 = 2 * np.pi - C1 - C2
RS = 1.0 / np.sqrt(float(PP))

GB, CVB, KSB, GTB, AOB, LNG, LNB, OB, RB2, EB3, WD = (
    0, 8, 264, 392, 394, 658, 722, 786, 850, 856, 1240)
NBIAS = 1245


def build(nc, t, out):
    with ExitStack() as ctx:
        ctx.enter_context(nc.allow_non_contiguous_dma(reason="small weights are laid out on their way in"))
        def sb(name, shape, dt=F32):
            return ctx.enter_context(nc.sbuf_tensor(name, shape, dt))[tuple(slice(None) for _ in shape)]

        psum = ctx.enter_context(nc.psum_tensor("psum", [128, 8, 512], F32))
        bank = [psum[:, i, :] for i in range(8)]
        xbuf = nc.dram_tensor("expert_in", [E0 * ROWS, D], F32, kind="Internal").ap()
        ybuf = nc.dram_tensor("expert_out", [E0 * ROWS, D], F32, kind="Internal").ap()

        H = sb("H", [R, NP, NJ, 2, D])
        XN = sb("XN", [R, NP, NJ, 2, D])
        XT = sb("XT", [128, NP * L])
        ident = sb("ident", [128, 128])
        identb = sb("identb", [128, 128], BF16)
        triu = sb("triu", [128, 128])
        ones = sb("ones", [128, 128])
        mhalf = sb("mhalf", [128, 64])
        zero1 = sb("zero1", [128, 1])
        lnst = sb("lnst", [R, 4, NP, 2 * NJ])
        bias = sb("bias", [128, NBIAS])
        iota8 = sb("iota8", [R, 8])
        trig = sb("trig", [R, 2, NJ * PP + WN])
        halfpi = sb("halfpi", [128, 1])

        WCOLS = [("gw", 16), ("hop1", 128), ("hop2", 264), ("wta", 320), ("ksk1", 128), ("ksm", 128), ("sg1", 64), ("ksk2", 64), ("sg2", 2), ("outw", 128),
                 ("rw1", 64), ("rw2", 12), ("b1", 16), ("b2", 4), ("e1b", 3), ("e2b", 3), ("kb", 1), ("sgb1", 1),
                 ("hopb", 1), ("rb1", 1)]
        wall = sb("wall", [128, sum(n for _, n in WCOLS)])
        W, at = {}, 0
        for name, n in WCOLS:
            W[name] = wall[:, at:at + n]
            at += n
        qkp = sb("qkp", [128, 2, 2, HEADS * QR])
        vox = sb("vox", [128, 4, 130])
        slot_in = sb("slot_in", [R, NG], U32)
        slot_out = sb("slot_out", [R, NG], U32)
        prob = sb("prob", [R, NG])
        pk = sb("pk", [R, NG])

        ASIZE = 37660
        arena = sb("arena", [128, ASIZE])

        def view(at, shape, dt=F32, parts=128):
            n = int(np.prod(shape))
            w = n if dt != BF16 else (n + 1) // 2
            assert at + w <= ASIZE, (at, shape)
            v = arena[0:parts, at:at + w]
            if dt != F32:
                v = v.bitcast(dt)
            if len(shape) > 1:
                dims = [f"d{i}" for i in range(len(shape))]
                v = v.rearrange(f"p ({' '.join(dims)}) -> p {' '.join(dims)}", **dict(zip(dims[1:], shape[1:])))
            return v, at + w

        Fw, at = view(0, [NB * KT, 160], parts=96)
        Wout, at = view(at, [NS * B, D], parts=96)
        P4, at = view(at, [256], parts=4)
        W96, at = view(at, [256], parts=96)
        xc, at = view(at, [SEG], parts=96)
        xs, at = view(at, [SEG], parts=96)
        xr, at = view(at, [SEG], parts=96)
        bmask, at = view(at, [B], parts=96)
        m24, at = view(at, [NS * B], parts=96)
        R4, at = view(at, [96], parts=4)
        bn, at = view(at, [3, NB], parts=96)
        ppt, at = view(at, [NJ * R], parts=PP)
        outb, at = view(at, [D], parts=R)
        phases, at = view(at, [NJ * PP + WN], parts=R)
        ppx, at = view(at, [NJ, PP], parts=R)
        qload, at = view(at, [2, 2, 192])
        voload, at = view(at, [2, 4, D])
        early = [("hop1b", 128), ("kskb", 128), ("kcet", 128), ("kce", 64), ("kb1", 1), ("kceb", 1)]
        wearly, at = view(at, [sum(n for _, n in early)])
        col = 0
        for name, n in early:
            W[name] = wearly[:, col:col + n]
            col += n
        zeros = XN[:, 0].rearrange("r j a d -> r (j a d)")[:, 0:512]
        PAR, OW = NB * CIN * KT, NB * CIN * KT + 5 * NB
        SQ, at_sq = view(ASIZE - 2 * 768, [2, 768], parts=R)
        assert at <= ASIZE - 2 * 768
        PPF = sb("PPF", [128, L])

        QA, at = view(0, [2, HEADS, L], BF16)
        QB, at = view(at, [2, HEADS, L], BF16)
        KA, at = view(at, [2, HEADS, L], BF16)
        KB, at = view(at, [2, HEADS, L], BF16)
        SP, at = view(at, [2, 3, L], BF16)
        RR, at = view(at, [2, HALF])
        CT, at = view(at, [2, 4, L])
        PR, at = view(at, [4, L], parts=R)
        MX, at = view(at, [2, 24], parts=R)
        M1, at = view(at, [2, 12], parts=R)
        MR, at = view(at, [2, 12], parts=R)
        NM, at = view(at, [2, 36], BF16, parts=R)
        MT, at = view(at, [2, 126], BF16, parts=36)
        RD, at = view(at, [2, 4], parts=R)
        OT, at = view(at, [8, D], parts=R)
        OR, at = view(at, [D], parts=R)
        XSQ, at = view(at, [NJ, D], parts=R)
        lnb, at = view(at, [4, NJ], parts=R)
        LG, at = view(at, [NJ, E0], parts=R)
        LD, at = view(at, [NJ, E0], parts=R)
        EQ, at = view(at, [NJ, E0], parts=R)
        OH, at = view(at, [NJ, E0], parts=R)
        SO, at = view(at, [NJ + 1, E0], parts=R)
        PX, at = view(at, [NJ, E0], parts=R)
        r1, at = view(at, [9, NJ], parts=R)

        w1p, at = view(0, [E0, F0])
        w2e, at = view(at, [E0, 2, D])
        XB, at = view(at, [4, 8, 128], parts=R)
        XBT, at = view(at, [4, ROWS])
        HM, at = view(at, [2, 2, 2, CAP])
        YT, at = view(at, [4, ROWS])
        YG, at = view(at, [NG, D], parts=R)
        big, at = view(at, [2, 768], parts=R)
        msk, at = view(at, [2, 768], parts=R)
        mski = [msk[:, i, :].bitcast(U32) for i in range(2)]
        assert at <= ASIZE - 2 * 768

        HG, at = view(0, [NP * L])
        KG, at = view(at, [NP * L])
        SG, at = view(at, [NP * L])
        CX, at = view(at, [NP * L])
        CV, at = view(at, [NT, 2, 2, D], parts=R)
        TC, at = view(at, [NG, PH, PP], parts=R)
        TK, at = view(at, [NT, 2, 2, PP], parts=R)
        SC, _ = view(0, [NG, PH, PP], parts=R)
        SK, _ = view(6144, [NT, 2, 2, PP], parts=R)
        QF, _ = view(9216, [8, 2 * R])
        QQ = TC.rearrange("r g h p -> r g (h p)")
        FF = SC.rearrange("r g h p -> r g (h p)")
        CO = TK.rearrange("r n k a p -> r n (k a p)")
        t_end = at
        PT, at = view(t_end, [4, 2 * NJ, PH, PP], parts=R)
        UV, at = view(at, [2, 2 * NJ, PP], parts=R)
        UT, at = view(at, [2, 2 * NJ, PP], parts=R)
        SM, at2 = view(t_end, [4, 2, 2, R], parts=R)
        ST, at2 = view(at2, [NJ, NP, 2, D])
        assert at2 <= at
        WA, at = view(at, [3, NG * PH], parts=R)
        WE, at_ = view(9216, [NG * PH, WN], parts=R)
        WX, at_ = view(at_, [NG * PH, WN], parts=R)
        GA, at = view(at, [6, NG], parts=R)
        WS, at_ = view(9216 + 2000, [NG * PH], parts=R)
        hdl, _ = view(at_, [WN], parts=R)
        assert at <= ASIZE - 2 * 768, at
        pos1, _ = view(t_end, [L])
        HT, _ = view(t_end + L, [2, HALF])

        e1w, at = view(0, [2, 3, 128])
        e2w, at = view(at, [3, 128])
        e3w, at = view(at, [3, 128])
        RH, at = view(at, [NP * L])
        H1, at = view(at, [4, HALF])
        H2, at = view(at, [3, NP * L])
        GL, at = view(at, [NG, E1], parts=R)
        GE, at = view(at, [NG, E1], parts=R)
        GO, at = view(at, [NG, E1], parts=R)
        GC, at = view(at, [NG, E1], parts=R)
        GW, at = view(at, [NG, E1], parts=R)
        g1, at = view(at, [8, NG], parts=R)
        YO, at = view(at, [2, 6, D], parts=R)
        YR, at = view(at, [2, D], parts=R)
        assert at <= ASIZE - 2 * 768, at

        S = {}

        def sem(*names):
            for n in names:
                S[n] = ctx.enter_context(nc.semaphore(n))

        sem(*[f"bank_full{i}" for i in range(8)], *[f"bank_free{i}" for i in range(8)])
        sem("dve_chain", "act_chain", "pool_chain")
        sem("zeroed", "dma_conv", "dma_weights", "consts", "w96", "conv_w", "bn_var", "bn_rstd", 
            "conv_x", "ln_xc", "ln_sq", "ln_var", "ln_rstd", "xn", "vo_ready", "xbuf_zero",
            "ppt", "ppf", "trig_r", "trig_done")
        sem("ring_full", "ring_free", "split1", "resid", "split2", "split3", "qk_dma0", "qk_dma1", "kb_ones", "v_ready",
            "mx_half", "mx_neg", "shift_in", "shift_out", "shift_dma", "st_done", "exp_done", "pv_done", "ctx_out",
            "att_h", "lnb_sum", "lnb_x", "lnb_ssq", "lnb_done", "onehot_sum", "pos_ready", "big_set", "dma_prep")
        sem("late_zero", "w_late", "big", "route_ld", "route_ex", "onehot", "slots", "scattered", "xb_loaded",
            "y_stored", "gathered0", "gathered1", "gathered2", "gathered3",
            "pos", "cx", "hop_act", "tanh", "width", "gate", "warg", "wexp", "wab", "gc", "rg", "sines", "absd",
            "cosines", "prod", "vsum", "uv", "qf_ready", "ff", "state", "h_pre", "lnx",
            "route1", "route1_ex", "h4", "stored")
        gathered = [S["gathered0"], S["gathered1"], S["gathered2"], S["gathered3"]]
        full = [S[f"bank_full{i}"] for i in range(8)]
        free = [S[f"bank_free{i}"] for i in range(8)]

        jobs = {}

        def take(pe, name):
            k = len(jobs)
            jobs[name] = k
            if k >= 8:
                pe.wait_ge(free[k % 8], k // 8)
            return bank[k % 8], full[k % 8]

        def filled(eng, name):
            k = jobs[name]
            eng.wait_ge(full[k % 8], k // 8 + 1)
            return bank[k % 8], free[k % 8]

        def emptied(eng, name):
            k = jobs[name]
            eng.wait_ge(free[k % 8], k // 8 + 1)

        def pairs(buf, p):
            return buf[:, p].rearrange("r j a d -> r (j a) d")

        def over(ap, n, width):
            return ap.unsqueeze(2).to_broadcast([ap.shape[0], n, width])

        def rows(ap, n):
            return ap.unsqueeze(1).to_broadcast([ap.shape[0], n, ap.shape[1]])

        taps = []
        for i in range(NB):
            mm = [(2, 0, 0, SEG, 0)]
            for tap, shift in ((1, 2 ** i), (0, 2 ** (i + 1))):
                q, r = divmod(shift, SEG)
                if q < NS:
                    mm.append((tap, q, r, SEG, 0))
                if q + 1 < NS and r:
                    mm.append((tap, q + 1, 0, r, SEG - r))
            taps.append(mm)

        NU = 4 * B
        mx, im, pos, sums, kept, sl, sx, tx, sy = (r1[:, i, :] for i in range(9))
        ln_base = (0, 2, 6, 10)
        ffn_order = [("h1", 0), ("h1", 1), ("y", 0), ("h1", 2), ("y", 1), ("yb", 0), ("h1", 3), ("y", 2), ("yb", 1),
                     ("y", 3), ("yb", 2), ("yb", 3)]
        units1 = [(a, p, th, ep) for a in range(2) for p in range(NP) for th in range(2) for ep in range(3)]

        lns = [(1, 2), (1, 2 + NP)]
        for b in range(B):
            if b == 1:
                lns += [(1, 3), (1, 3 + NP)]
            if b:
                lns.append((2, b - 1))
        lns.append((2, B - 1))
        ln_at = {x: k for k, x in enumerate(lns)}

        def ring_jobs(n, c):
            found = []
            if n + 2 < NU:
                found += [("score", n + 2, 4 * c + i) for i in range(4)]
            if c == 1 and n + 1 < NU:
                found.append(("shift", n + 1))
            b, hp = divmod(n, 4)
            if hp < 2 and b + 1 < B and c >= 2:
                found.append(("proj", b + 1, hp, (c - 2) // 2, c % 2))
            k = 6 * hp + c - 2
            if b > 0 and 0 <= k < 12:
                found.append(("out", b - 1, k // 2, k % 2))
            if b < 2 and hp == 2 and c < 2:
                found.append(("xt", 1, b + 2, c))
            if b > 0 and hp == 3:
                found += {0: [("xt", 2, b - 1, 0)], 1: [("xt", 2, b - 1, 1)], 2: [("logits", b - 1)],
                          4: [("pos", b - 1)]}.get(c, [])
            return found

        def side_jobs(n, c):
            b, hp = divmod(n, 4)
            found = []
            if b < 2 and hp < 2 and c in (2, 4):
                found.append(("ln_mean" if c == 2 else "ln_std", 1, b + 2 + NP * hp))
            if b > 0:
                if hp == 2 and c in (3, 4):
                    found.append(("ln_mean" if c == 3 else "ln_std", 2, b - 1))
                if hp == 3 and c in (2, 3):
                    found.append(("choose" if c == 2 else "weigh", b - 1))
            if b > 1:
                if hp == 0 and c == 2:
                    found.append(("slots", b - 2))
                if hp < 2 and c >= 3:
                    found.append(("scatter", b - 2, 3 * hp + c - 3))
            return found

        before = [("proj", 0, g, qk, th) for g in range(2) for qk in range(2) for th in range(2)]
        before += [("score", n, i) for n in range(1) for i in range(24)] + [("shift", 0)]
        before += [("score", 1, i) for i in range(24)]
        b = B - 1
        after = [("slots", b - 1)] + [("scatter", b - 1, j) for j in range(NJ)]
        after += [("out", b, j, h) for j in range(NJ) for h in range(2)]
        after += [("ln_mean", 2, b), ("ln_std", 2, b), ("xt", 2, b, 0), ("xt", 2, b, 1), ("logits", b), ("choose", b),
                  ("weigh", b), ("pos", b), ("slots", b)] + [("scatter", b, j) for j in range(NJ)]
        order = before + [x for n in range(NU) for c in range(6) for x in ring_jobs(n, c) + side_jobs(n, c)] + after
        on_ring = ("proj", "score", "shift", "out", "xt", "logits", "pos")
        ring_at = {x: k for k, x in enumerate(y for y in order if y[0] in on_ring)}
        nproj = {x: k for k, x in enumerate(y for y in order if y[0] == "proj")}
        ring_bank = [bank[0], bank[1]]
        st_bank = [[bank[2], bank[3]], [bank[4], bank[5]]]
        ctx_bank = [bank[6], bank[7]]

        wd = []
        prep = []
        for qk, name in enumerate(("L0_attn_Q", "L0_attn_K")):
            prep.append((qload[:, qk, :, 64:128], t[name].rearrange("(g h) r d -> (h r) g d", g=2)))
        for h2 in range(2):
            rowsl = slice(64 * h2, 64 * h2 + 64)
            vo = t["L0_attn_VO"].rearrange("(hp h) d e -> h d hp e", h=2)[h2]
            prep.append((voload[rowsl, 0, :, :], vo))
            prep.append((voload[rowsl, 1, :, :], t["L0_attn_VO"].rearrange("(hp h) d e -> h d hp e", h=2)[h2, 63]
                       .partition_broadcast(64)))
        for a in range(2):
            r = slice(64 * a, 64 * a + 64)
            wd += [(W["gw"][r, 8 * a:8 * a + 8], t["L0_ffn_gate_w"]),
                   (W["hop1"][r, 64 * a:64 * a + 64], t["L1_attn_hop_w1"][0:64]),
                   (W["hop2"][r, 132 * a:132 * a + 132], t["L1_attn_hop_w2"]),
                   (W["wta"][r, 128 * a:128 * a + 64], t["L1_attn_mc_w"]),
                   (W["wta"][r, 128 * a + 64:128 * a + 128], t["L1_attn_ve_w"]),
                   (W["wta"][r, 256 + 32 * a:288 + 32 * a], t["L1_attn_cpe_w"]),
                   (W["ksk1"][r, 64 * a:64 * a + 64], t["L1_attn_ksk_w1"][0:64]),
                   (W["sg1"][r, 32 * a:32 * a + 32], t["L1_attn_sg_w1"]),
                   (W["ksk2"][r, 32 * a:32 * a + 32], t["L1_attn_ksk_w2"]),
                   (W["sg2"][32 * a:32 * a + 32, a:a + 1], t["L1_attn_sg_w2"]),
                   (W["outw"][r, 64 * a:64 * a + 64], t["L1_attn_out_w"]),
                   (W["rw1"][r, 32 * a:32 * a + 32], t["L1_ffn_router_w1"]),
                   (W["rw2"][32 * a:32 * a + 32, 6 * a:6 * a + 6], t["L1_ffn_router_w2"]),
                   (W["b2"][r, :], t["L0_ffn_b2"][4 * a:4 * a + 4].rearrange("e d -> d e")),
                   (W["e1b"][r, :], t["L1_ffn_expert_b1"].rearrange("(ep e) h -> e h ep", e=2)[a]),
                   (W["e2b"][r, :], t["L1_ffn_expert_b2"].rearrange("(ep e) h -> e h ep", e=2)[a]),
                   (W["sgb1"][32 * a:32 * a + 32, :], t["L1_attn_sg_b1"].unsqueeze(1)),
                   (W["rb1"][32 * a:32 * a + 32, :], t["L1_ffn_router_b1"].unsqueeze(1))]
            prep += [(W["hop1b"][0:32, 64 * a:64 * a + 64], t["L1_attn_hop_w1"][64:96]),
                     (W["kskb"][0:64, 64 * a:64 * a + 64], t["L1_attn_ksk_w1"][64:128]),
                     (W["kb1"][r, :], t["L1_attn_ksk_b1"].unsqueeze(1)),
                     (W["hopb"][r, :], t["L1_attn_hop_b1"].unsqueeze(1))]
            for at_, name, n in ((CVB + 128 * a, "mc_b", 64), (CVB + 128 * a + 64, "ve_b", 64),
                                 (KSB + 32 * a, "cpe_b", 32), (KSB + 64 + 32 * a, "ksk_b2", 32),
                                 (GTB + a, "sg_b2", 1), (AOB + 132 * a, "hop_b2", 132)):
                wd.append((bias[:, at_:at_ + n], t["L1_attn_" + name].partition_broadcast(128)))
        for at_, name, n in ((GB, "L0_ffn_gate_b", 8), (LNG, "L1_attn_ln_g", 64), (LNB, "L1_attn_ln_b", 64),
                             (OB, "L1_attn_out_b", 64), (RB2, "L1_ffn_router_b2", 6)):
            wd.append((bias[:, at_:at_ + n], t[name].partition_broadcast(128)))
        wd.append((bias[:, EB3:EB3 + 384], t["L1_ffn_expert_b3"].rearrange("e d -> (e d)").partition_broadcast(128)))
        wd.append((W["b1"][:, :], t["L0_ffn_b1"].rearrange("e (h f) -> f (e h)", h=2)))
        prep.append((bias[:, WD:WD + WN], t["L1_attn_window_deltas"].partition_broadcast(128)))
        prep.append((W["kceb"][0:64, :], t["L1_attn_kce_b"].unsqueeze(1)))
        prep.append((W["kce"][0:64, :], t["L1_attn_kce_w"]))
        prep.append((ppx[:, :, :], t["L1_attn_pos_phases"][0:L].rearrange("(j r) p -> r j p", r=R)))

        block = ctx.enter_context(nc.Block())

        @block.tensor
        def _(pe):
            pe.wait_ge(S["dma_conv"], 16 * 11)
            pe.wait_ge(S["consts"], 1)
            ps, done = take(pe, "w96")
            pe.matmul(ps[0:96, 0:OW + D], R4, P4[:, 0:OW + D], start=True, stop=True).then_inc(done, 1)
            pe.wait_ge(S["conv_w"], 1)
            for i in range(NB):
                ps, done = take(pe, ("conv", i))
                if i:
                    pe.wait_ge(S["conv_x"], i)
                for n, (tap, q, lo, hi, src) in enumerate(taps[i]):
                    last = pe.matmul(ps[0:96, lo:hi], Fw[:, i * KT + tap, 64 - 32 * q:160 - 32 * q],
                                     xc[:, src:src + hi - lo], start=(n == 0), stop=(n == len(taps[i]) - 1))
                last.then_inc(done, 1)
                if i == 4:
                    pe.wait_ge(S["dma_prep"], 16 * len(prep))
                    pe.wait_ge(S["consts"], 2)
                    for qk in range(2):
                        for a in range(2):
                            ps, done = take(pe, ("qkp", qk, a))
                            for g in range(2):
                                last = pe.transpose(ps[:, g * 128:(g + 1) * 128],
                                                    qload[:, qk, g, 64 - 64 * a:192 - 64 * a], ident)
                            last.then_inc(done, 1)
                if i == 5:
                    ps, done = take(pe, "kcet")
                    pe.transpose(ps[0:64, 0:64], W["kce"][0:64, :], ident[0:64, 0:64]).then_inc(done, 1)
                    ps, done = take(pe, "kb")
                    pe.matmul(ps[:, 0:1], W["kskb"][0:64, :], W["kceb"][0:64, :], start=True, stop=True).then_inc(done, 1)
                    for h in range(2):
                        ps, done = take(pe, ("ppt", h))
                        for n in range(3):
                            last = pe.transpose(ps[0:PP, n * R:(n + 1) * R], ppx[:, 3 * h + n, :], ident[0:R, 0:R])
                        last.then_inc(done, 1)
                if i == 6:
                    emptied(pe, "kcet")
                    emptied(pe, "kb")
                    ps, done = take(pe, "ksm")
                    pe.matmul(ps[:, 0:64], W["kcet"][0:64, :], W["kskb"][0:64, 0:64], start=True, stop=True)\
                        .then_inc(done, 1)
                    emptied(pe, ("ppt", 0))
                    emptied(pe, ("ppt", 1))
                    for h in range(2):
                        ps, done = take(pe, ("ppf", h))
                        pe.matmul(ps[:, 0:HALF], W["hop1b"][0:PP, :], ppt[:, h * HALF:(h + 1) * HALF],
                                  start=True, stop=True).then_inc(done, 1)
            pe.wait_ge(S["conv_x"], NB)
            for half in range(2):
                for s in range(NS):
                    ps, done = take(pe, ("h0", half, s))
                    pe.matmul(ps[0:R, :], xc[:, half * R:(half + 1) * R], Wout[:, 8 * s:8 * s + 8, :],
                              start=True, stop=True).then_inc(done, 1)

            def transposes(name, src, ready, base, count):
                for p in range(count):
                    pe.wait_ge(ready, base + p + 1)
                    for h in range(2):
                        ps, done = take(pe, (name, p, h))
                        for n in range(3):
                            last = pe.transpose(ps[:, n * R:(n + 1) * R],
                                                src[:, p, 3 * h + n].rearrange("r a d -> r (a d)"),
                                                ident[0:R, 0:R])
                        last.then_inc(done, 1)

            transposes("xt1", XN, S["xn"], 0, 2)

            for k in range(len(jobs) - 8, len(jobs)):
                pe.wait_ge(free[k % 8], k // 8 + 1)
            
            def ring(job):
                k = ring_at[job]
                if k >= 2:
                    pe.wait_ge(S["ring_free"], k - 1)
                ps = ring_bank[k % 2]
                kind = job[0]
                if kind == "proj":
                    _, b, g, qk, th = job
                    p, a = b % NP, b // NP
                    if ("xt", 1, b, 1) in ring_at:
                        pe.wait_ge(S["ring_free"], ring_at[("xt", 1, b, 1)] + 1)
                    last = pe.matmul(ps[:, 0:HALF], qkp[:, a, qk, g * 128:(g + 1) * 128],
                                     XT[:, p * L + th * HALF:p * L + (th + 1) * HALF], start=True, stop=True)
                elif kind == "score":
                    _, n, i = job
                    b, hp = divmod(n, 4)
                    h2, j, half = i // 12, i // 2 % 6, i % 2
                    if i == 0:
                        pe.wait_ge(S["qk_dma0"] if hp < 2 else S["qk_dma1"], 16 * 12 * (b + 1))
                    h = 2 * hp + h2
                    last = pe.matmul(ps[0:R, 0:HALF], QA[0:96, b % 2, h, j * R:(j + 1) * R],
                                     KA[0:96, b % 2, h, half * HALF:(half + 1) * HALF], start=True, stop=True)
                elif kind == "shift":
                    n = job[1]
                    pe.wait_ge(S["shift_in"], n + 1)
                    last = pe.transpose(ps[0:36, 0:63].bitcast(BF16)[:, 0:R],
                                        NM[:, n % 2, :], identb[0:R, 0:R])
                elif kind == "xt":
                    _, k_, b, h = job
                    p = b % NP
                    pe.wait_ge(S["lnb_done"], ln_at[(k_, b + NP if k_ == 1 else b)] + 1)
                    for i in range(3):
                        last = pe.transpose(ps[:, i * R:(i + 1) * R],
                                            XN[:, p, 3 * h + i].rearrange("r a d -> r (a d)"), ident[0:R, 0:R])
                elif kind == "logits":
                    b = job[1]
                    p, a = b % NP, b // NP
                    pe.wait_ge(S["ring_free"], ring_at[("xt", 2, b, 1)] + 1)
                    for j in range(NJ):
                        c = p * L + j * R
                        last = pe.matmul(ps[0:R, E0 * j:E0 * j + E0], XT[:, c:c + R],
                                         W["gw"][:, E0 * a:E0 * a + E0], start=True, stop=True)
                elif kind == "pos":
                    b = job[1]
                    pe.wait_ge(S["onehot"], b + 1)
                    pe.wait_ge(S["onehot_sum"], b + 1)
                    pe.matmul(ps[0:R, 0:NJ * E0], triu[0:R, 0:R], OH, start=True, stop=False)
                    last = pe.matmul(ps[0:R, 0:NJ * E0], ones[0:R, 0:R], SO[:, 0:NJ, :], start=False, stop=True)
                else:
                    _, b, j, h = job
                    for i in range(2):
                        hp = 2 * h + i
                        if j == 0 and i == 0:
                            pe.wait_ge(S["ctx_out"], 2 * (4 * b + 2 * h + 2))
                        last = pe.matmul(ps[0:R, i * 130:(i + 1) * 130], CT[:, b % 2, hp, j * R:(j + 1) * R],
                                         vox[:, hp, :], start=True, stop=True)
                last.then_inc(S["ring_full"], 1)

            def scores_t(n, c, h2):
                b, hp = divmod(n, 4)
                x = 12 * n + 2 * c + h2
                if x >= 2:
                    pe.wait_ge(S["exp_done"], x - 1)
                if c == 0 and h2 == 0:
                    pe.wait_ge(S["shift_dma"], 48 * (n + 1))
                    if n == 0:
                        pe.wait_ge(S["kb_ones"], 2)
                h = 2 * hp + h2
                for th in range(2):
                    cols = slice(th * HALF, (th + 1) * HALF)
                    ps = st_bank[h2][th][0:R, 0:HALF]
                    pe.matmul(ps, KA[0:96, b % 2, h, c * R:(c + 1) * R], QA[0:96, b % 2, h, cols],
                              start=True, stop=False)
                    last = pe.matmul(ps, KB[0:99, b % 2, h, c * R:(c + 1) * R], QB[0:99, b % 2, h, cols],
                                     start=False, stop=True)
                last.then_inc(S["st_done"], 1)

            def values(n, c, th):
                b = n // 4
                p, a = b % NP, b // NP
                if th == 0:
                    pe.wait_ge(S["exp_done"], 12 * n + 2 * c + 2)
                    if c == 0:
                        pe.wait_ge(S["v_ready"], p + 1)
                if c == 0 and n:
                    pe.wait_ge(S["ctx_out"], 2 * n - 1 + th)
                for h2 in range(2):
                    last = pe.matmul(ctx_bank[th][64 * h2:64 * h2 + 64, 0:HALF], XN[:, p, c, a, :],
                                     PR[:, (2 * c + h2) % 4, th * HALF:(th + 1) * HALF],
                                     start=(c == 0), stop=(c == 5), tile_position=(0, 64 * h2))
                if th == 1:
                    last.then_inc(S["pv_done"], 1)

            for job in before:
                ring(job)
            for n in range(NU):
                for c in range(6):
                    js = ring_jobs(n, c)
                    scores_t(n, c, 0)
                    for job in js[0:1]:
                        ring(job)
                    scores_t(n, c, 1)
                    for job in js[1:2]:
                        ring(job)
                    u = 6 * n + c - 1
                    if u >= 0:
                        values(u // 6, u % 6, 0)
                    for job in js[2:3]:
                        ring(job)
                    if u >= 0:
                        values(u // 6, u % 6, 1)
                    for job in js[3:]:
                        ring(job)
            values(NU - 1, 5, 0)
            values(NU - 1, 5, 1)
            for job in after:
                if job in ring_at:
                    ring(job)

            pe.wait_ge(S["xb_loaded"], 16 * 8)
            for e in range(4):
                for h in range(2):
                    ps, done = take(pe, ("xbt", e, h))
                    for n in range(4):
                        last = pe.transpose(ps[:, n * R:(n + 1) * R], XB[:, e, 4 * h + n, :], ident[0:R, 0:R])
                    last.then_inc(done, 1)
            pe.wait_ge(S["w_late"], 16 * 3)

            def expert_in(e):
                emptied(pe, ("xbt", e, 0))
                emptied(pe, ("xbt", e, 1))
                for a in range(2):
                    for fh in range(2):
                        for nn in range(2):
                            ps, done = take(pe, ("h1", e, a, fh, nn))
                            pe.matmul(ps[:, 0:CH], w1p[:, e + 4 * a, fh * 128:(fh + 1) * 128],
                                      XBT[:, e, nn * CH:(nn + 1) * CH], start=True, stop=True).then_inc(done, 1)

            def expert_out(e):
                for a in range(2):
                    for fh in range(2):
                        for nn in range(2):
                            emptied(pe, ("h1", e, a, fh, nn))
                for nn in range(2):
                    ps, done = take(pe, ("y", e, nn))
                    for fh in range(2):
                        for a in range(2):
                            last = pe.matmul(ps[64 * a:64 * a + 64, 0:CH], w2e[:, e + 4 * a, fh, :],
                                             HM[:, e % 2, a, fh, nn * CH:(nn + 1) * CH],
                                             start=(fh == 0), stop=(fh == 1), tile_position=(0, 64 * a))
                    last.then_inc(done, 1)

            def expert_back(e):
                emptied(pe, ("y", e, 0))
                emptied(pe, ("y", e, 1))
                pe.wait_ge(S["big"], 2)
                for h in range(2):
                    ps, done = take(pe, ("yb", e, h))
                    for n in range(4):
                        last = pe.transpose(ps[0:R, n * 128:(n + 1) * 128],
                                            YT[:, e, (4 * h + n) * R:(4 * h + n + 1) * R], ident)
                    last.then_inc(done, 1)

            expert_in(0)
            for e in range(4):
                if e < 3:
                    expert_in(e + 1)
                expert_out(e)
                if e:
                    expert_back(e - 1)
            expert_back(3)

            transposes("xt3", XN, S["xn"], 2, NP)
            for p in range(NP):
                emptied(pe, ("xt3", p, 0))
                emptied(pe, ("xt3", p, 1))
                for th in range(2):
                    cols = slice(p * L + th * HALF, p * L + (th + 1) * HALF)
                    for name, w in (("hop", W["hop1"]), ("sg", W["sg1"])):
                        ps, done = take(pe, (name, p, th))
                        pe.matmul(ps[0:w.shape[1], 0:HALF], w, XT[:, cols], start=True, stop=True).then_inc(done, 1)
                    if th == 0:
                        pe.wait_ge(S["cx"], p + 1)
                    ps, done = take(pe, ("ksk", p, th))
                    pe.matmul(ps[:, 0:HALF], W["ksk1"], XT[:, cols], start=True, stop=False)
                    pe.matmul(ps[:, 0:HALF], W["ksm"], CX[:, cols], start=False, stop=True).then_inc(done, 1)
            for p in range(NP):
                for j in range(NJ):
                    i = p * NJ + j
                    if j == 0:
                        for th in range(2):
                            emptied(pe, ("ksk", p, th))
                        pe.wait_ge(S["hop_act"], 2 * (p + 1))
                    cols = slice(i * R, (i + 1) * R)
                    ps, done = take(pe, ("tok", i))
                    pe.matmul(ps[0:R, 0:320], XT[:, cols], W["wta"], start=True, stop=True)
                    pe.matmul(ps[0:R, 320:384], KG[:, cols], W["ksk2"], start=True, stop=True)
                    pe.matmul(ps[0:R, 384:386], SG[0:64, cols], W["sg2"][0:64, :], start=True, stop=True)\
                        .then_inc(done, 1)
                    ps, done = take(pe, ("ao", i))
                    pe.matmul(ps[0:R, 0:264], HG[:, cols], W["hop2"], start=True, stop=True).then_inc(done, 1)
            pe.wait_ge(S["gate"], 1)
            for name, m in (("gcum", triu), ("gtot", ones)):
                ps, done = take(pe, name)
                pe.matmul(ps[0:R, 0:NG], m[0:R, 0:R], GA[:, 0, :], start=True, stop=True).then_inc(done, 1)

            steps = [(j, p) for j in range(NJ) for p in range(NP)]

            def features(x):
                j, p = steps[x]
                if x < NP:
                    pe.wait_ge(S["qf_ready"], p + 1)
                    pe.wait_ge(S["ff"], p + 1)
                g = (p * NJ + j) * 2
                for a in range(2):
                    ps, done = take(pe, ("qf", x, a))
                    pe.transpose(ps[:, 0:R], QQ[:, g + a, :], ident[0:R, 0:R])
                    pe.transpose(ps[:, R:2 * R], FF[:, g + a, :], ident[0:R, 0:R]).then_inc(done, 1)

            def masked(x):
                j, p = steps[x]
                g = (p * NJ + j) * 2
                for k in range(2):
                    ps, done = take(pe, ("sm", x, k))
                    for a in range(2):
                        if k == 0:
                            emptied(pe, ("qf", x, a))
                        q = QF[64 * k:64 * k + 64, (2 * x + a) % 8, :]
                        last = pe.matmul(ps[0:R, a * R:(a + 1) * R], q[:, R:2 * R], q[:, 0:R], start=True, stop=True)
                    last.then_inc(done, 1)
                if j < NJ - 1:
                    ps, done = take(pe, ("state", x))
                    for a in range(2):
                        last = pe.matmul(ps[:, a * 128:(a + 1) * 128], FF[:, g + a, :],
                                         CV[:, g // 2, a].rearrange("r c d -> r (c d)"), start=True, stop=True)
                    last.then_inc(done, 1)

            def retrieved(x):
                j, p = steps[x]
                g = (p * NJ + j) * 2
                emptied(pe, ("sm", x, 0))
                emptied(pe, ("sm", x, 1))
                if j:
                    pe.wait_ge(S["state"], 2 * (x - NP + 1))
                ps, done = take(pe, ("ret", x))
                for a in range(2):
                    o = ps[0:R, a * D:(a + 1) * D]
                    pe.matmul(o, SM[:, x % 4, 0, a, :], CV[:, g // 2, a, 0, :], start=True, stop=False)
                    last = pe.matmul(o, SM[:, x % 4, 1, a, :], CV[:, g // 2, a, 1, :], start=False, stop=(j == 0))
                    if j:
                        last = pe.matmul(o, QF[:, (2 * x + a) % 8, 0:R], ST[:, j, p, a, :], start=False, stop=True)
                last.then_inc(done, 1)

            for x in range(NT + 2):
                if x < NT:
                    features(x)
                if 1 <= x <= NT:
                    masked(x - 1)
                if x >= 2:
                    retrieved(x - 2)
            for p in range(NP):
                pe.wait_ge(S["lnx"], p + 1)
                for h in range(2):
                    ps, done = take(pe, ("xt4", p, h))
                    for n in range(3):
                        last = pe.transpose(ps[:, n * R:(n + 1) * R], CO[:, p * NJ + 3 * h + n, :], ident[0:R, 0:R])
                    last.then_inc(done, 1)
            for p in range(NP):
                emptied(pe, ("xt4", p, 0))
                emptied(pe, ("xt4", p, 1))
                for h in range(2):
                    ps, done = take(pe, ("o1", p, h))
                    for n in range(3):
                        c = p * L + (3 * h + n) * R
                        last = pe.matmul(ps[0:R, n * 128:(n + 1) * 128], XT[:, c:c + R], W["outw"], start=True, stop=True)
                    last.then_inc(done, 1)

            transposes("xt5", XN, S["xn"], 10, NP)
            pe.wait_ge(S["w_late"], 16 * 9)
            for p in range(NP):
                emptied(pe, ("xt5", p, 0))
                emptied(pe, ("xt5", p, 1))
                for th in range(2):
                    cols = slice(p * L + th * HALF, p * L + (th + 1) * HALF)
                    ps, done = take(pe, ("rh", p, th))
                    pe.matmul(ps[0:64, 0:HALF], W["rw1"], XT[:, cols], start=True, stop=True).then_inc(done, 1)
            for p in range(NP):
                emptied(pe, ("rh", p, 0))
                emptied(pe, ("rh", p, 1))
            ps, done = take(pe, "logits1")
            for i in range(NT):
                last = pe.matmul(ps[0:R, 12 * i:12 * i + 12], RH[0:64, i * R:(i + 1) * R], W["rw2"][0:64, :],
                                 start=True, stop=True)
            last.then_inc(done, 1)
            units = units1

            def layer1(x):
                a, p, th, ep = units[x]
                ps, done = take(pe, ("l1", x))
                pe.matmul(ps[:, 0:HALF], e1w[:, a, ep, :], XT[:, p * L + th * HALF:p * L + (th + 1) * HALF],
                          start=True, stop=True).then_inc(done, 1)

            def layer2(x):
                a, p, th, ep = units[x]
                emptied(pe, ("l1", x))
                ps, done = take(pe, ("l2", x))
                pe.matmul(ps[:, 0:HALF], e2w[:, ep, :], H1[:, x % 4, :], start=True, stop=True).then_inc(done, 1)

            def layer3(a, p, th):
                x0 = 3 * ((a * NP + p) * 2 + th)
                for ep in range(3):
                    emptied(pe, ("l2", x0 + ep))
                for n in range(3):
                    j = 3 * th + n
                    ps, done = take(pe, ("l3", a, p, j))
                    for ep in range(3):
                        last = pe.matmul(ps[0:R, ep * 128:(ep + 1) * 128],
                                         H2[:, ep, p * L + j * R:p * L + (j + 1) * R], e3w[:, ep, :],
                                         start=True, stop=True)
                    last.then_inc(done, 1)

            NX = len(units)
            for x in range(NX + 1):
                if x < NX:
                    layer1(x)
                if x:
                    layer2(x - 1)
                    if x >= 6 and x % 3 == 0:
                        layer3(*units[x - 6][0:3])
            layer3(*units[NX - 3][0:3])

        @block.sync
        def _(sp):
            for s in range(NS):
                sp.dma_start(xc[32 * s:32 * s + 32, :],
                             t["x"].rearrange("b c (s l) -> s (b c) l", s=NS)[s]).then_inc(S["dma_conv"], 16)
            sp.dma_start(P4[:, 0:PAR].rearrange("c (i o k) -> c i o k", i=NB, o=CIN),
                         t["L0_tok_conv_w"].rearrange("i o c k -> c i o k")).then_inc(S["dma_conv"], 16)
            for n, name in enumerate(("conv_b", "bn_gamma", "bn_beta", "bn_mean", "bn_var")):
                sp.dma_start(P4[:, PAR + n * NB:PAR + (n + 1) * NB],
                             t["L0_tok_" + name].rearrange("i c -> c i")).then_inc(S["dma_conv"], 16)
            sp.dma_start(P4[:, OW:OW + D], t["L0_tok_out_w"].rearrange("v c o -> c (v o)")).then_inc(S["dma_conv"], 16)
            sp.dma_start(outb[:, :], t["L0_tok_out_b"].partition_broadcast(R)).then_inc(S["dma_conv"], 16)
            sp.wait_ge(S["zeroed"], 1)
            for e in range(E0):
                sp.dma_start(xbuf[e * ROWS:(e + 1) * ROWS].rearrange("(r c) d -> r (c d)", r=R), zeros)\
                    .then_inc(S["xbuf_zero"], 16)
            sp.wait_ge(S["zeroed"], 2)
            for dst, src in prep:
                sp.dma_start(dst, src).then_inc(S["dma_prep"], 16)
            for dst, src in wd:
                sp.dma_start(dst, src).then_inc(S["dma_weights"], 16)

            for job in order:
                if job[0] == "proj" and job[4] == 1:
                    _, b, g, qk, th = job
                    dma = S["qk_dma0"] if g == 0 else S["qk_dma1"]
                    sp.wait_ge(S["split3"], nproj[job] + 1)
                    if b >= 2:
                        sp.wait_ge(S["st_done"], 48 * (b - 1))
                    for arr, terms in (((QA, (0, 0, 1)), (QB, (0, 2, 1))), ((KA, (0, 1, 0)), (KB, (2, 0, 1))))[qk]:
                        for s, term in enumerate(terms):
                            sp.dma_start(arr[32 * s:32 * s + 32, b % 2, 4 * g:4 * g + 4, :],
                                         SP[:, qk, term, :]).then_inc(dma, 16)
                if job[0] == "shift":
                    n = job[1]
                    b, hp = divmod(n, 4)
                    sp.wait_ge(S["ring_free"], ring_at[job] + 1)
                    for term in range(3):
                        dst = QB[96 + term:97 + term, b % 2, 2 * hp:2 * hp + 2, :]
                        sp.dma_start(dst.rearrange("o h (j r) -> o (h j) r", r=R), MT[12 * term:12 * term + 12, n % 2, 0:R])\
                            .then_inc(S["shift_dma"], 16)

            sp.wait_ge(S["late_zero"], 1)
            sp.dma_start(w1p[0:64, 0:4, :], t["L0_ffn_w1"][0:4].rearrange("e d f -> d e f")).then_inc(S["w_late"], 16)
            sp.dma_start(w1p[64:128, 4:8, :], t["L0_ffn_w1"][4:8].rearrange("e d f -> d e f")).then_inc(S["w_late"], 16)
            sp.dma_start(w2e.rearrange("f e h d -> f (e h) d"),
                         t["L0_ffn_w2"].rearrange("e (h f) d -> f (e h) d", h=2)).then_inc(S["w_late"], 16)
            sp.wait_ge(S["scattered"], 16 * NG)
            for e in range(4):
                for a in range(2):
                    r0 = (e + 4 * a) * ROWS
                    sp.dma_start(XB[:, e, :, a * D:(a + 1) * D],
                                 xbuf[r0:r0 + ROWS].rearrange("(c r) d -> r c d", r=R)).then_inc(S["xb_loaded"], 16)
            for e in range(4):
                emptied(sp, ("yb", e, 0))
                emptied(sp, ("yb", e, 1))
                for a in range(2):
                    r0 = (e + 4 * a) * ROWS
                    sp.dma_start(ybuf[r0:r0 + ROWS].rearrange("(c r) d -> r c d", r=R),
                                 XB[:, e, :, a * D:(a + 1) * D]).then_inc(S["y_stored"], 16)
            sp.wait_ge(S["late_zero"], 2)
            for a in range(2):
                r = slice(64 * a, 64 * a + 64)
                w1, w2, w3 = (t["L1_ffn_expert_w" + str(n)].rearrange("(ep e) d h -> e d ep h", e=2)
                              for n in (1, 2, 3))
                sp.dma_start(e1w[r, a].rearrange("d ep (e h) -> d (ep e) h", e=2),
                             t["L1_ffn_expert_w1"].rearrange("e d h -> d e h")).then_inc(S["w_late"], 16)
                sp.dma_start(e2w[r, :, 64 * a:64 * a + 64], w2[a]).then_inc(S["w_late"], 16)
                sp.dma_start(e3w[r, :, 64 * a:64 * a + 64], w3[a]).then_inc(S["w_late"], 16)
            for a in range(2):
                for p in range(NP):
                    sp.wait_ge(S["h4"], NJ * (a * NP + p + 1))
                    sp.dma_start(out[p + 4 * a].rearrange("(j r) d -> r j d", r=R), H[:, p, :, a, :])\
                        .then_inc(S["stored"], 16)
            sp.wait_ge(S["stored"], 16 * B)

        @block.gpsimd
        def _(pool):
            n_ = [0]

            def link(ins):
                n_[0] += 1
                ins.then_inc(S["pool_chain"], 1)
                pool.wait_ge(S["pool_chain"], n_[0])

            pool.memset(R4, 0.0)
            pool.memset(bmask, 1.0)
            link(pool.memset(m24, 1.0))
            v = R4.rearrange("c (g k) -> c g k", k=CIN)
            pool.affine_select(out=v, in_=v, compare_op=ALU.not_equal, fill=1.0, base=0,
                               pattern=[[0, NS * B], [-1, CIN]], channel_multiplier=1).then_inc(S["consts"], 1)
            masks = [bmask[32 * s:32 * s + 32, :] for s in range(NS)] + [m24]
            for v in masks:
                link(pool.affine_select(out=v, in_=v, compare_op=ALU.is_ge, fill=0.0, base=0,
                                        pattern=[[-CIN, v.shape[1]]], channel_multiplier=1))
                link(pool.affine_select(out=v, in_=v, compare_op=ALU.is_ge, fill=0.0, base=CIN - 1,
                                        pattern=[[CIN, v.shape[1]]], channel_multiplier=-1))
            pool.memset(Fw, 0.0)
            pool.memset(ident[:, :], 0.0)
            pool.memset(triu[:, :], 1.0)
            pool.memset(ones[:, :], 1.0)
            pool.memset(mhalf[:, :], -0.5)
            link(pool.memset(halfpi[:, :], PI / 2))
            pool.affine_select(out=ident[:, :], in_=ident[:, :], compare_op=ALU.not_equal, fill=1.0, base=0,
                               pattern=[[-1, 128]], channel_multiplier=1).then_inc(S["consts"], 1)
            pool.affine_select(out=triu[:, :], in_=triu[:, :], compare_op=ALU.is_ge, fill=0.0, base=0,
                               pattern=[[1, 128]], channel_multiplier=-1)
            pool.memset(zero1[:, :], 0.0)
            pool.memset(wearly, 0.0)
            pool.memset(zeros, 0.0).then_inc(S["zeroed"], 1)
            pool.memset(qload, 0.0)
            pool.memset(wall[:, :], 0.0)
            pool.memset(vox[:, :, :], 0.0).then_inc(S["zeroed"], 1)
            pool.wait_ge(S["consts"], 2)
            pool.tensor_copy(identb[:, :], ident[:, :]).then_inc(S["consts"], 1)
            pool.iota(out=iota8[:, :], pattern=[[1, E0]], base=-E0, channel_multiplier=0,
                      allow_small_or_imprecise_dtypes=True).then_inc(S["consts"], 1)
            pool.wait_ge(S["bn_var"], 1)
            pool.tensor_tensor(bn[:, 1, :], bn[:, 0, :], mhalf[0:96, 0:NB], ALU.pow).then_inc(S["bn_rstd"], 1)
            pool.wait_ge(S["vo_ready"], 1)
            for h2 in range(2):
                v = vox[:, :, 65 * h2 + 64:65 * h2 + 65]
                ins = pool.affine_select(out=v, in_=v, compare_op=ALU.not_equal, fill=1.0, base=-(63 + 64 * h2),
                                         pattern=[[0, 4], [0, 1]], channel_multiplier=1)
            ins.then_inc(S["vo_ready"], 1)

            def ln_rstd(k):
                for p in range(2 if k == 0 else NP):
                    pool.wait_ge(S["ln_var"], ln_base[k] + p + 1)
                    pool.tensor_tensor(lnst[:, 3, p, :], lnst[:, 2, p, :], mhalf[0:R, 0:2 * NJ], ALU.pow)\
                        .then_inc(S["ln_rstd"], 1)

            ln_rstd(0)

            pool.wait_ge(S["ln_rstd"], 2)
            for a in range(2):
                pool.memset(KB[96:99, a], 1.0).then_inc(S["kb_ones"], 1)
                pool.wait_ge(S["kb_ones"], a + 1)

            def values_ready(p):
                pool.memset(XN[:, p, :, :, D - 1:D], 1.0).then_inc(S["v_ready"], 1)

            link(pool.memset(SO[:, NJ, :], 0.0))
            for p in range(2):
                for h in range(2):
                    pool.wait_ge(full[jobs[("xt1", p, h)] % 8], jobs[("xt1", p, h)] // 8 + 1)
                values_ready(p)
            for job in order:
                kind = job[0]
                if kind == "proj":
                    _, b, g, qk, th = job
                    q = nproj[job]
                    cols = slice(th * HALF, (th + 1) * HALF)
                    pool.wait_ge(S["ring_free"], ring_at[job] + 1)
                    link(pool.tensor_copy(SP[:, qk, 1, cols], RR[:, q % 2, :]))
                    pool.tensor_tensor(SP[:, qk, 2, cols], RR[:, q % 2, :], SP[:, qk, 1, cols], ALU.subtract)\
                        .then_inc(S["split3"], 1)
                elif kind == "score" and job[2] == 23:
                    n = job[1]
                    pool.wait_ge(S["mx_neg"], n + 1)
                    if n >= 2:
                        pool.wait_ge(S["ring_full"], ring_at[("shift", n - 2)] + 1)
                    m, nm = M1[:, n % 2, :], NM[:, n % 2, :]
                    link(pool.tensor_scalar(nm[:, 0:12], m, -1.0, None, ALU.mult))
                    link(pool.tensor_tensor(MR[:, 0, :], m, nm[:, 0:12], ALU.add))
                    link(pool.tensor_scalar(nm[:, 12:24], MR[:, 0, :], -1.0, None, ALU.mult))
                    link(pool.tensor_tensor(MR[:, 1, :], MR[:, 0, :], nm[:, 12:24], ALU.add))
                    pool.tensor_scalar(nm[:, 24:36], MR[:, 1, :], -1.0, None, ALU.mult).then_inc(S["shift_in"], 1)
                elif kind == "xt" and job[1] == 1 and job[3] == 1:
                    pool.wait_ge(S["ring_full"], ring_at[job] + 1)
                    values_ready(job[2])
                elif kind == "ln_mean":
                    k, b = ln_at[job[1:3]], job[2]
                    p, a = b % NP, b // NP
                    pool.wait_ge(S["lnb_sum"], k + 1)
                    x = XN[:, p, :, a, :]
                    link(pool.tensor_scalar(lnb[:, 1, :], lnb[:, 0, :], -1.0 / D, None, ALU.mult))
                    link(pool.tensor_tensor(x, H[:, p, :, a, :], over(lnb[:, 1, :], NJ, D), ALU.add))
                    pool.tensor_tensor(XSQ, x, x, ALU.mult).then_inc(S["lnb_x"], 1)
                elif kind == "ln_std":
                    k, b = ln_at[job[1:3]], job[2]
                    p, a = b % NP, b // NP
                    pool.wait_ge(S["lnb_ssq"], k + 1)
                    x = XN[:, p, :, a, :]
                    link(pool.tensor_scalar(lnb[:, 3, :], lnb[:, 2, :], 1.0 / D, EPS, ALU.mult, ALU.add))
                    link(pool.tensor_tensor(lnb[:, 3, :], lnb[:, 3, :], mhalf[0:R, 0:NJ], ALU.pow))
                    pool.tensor_tensor(x, x, over(lnb[:, 3, :], NJ, D), ALU.mult).then_inc(S["lnb_done"], 1)
                elif kind == "choose":
                    b = job[1]
                    pool.wait_ge(S["onehot"], b + 1)
                    link(pool.tensor_copy(SO[:, 0, :], SO[:, NJ, :]))
                    for j in range(NJ):
                        ins = pool.tensor_tensor(SO[:, j + 1, :], SO[:, j, :], OH[:, j, :], ALU.add)
                        if j < NJ - 1:
                            link(ins)
                    ins.then_inc(S["onehot_sum"], 1)
                elif kind == "slots":
                    b = job[1]
                    tiles = slice(NJ * b, NJ * b + NJ)
                    pool.wait_ge(S["pos_ready"], b + 1)
                    link(pool.tensor_scalar(kept, pos, float(CAP), None, ALU.is_le))
                    link(pool.tensor_tensor(pk[:, tiles], prob[:, tiles], kept, ALU.mult))
                    link(pool.tensor_scalar(sl, im, float(ROWS), float(E0 * ROWS), ALU.mult, ALU.add))
                    link(pool.tensor_scalar(tx, kept, -65536.0, 65535.0, ALU.mult, ALU.add))
                    link(pool.tensor_tensor(sx, sl, pos, ALU.add))
                    link(pool.tensor_tensor(sx, sx, tx, ALU.add))
                    link(pool.tensor_copy(slot_in[:, tiles], sx))
                    link(pool.tensor_scalar(sy, pos, float(CAP), -1.0, ALU.min, ALU.add))
                    link(pool.tensor_tensor(sy, sy, sl, ALU.add))
                    link(pool.tensor_copy(slot_out[:, tiles], sy))
                    if b == 0:
                        pool.wait_ge(S["xbuf_zero"], 16 * E0)
                elif kind == "scatter":
                    _, b, j = job
                    p, a = b % NP, b // NP
                    g = b * NJ + j
                    pool.indirect_dma_start(out=xbuf, out_offset=bass.IndirectOffsetOnAxis(ap=slot_in[:, g:g + 1],
                                                                                           axis=0),
                                            in_=XN[:, p, j, a, :], in_offset=None, bounds_check=E0 * ROWS - 1,
                                            oob_is_err=False).then_inc(S["scattered"], 16)
                if job == after[NJ]:
                    pool.wait_ge(S["st_done"], 12 * NU)
                    pool.memset(w1p, 0.0).then_inc(S["late_zero"], 1)
                    pool.wait_ge(S["late_zero"], 1)

            pool.memset(big[:, 0, :], 1.0e4)
            pool.memset(big[:, 1, :], -1.0e4).then_inc(S["big"], 1)
            pool.memset(YT[:, :, CAP:ROWS], 0.0).then_inc(S["big"], 1)
            pool.wait_ge(S["y_stored"], 16 * 8)
            for p in range(NP):
                for j in range(NJ):
                    for a in range(2):
                        g, i = a * NT + p * NJ + j, (p * NJ + j) * 2 + a
                        pool.indirect_dma_start(
                            out=YG[:, i, :], out_offset=None, in_=ybuf,
                            in_offset=bass.IndirectOffsetOnAxis(ap=slot_out[:, g:g + 1], axis=0),
                            bounds_check=E0 * ROWS - 1, oob_is_err=False).then_inc(gathered[p], 16)

            ln_rstd(1)
            pool.wait_ge(S["ln_xc"], 3)
            pool.iota(out=pos1, pattern=[[1, L]], base=1, channel_multiplier=0,
                      allow_small_or_imprecise_dtypes=True).then_inc(S["pos"], 1)
            for p in range(NP):
                pool.wait_ge(S["xn"], 2 + p + 1)
                link(pool.tensor_tensor(pairs(H, p), pairs(H, p), pairs(XN, p), ALU.add))
                pool.tensor_tensor(pairs(H, p), pairs(H, p), rows(bias[0:R, OB:OB + D], 2 * NJ), ALU.add)\
                    .then_inc(S["h_pre"], 1)
            pool.wait_ge(S["gc"], 1)
            link(pool.tensor_tensor(GA[:, 5, :], GA[:, 4, :], mhalf[0:R, 0:NG], ALU.pow))
            link(pool.tensor_scalar(GA[:, 5, :], GA[:, 5, :], RS, None, ALU.mult))
            for p in range(NP):
                g = slice(12 * p, 12 * p + 12)
                pool.wait_ge(S["cosines"], 2 * (p + 1))
                pool.wait_ge(S["wab"], 1)
                if p:
                    pool.wait_ge(S["uv"], p)
                cc, sc = (x[:, g].rearrange("r g h p -> r (g h) p") for x in (TC, SC))
                wa, wb = (over(WA[:, i, 48 * p:48 * p + 48], 48, PP) for i in range(2))
                p2, p3 = (PT[:, i].rearrange("r g h p -> r (g h) p") for i in (2, 3))
                pool.tensor_tensor(p2, sc, wa, ALU.mult)
                link(pool.tensor_tensor(p3, cc, wb, ALU.mult))
                pool.tensor_tensor(p2, p2, p3, ALU.add).then_inc(S["vsum"], 1)
                pool.wait_ge(S["prod"], p + 1)
                pool.wait_ge(S["vsum"], p + 1)
                for i, x in ((0, TK), (1, SK)):
                    kk, ss = (x[:, NJ * p:NJ * p + NJ, w] for w in (0, 1))
                    fs, fq = (v[:, g, 64 + 32 * i:96 + 32 * i].rearrange("r (j a) p -> r j a p", a=2)
                              for v in (FF, QQ))
                    pool.tensor_copy(fs, ss)
                    pool.tensor_tensor(fq, kk, over(GA[:, 5, g], 12, PP).rearrange("r (j a) p -> r j a p", a=2),
                                       ALU.mult)
                    pool.tensor_copy(FF[:, g, 32 * i:32 * i + 32].rearrange("r (j a) p -> r j a p", a=2),
                                     trig[:, i, 0:NJ * PP].rearrange("r (j p) -> r j p", p=PP).unsqueeze(2)
                                     .to_broadcast([R, NJ, 2, PP]))
                pool.tensor_tensor(CV[:, NJ * p:NJ * p + NJ, :, 1, :].rearrange("r j a d -> r (j a) d"),
                                   CV[:, NJ * p:NJ * p + NJ, :, 1, :].rearrange("r j a d -> r (j a) d"),
                                   over(GA[:, 0, g], 12, D), ALU.mult).then_inc(S["ff"], 1)
            ln_rstd(2)
            for p in range(NP):
                v = CO[:, NJ * p:NJ * p + NJ, :].rearrange("r j (a d) -> r (j a) d", a=2)
                pool.wait_ge(S["xn"], 6 + p + 1)
                link(pool.tensor_tensor(v, v, rows(bias[0:R, LNG:LNG + D], 12), ALU.mult))
                pool.tensor_tensor(v, v, rows(bias[0:R, LNB:LNB + D], 12), ALU.add).then_inc(S["lnx"], 1)

            for p in range(NP):
                emptied(pool, ("o1", p, 1))
            pool.memset(e1w, 0.0)
            pool.memset(e2w, 0.0)
            pool.memset(e3w, 0.0).then_inc(S["late_zero"], 1)
            ln_rstd(3)

        @block.scalar
        def _(act):
            for i in range(NB):
                ps, done = filled(act, ("conv", i))
                if i == 0:
                    act.wait_ge(S["w96"], 1)
                act.activation(xr, ps[0:96, 0:SEG], ACT.Relu, bias=W96[:, PAR + i:PAR + i + 1]).then_inc(done, 1)
                if i == 4:
                    for qk in range(2):
                        for a in range(2):
                            ps, done = filled(act, ("qkp", qk, a))
                            act.wait_ge(S["zeroed"], 2)
                            act.activation(qkp[:, a, qk, :].rearrange("p (g r h) -> p g h r", g=2, h=4),
                                           ps[:, 0:256].rearrange("p (g h r) -> p g h r", g=2, h=4), ACT.Copy)\
                               .then_inc(done, 1)
                if i == 5:
                    ps, done = filled(act, "kcet")
                    act.activation(W["kcet"][0:64, 0:64], ps[0:64, 0:64], ACT.Copy)
                    act.activation(W["kcet"][0:64, 64:128], ps[0:64, 0:64], ACT.Copy).then_inc(done, 1)
                    ps2, done2 = filled(act, "kb")
                    act.activation(W["kb"], ps2[:, 0:1], ACT.Identity, bias=W["kb1"]).then_inc(done2, 1)
                    for h in range(2):
                        ps, done = filled(act, ("ppt", h))
                        act.activation(ppt[:, h * HALF:(h + 1) * HALF], ps[0:PP, 0:HALF], ACT.Copy)\
                           .then_inc(done, 1)
                if i == 6:
                    ps, done = filled(act, "ksm")
                    for a in range(2):
                        r = slice(64 * a, 64 * a + 64)
                        last = act.activation(W["ksm"][r, 64 * a:64 * a + 64], ps[r, 0:64], ACT.Copy)
                    last.then_inc(done, 1)
                    for h in range(2):
                        ps, done = filled(act, ("ppf", h))
                        act.activation(PPF[:, h * HALF:(h + 1) * HALF], ps[:, 0:HALF], ACT.Identity, bias=W["hopb"])\
                           .then_inc(done, 1)
            act.wait_ge(S["trig_r"], 1)
            act.activation(trig[:, 1, :], phases, ACT.Sin).then_inc(S["trig_done"], 1)
            act.activation(trig[:, 0, :], trig[:, 0, :], ACT.Sin, bias=halfpi[0:R, :], scale=-1.0)\
               .then_inc(S["trig_done"], 1)

            def ln_squares(k, src):
                for p in range(2 if k == 0 else NP):
                    act.wait_ge(S["ln_xc"], ln_base[k] + p + 1)
                    if p >= 2:
                        act.wait_ge(S["ln_var"], ln_base[k] + p - 1)
                    act.activation(SQ[:, p % 2, :], src(p), ACT.Square).then_inc(S["ln_sq"], 1)

            def xn_flat(p):
                return XN[:, p].rearrange("r j a d -> r (j a d)")

            def to_xt(name, count=NP):
                for p in range(count):
                    for h in range(2):
                        ps, done = filled(act, (name, p, h))
                        act.activation(XT[:, p * L + h * HALF:p * L + (h + 1) * HALF], ps[:, 0:HALF], ACT.Copy)\
                           .then_inc(done, 1)

            ln_squares(0, xn_flat)
            to_xt("xt1", 2)

            def split1(job):
                _, b, g, qk, th = job
                k = ring_at[job]
                act.wait_ge(S["ring_full"], k + 1)
                group = 2 * b + g
                if group and qk == 0 and th == 0:
                    prev = group - 1
                    act.wait_ge((S["qk_dma0"], S["qk_dma1"])[prev % 2], 16 * 12 * (prev // 2 + 1))
                act.activation(SP[:, qk, 0, th * HALF:(th + 1) * HALF], ring_bank[k % 2][:, 0:HALF], ACT.Copy,
                               scale=(0.125 if qk == 0 else 1.0)).then_inc(S["split1"], 1)

            def exp_(n, c, h2):
                x = 12 * n + 2 * c + h2
                act.wait_ge(S["st_done"], x + 1)
                if x >= 4:
                    act.wait_ge(S["pv_done"], x // 2 - 1)
                act.activation(PR[:, x % 4, :].rearrange("r (h c) -> r h c", h=2),
                               psum[0:R, 2 + 2 * h2:4 + 2 * h2, 0:HALF], ACT.Exp).then_inc(S["exp_done"], 1)

            def ctx_out(n):
                b, hp = divmod(n, 4)
                act.wait_ge(S["pv_done"], 6 * (n + 1))
                if b >= 2:
                    act.wait_ge(S["ring_full"], ring_at[("out", b - 2, NJ - 1, 1)] + 1)
                for th in range(2):
                    act.activation(CT[:, b % 2, hp, th * HALF:(th + 1) * HALF], ctx_bank[th][:, 0:HALF], ACT.Copy)\
                       .then_inc(S["ctx_out"], 1)

            def weigh(b):
                act.wait_ge(S["route_ld"], b + 1)
                act.activation(LD, LD, ACT.Exp).then_inc(S["route_ex"], 1)

            for job in before:
                if job[0] == "proj":
                    split1(job)
            for n in range(NU):
                for c in range(6):
                    exp_(n, c, 0)
                    exp_(n, c, 1)
                    if c == 0 and n:
                        ctx_out(n - 1)
                    for job in ring_jobs(n, c) + side_jobs(n, c):
                        if job[0] == "proj":
                            split1(job)
                        elif job[0] == "weigh":
                            weigh(job[1])
            ctx_out(NU - 1)
            weigh(B - 1)

            def copy_out(name, dst):
                ps, done = filled(act, name)
                k = jobs[name]
                act.activation(dst, ps[0:dst.shape[0], 0:dst.shape[1]], ACT.Copy).then_inc(done, 1)

            for e in range(4):
                copy_out(("xbt", e, 0), XBT[:, e, 0:4 * R])
            for kind, e in ffn_order:
                if kind == "h1":
                    for a in range(2):
                        for nn in range(2):
                            name = ("h1", e, a, 0, nn)
                            ps, done = filled(act, name)
                            act.activation(HM[:, e % 2, a, 0, nn * CH:(nn + 1) * CH], ps[:, 0:CH], ACT.Relu,
                                           bias=W["b1"][:, 2 * (e + 4 * a):2 * (e + 4 * a) + 1]).then_inc(done, 1)
                elif kind == "y":
                    for nn in range(2):
                        ps, done = filled(act, ("y", e, nn))
                        act.activation(YT[:, e, nn * CH:(nn + 1) * CH], ps[:, 0:CH], ACT.Identity,
                                       bias=W["b2"][:, e:e + 1]).then_inc(done, 1)
                else:
                    copy_out(("yb", e, 0), XB[:, e, 0:4, :].rearrange("r c d -> r (c d)"))

            ln_squares(1, xn_flat)
            to_xt("xt3")
            for p in range(NP):
                for th in range(2):
                    cols = slice(p * L + th * HALF, p * L + (th + 1) * HALF)
                    emptied(act, ("hop", p, th))
                    act.activation(HG[:, cols], HT[:, th, :], ACT.Gelu).then_inc(S["hop_act"], 1)
                    for name, dst, b_, w in (("sg", SG, W["sgb1"], 64), ("ksk", KG, W["kb"], 128)):
                        ps, done = filled(act, (name, p, th))
                        act.activation(dst[0:w, cols], ps[0:w, 0:HALF], ACT.Gelu, bias=b_[0:w, :]).then_inc(done, 1)
            for p in range(NP):
                for i in range(NJ * p, NJ * p + NJ):
                    emptied(act, ("ao", i))
                for x, dim in ((TC[:, 12 * p:12 * p + 12], "r g h p -> r (g h p)"),
                               (TK[:, NJ * p:NJ * p + NJ], "r j k a p -> r (j k a p)")):
                    x = x.rearrange(dim)
                    act.activation(x, x, ACT.Tanh).then_inc(S["tanh"], 1)
            act.activation(WS, WS, ACT.Sigmoid).then_inc(S["width"], 1)
            act.activation(GA[:, 0, :], GA[:, 1, :], ACT.Sigmoid).then_inc(S["gate"], 1)
            act.wait_ge(S["warg"], 1)
            act.activation(WE, WE, ACT.Exp).then_inc(S["wexp"], 1)
            act.wait_ge(S["tanh"], 2 * NP)
            for p in range(NP):
                for x, y, dim in ((TC[:, 12 * p:12 * p + 12], SC[:, 12 * p:12 * p + 12], "r g h p -> r (g h p)"),
                                  (TK[:, NJ * p:NJ * p + NJ], SK[:, NJ * p:NJ * p + NJ], "r j k a p -> r (j k a p)")):
                    act.activation(y.rearrange(dim), x.rearrange(dim), ACT.Sin, scale=PI_IN).then_inc(S["sines"], 1)
            for p in range(NP):
                act.wait_ge(S["absd"], 2 * (p + 1))
                for x, dim in ((TC[:, 12 * p:12 * p + 12], "r g h p -> r (g h p)"),
                               (TK[:, NJ * p:NJ * p + NJ], "r j k a p -> r (j k a p)")):
                    x = x.rearrange(dim)
                    act.activation(x, x, ACT.Sin, bias=halfpi[0:R, :], scale=-PI).then_inc(S["cosines"], 1)

            def feature_tiles(x):
                for a in range(2):
                    ps, done = filled(act, ("qf", x, a))
                    if x >= 4:
                        k = jobs[("ret", x - 4)]
                        act.wait_ge(full[k % 8], k // 8 + 1)
                    act.activation(QF[:, (2 * x + a) % 8, :], ps[:, 0:2 * R], ACT.Copy).then_inc(done, 1)

            def retrieved_out(x):
                j, p = x // NP, x % NP
                ps, done = filled(act, ("ret", x))
                act.wait_ge(S["ff"], NP)
                act.activation(CO[:, p * NJ + j, :], ps[0:R, 0:128], ACT.Copy).then_inc(done, 1)

            for x in range(NT + 2):
                if x < NT:
                    feature_tiles(x)
                if x >= 2:
                    retrieved_out(x - 2)
            ln_squares(2, lambda p: CO[:, NJ * p:NJ * p + NJ, :].rearrange("r j d -> r (j d)"))
            to_xt("xt4")

            ln_squares(3, xn_flat)
            to_xt("xt5")
            for p in range(NP):
                for th in range(2):
                    name = ("rh", p, th)
                    ps, done = filled(act, name)
                    act.activation(RH[0:64, p * L + th * HALF:p * L + (th + 1) * HALF], ps[0:64, 0:HALF], ACT.Relu,
                                   bias=W["rb1"][0:64, :]).then_inc(done, 1)
            act.wait_ge(S["route1"], 1)
            act.activation(GE, GE, ACT.Exp).then_inc(S["route1_ex"], 1)
            act.wait_ge(S["route1"], 2)
            act.activation(g1[:, 3, :], g1[:, 2, :], ACT.Exp).then_inc(S["route1_ex"], 1)
            act.wait_ge(S["route1"], 3)
            act.activation(g1[:, 5, :], g1[:, 4, :], ACT.Exp).then_inc(S["route1_ex"], 1)

            def hidden_out(layer, x):
                a, p, th, ep = units1[x]
                name = (f"l{layer}", x)
                dst = H1[:, x % 4, :] if layer == 1 else H2[:, ep, p * L + th * HALF:p * L + (th + 1) * HALF]
                b_ = (W["e1b"] if layer == 1 else W["e2b"])[:, ep:ep + 1]
                ps, done = filled(act, name)
                act.activation(dst, ps[:, 0:HALF], ACT.Relu, bias=b_).then_inc(done, 1)

            for x in range(len(units1) + 1):
                if x < len(units1):
                    hidden_out(1, x)
                if x:
                    hidden_out(2, x - 1)

        @block.vector
        def _(dve):
            n_ = [0]

            def link(ins):
                n_[0] += 1
                ins.then_inc(S["dve_chain"], 1)
                dve.wait_ge(S["dve_chain"], n_[0])

            ps, done96 = filled(dve, "w96")
            link(dve.tensor_copy(W96[:, 0:OW + D], ps[0:96, 0:OW + D]))
            dve.tensor_scalar(bn[:, 0, :], W96[:, PAR + 4 * NB:PAR + 5 * NB], EPS, None, ALU.add)\
               .then_inc(S["bn_var"], 1)
            dve.wait_ge(S["consts"], 2)
            wk = W96[:, 0:PAR].rearrange("p (i o k) -> p i o k", i=NB, o=CIN)
            fk = Fw.rearrange("p (i k) c -> p i k c", k=KT)
            for s in range(NS):
                r = slice(32 * s, 32 * s + 32)
                for tap in range(KT):
                    last = dve.tensor_tensor(
                        fk[r, :, tap, 64 + 32 * s:96 + 32 * s].rearrange("p i (b o) -> p i b o", b=B),
                        wk[r, :, :, tap].unsqueeze(2).to_broadcast([32, NB, B, CIN]),
                        bmask[r].unsqueeze(1).unsqueeze(3).to_broadcast([32, NB, B, CIN]), ALU.mult)
            last.then_inc(S["conv_w"], 1)
            dve.wait_ge(S["bn_rstd"], 1)
            link(dve.tensor_tensor(bn[:, 1, :], bn[:, 1, :], W96[:, PAR + NB:PAR + 2 * NB], ALU.mult))
            link(dve.tensor_tensor(bn[:, 0, :], bn[:, 1, :], W96[:, PAR + 3 * NB:PAR + 4 * NB], ALU.mult))
            link(dve.tensor_tensor(bn[:, 2, :], W96[:, PAR + 2 * NB:PAR + 3 * NB], bn[:, 0, :], ALU.subtract))
            dve.sem_inc(S["w96"], 1)
            dve.sem_inc(done96, 1)
            for i in range(NB):
                link(dve.tensor_scalar(xs, xc, bn[:, 2, i:i + 1], None, ALU.add))
                if i == 1:
                    dve.tensor_tensor(Wout, rows(W96[:, OW:OW + D], NS * B), over(m24, NS * B, D), ALU.mult)
                if i == 5:
                    dve.wait_ge(S["dma_prep"], 16 * len(prep))
                    for h2 in range(2):
                        r = slice(64 * h2, 64 * h2 + 64)
                        last = dve.tensor_tensor(vox[r, :, 65 * h2:65 * h2 + D], voload[r, 0], voload[r, 1],
                                                 ALU.subtract)
                    last.then_inc(S["vo_ready"], 1)
                emptied(dve, ("conv", i))
                ins = dve.scalar_tensor_tensor(xc, xr, bn[:, 1, i:i + 1], xs, ALU.mult, ALU.add)
                ins.then_inc(S["conv_x"], 1)
                dve.wait_ge(S["conv_x"], i + 1)
                if i == 6:
                    x0, x1 = phases, trig[:, 0, :]
                    dve.tensor_scalar(x0[:, NJ * PP:], bias[0:R, WD:WD + WN], 0.1, None, ALU.mult)
                    link(dve.tensor_copy(x0[:, 0:NJ * PP], ppx.rearrange("r j p -> r (j p)")))
                    link(dve.tensor_scalar(x1, x0, 1.0 / (2 * np.pi), MAGIC, ALU.mult, ALU.add))
                    link(dve.tensor_scalar(x1, x1, MAGIC, None, ALU.subtract))
                    for c in (C1, C2, C3):
                        link(dve.scalar_tensor_tensor(x0, x1, -c, x0, ALU.mult, ALU.add))
                    link(dve.tensor_scalar(x0, x0, PI_IN, -PI_IN, ALU.min, ALU.max))
                    dve.scalar_tensor_tensor(x1, x0, -1.0, x0, ALU.mult, ALU.max).then_inc(S["trig_r"], 1)
            for half in range(2):
                for s in range(NS):
                    ps, done = filled(dve, ("h0", half, s))
                    for a in range(2):
                        last = dve.tensor_tensor(H[:, :, 2 * s + half, a, :],
                                                 ps[0:R, 256 * a:256 * a + 256].rearrange("r (p d) -> r p d", p=NP),
                                                 rows(outb[:, :], NP), ALU.add)
                    last.then_inc(done, 1)
            k = jobs[("h0", 1, NS - 1)]
            dve.wait_ge(free[k % 8], k // 8 + 1)

            def layer_norm(k, src, dst):
                count = 2 if k == 0 else NP
                for p in range(count):
                    link(dve.reduce_sum(lnst[:, 0, p, :], src(p), AX))
                    link(dve.tensor_scalar(lnst[:, 1, p, :], lnst[:, 0, p, :], -1.0 / D, None, ALU.mult))
                    dve.tensor_tensor(dst(p), src(p), over(lnst[:, 1, p, :], 2 * NJ, D), ALU.add)\
                       .then_inc(S["ln_xc"], 1)
                for p in range(count):
                    dve.wait_ge(S["ln_sq"], ln_base[k] + p + 1)
                    link(dve.reduce_sum(lnst[:, 0, p, :], SQ[:, p % 2, :].rearrange("r (g d) -> r g d", d=D), AX))
                    dve.tensor_scalar(lnst[:, 2, p, :], lnst[:, 0, p, :], 1.0 / D, EPS, ALU.mult, ALU.add)\
                       .then_inc(S["ln_var"], 1)
                for p in range(count):
                    dve.wait_ge(S["ln_rstd"], ln_base[k] + p + 1)
                    dve.tensor_tensor(dst(p), dst(p), over(lnst[:, 3, p, :], 2 * NJ, D), ALU.mult)\
                       .then_inc(S["xn"], 1)

            hp_, xp_ = (lambda p: pairs(H, p)), (lambda p: pairs(XN, p))
            dve.wait_ge(S["xbuf_zero"], 16 * E0)
            layer_norm(0, hp_, xp_)

            for job in order:
                if job in ring_at:
                    k = ring_at[job]
                    ps = ring_bank[k % 2]
                    dve.wait_ge(S["ring_full"], k + 1)
                if job[0] == "score":
                    _, n, i = job
                    dve.reduce_max(MX[:, n % 2, i:i + 1], ps[0:R, 0:HALF], AX).then_inc(S["ring_free"], 1)
                    if i == 23:
                        dve.wait_ge(S["ring_free"], k + 1)
                        if n >= 2:
                            dve.wait_ge(S["shift_in"], n - 1)
                        dve.reduce_max(M1[:, n % 2, :], MX[:, n % 2, :].rearrange("r (t h) -> r t h", h=2), AX)\
                           .then_inc(S["mx_neg"], 1)
                elif job[0] == "proj":
                    _, b, g, qk, th = job
                    q = nproj[job]
                    dve.wait_ge(S["split1"], q + 1)
                    if q >= 2:
                        dve.wait_ge(S["split3"], q - 1)
                    dve.scalar_tensor_tensor(RR[:, q % 2, :], ps[:, 0:HALF], 0.125 if qk == 0 else 1.0,
                                             SP[:, qk, 0, th * HALF:(th + 1) * HALF], ALU.mult, ALU.subtract)\
                       .then_inc(S["ring_free"], 1)
                elif job[0] == "shift":
                    n = job[1]
                    if n >= 2:
                        dve.wait_ge(S["shift_dma"], 48 * (n - 1))
                    dve.tensor_copy(MT[:, n % 2, 0:R], ps[0:36, 0:63].bitcast(BF16)[:, 0:R]).then_inc(S["ring_free"], 1)
                elif job[0] == "xt":
                    _, which, b, h = job
                    p, a = b % NP, b // NP
                    r = slice(0, 128) if which == 1 else slice(64 * a, 64 * a + 64)
                    dve.tensor_copy(XT[r, p * L + h * HALF:p * L + (h + 1) * HALF], ps[r, 0:HALF])\
                       .then_inc(S["ring_free"], 1)
                elif job[0] == "logits":
                    dve.tensor_tensor(LG, ps[0:R, 0:NJ * E0].rearrange("r (g e) -> r g e", e=E0),
                                      rows(bias[0:R, GB:GB + E0], NJ), ALU.add).then_inc(S["ring_free"], 1)
                    dve.wait_ge(S["ring_free"], k + 1)
                elif job[0] == "choose":
                    link(dve.reduce_max(mx, LG, AX))
                    dve.tensor_tensor(LD, LG, over(mx, NJ, E0), ALU.subtract).then_inc(S["route_ld"], 1)
                    link(dve.tensor_tensor(EQ, LG, over(mx, NJ, E0), ALU.is_equal))
                    link(dve.tensor_tensor(EQ, EQ, rows(iota8, NJ), ALU.mult))
                    link(dve.tensor_reduce(im, EQ, AX, ALU.min))
                    dve.tensor_tensor(OH, rows(iota8, NJ), over(im, NJ, E0), ALU.is_equal).then_inc(S["onehot"], 1)
                elif job[0] == "pos":
                    b = job[1]
                    link(dve.tensor_tensor(PX, ps[0:R, 0:NJ * E0].rearrange("r (g e) -> r g e", e=E0), OH, ALU.mult))
                    dve.sem_inc(S["ring_free"], 1)
                    dve.wait_ge(S["route_ex"], b + 1)
                    dve.reduce_sum(pos, PX, AX)
                    link(dve.reduce_sum(sums, LD, AX))
                    dve.reciprocal(prob[:, NJ * b:NJ * b + NJ], sums).then_inc(S["pos_ready"], 1)
                elif job[0] == "ln_mean":
                    b = job[2]
                    if job[1] == 2:
                        dve.wait_ge(S["att_h"], NJ * (b + 1))
                    dve.reduce_sum(lnb[:, 0, :], H[:, b % NP, :, b // NP, :], AX).then_inc(S["lnb_sum"], 1)
                elif job[0] == "ln_std":
                    dve.wait_ge(S["lnb_x"], ln_at[job[1:3]] + 1)
                    dve.reduce_sum(lnb[:, 2, :], XSQ, AX).then_inc(S["lnb_ssq"], 1)
                elif job[0] == "out":
                    _, b, j, h = job
                    p, a = b % NP, b // NP
                    v = ps[0:R, 0:260].rearrange("r (h c) -> r h c", c=D + 1)
                    link(dve.reciprocal(RD[:, h, :].unsqueeze(2), v[:, :, D:D + 1]))
                    dve.tensor_tensor(OT[:, 4 * h:4 * h + 4, :], v[:, :, 0:D], over(RD[:, h, :], 4, D), ALU.mult)\
                       .then_inc(S["ring_free"], 1)
                    if h == 1:
                        dve.wait_ge(S["ring_free"], k + 1)
                        link(dve.reduce_sum(OR, OT.rearrange("r h d -> r d h"), AX))
                        dve.tensor_tensor(H[:, p, j, a, :], H[:, p, j, a, :], OR, ALU.add).then_inc(S["att_h"], 1)
            dve.wait_ge(S["att_h"], NJ * B)

            def copy_out(name, dst):
                ps, done = filled(dve, name)
                k = jobs[name]
                dve.tensor_copy(dst, ps[0:dst.shape[0], 0:dst.shape[1]]).then_inc(done, 1)

            for e in range(4):
                copy_out(("xbt", e, 1), XBT[:, e, 4 * R:8 * R])
            for kind, e in ffn_order:
                if kind == "h1":
                    for a in range(2):
                        for nn in range(2):
                            name = ("h1", e, a, 1, nn)
                            ps, done = filled(dve, name)
                            i = 2 * (e + 4 * a) + 1
                            dve.tensor_scalar(HM[:, e % 2, a, 1, nn * CH:(nn + 1) * CH], ps[:, 0:CH],
                                              W["b1"][:, i:i + 1], 0.0, ALU.add, ALU.max).then_inc(done, 1)
                elif kind == "yb":
                    copy_out(("yb", e, 1), XB[:, e, 4:8, :].rearrange("r c d -> r (c d)"))
            dve.wait_ge(S["big"], 2)
            for p in range(NP):
                dve.wait_ge(gathered[p], 16 * 12)
                y = YG[:, 12 * p:12 * p + 12, :]
                yf = y.rearrange("r g d -> r (g d)")
                w = pk.rearrange("r (a n j) -> r a n j", a=2, n=NP)[:, :, p, :].rearrange("r a j -> r j a")
                y4 = y.rearrange("r (j a) d -> r j a d", a=2)
                link(dve.tensor_tensor(y4, y4, w.unsqueeze(3).to_broadcast([R, NJ, 2, D]), ALU.mult))
                link(dve.tensor_scalar(msk[:, 0, :], yf, 3.4028235e38, None, ALU.is_gt))
                link(dve.copy_predicated(yf, mski[0], big[:, 0, :]))
                link(dve.tensor_scalar(msk[:, 0, :], yf, -3.4028235e38, None, ALU.is_lt))
                link(dve.copy_predicated(yf, mski[0], big[:, 1, :]))
                link(dve.tensor_tensor(msk[:, 1, :], yf, yf, ALU.not_equal))
                link(dve.copy_predicated(yf, mski[1], zero1[0:R, 0:1].to_broadcast([R, 768])))
                link(dve.tensor_tensor(pairs(H, p), pairs(H, p), y, ALU.add))

            layer_norm(1, hp_, xp_)
            dve.wait_ge(S["pos"], 1)
            link(dve.reciprocal(pos1, pos1))
            for p in range(NP):
                emptied(dve, ("xt3", p, 0))
                emptied(dve, ("xt3", p, 1))
                cols = slice(p * L, (p + 1) * L)
                link(dve.tensor_tensor_scan(CX[:, cols], ones[:, 0:1].to_broadcast([128, L]), XT[:, cols], 0.0, ALU.mult, ALU.add))
                dve.tensor_tensor(CX[:, cols], CX[:, cols], pos1, ALU.mult).then_inc(S["cx"], 1)
                for th in range(2):
                    ps, done = filled(dve, ("hop", p, th))
                    if p:
                        dve.wait_ge(S["hop_act"], 2 * (p - 1) + th + 1)
                    k = jobs[("hop", p, th)]
                    dve.tensor_tensor(HT[:, th, :], ps[:, 0:HALF], PPF[:, th * HALF:(th + 1) * HALF], ALU.add)\
                       .then_inc(done, 1)
            for i in range(NT):
                ps, done = filled(dve, ("tok", i))
                dve.tensor_tensor(CV[:, i].rearrange("r a c d -> r (a c d)"), ps[0:R, 0:256],
                                  bias[0:R, CVB:CVB + 256], ALU.add)
                dve.tensor_tensor(TK[:, i].rearrange("r k a p -> r (k a p)"), ps[0:R, 256:384],
                                  bias[0:R, KSB:KSB + 128], ALU.add)
                dve.tensor_tensor(GA[:, 1, 2 * i:2 * i + 2], ps[0:R, 384:386], bias[0:R, GTB:GTB + 2], ALU.add)\
                   .then_inc(done, 1)
                ps, done = filled(dve, ("ao", i))
                v = ps[0:R, 0:264].rearrange("r (g c) -> r g c", c=PP + 1)
                bv = bias[0:R, AOB:AOB + 264].rearrange("r (g c) -> r g c", c=PP + 1)
                dve.tensor_tensor(TC[:, 2 * i:2 * i + 2].rearrange("r g h p -> r (g h) p"), v[:, :, 0:PP],
                                  bv[:, :, 0:PP], ALU.add)
                dve.tensor_tensor(WS[:, 8 * i:8 * i + 8].unsqueeze(2), v[:, :, PP:], bv[:, :, PP:], ALU.add)\
                   .then_inc(done, 1)
            G4 = NG * PH
            link(dve.tensor_tensor(hdl, bias[0:R, WD:WD + WN], bias[0:R, WD:WD + WN], ALU.mult))
            link(dve.tensor_scalar(hdl, hdl, -0.5, None, ALU.mult))
            dve.wait_ge(S["width"], 1)
            link(dve.tensor_scalar(WS, WS, 2.0, 0.1, ALU.mult, ALU.add))
            link(dve.tensor_tensor(WS, WS, WS, ALU.mult))
            link(dve.tensor_scalar(WS, WS, 1e-6, None, ALU.add))
            link(dve.reciprocal(WS, WS))
            dve.tensor_tensor(WE, over(WS, G4, WN), rows(hdl, G4), ALU.mult).then_inc(S["warg"], 1)
            dve.wait_ge(S["wexp"], 1)
            for i in range(2):
                link(dve.tensor_tensor(WX, WE, rows(trig[:, i, NJ * PP:], G4), ALU.mult))
                link(dve.reduce_sum(WA[:, i, :], WX, AX))
            link(dve.reduce_sum(WA[:, 2, :], WE, AX))
            link(dve.tensor_scalar(WA[:, 2, :], WA[:, 2, :], 1e-6, None, ALU.add))
            link(dve.reciprocal(WA[:, 2, :], WA[:, 2, :]))
            link(dve.tensor_scalar(WA[:, 2, :], WA[:, 2, :], RS / PH, None, ALU.mult))
            for i in range(2):
                last = dve.tensor_tensor(WA[:, i, :], WA[:, i, :], WA[:, 2, :], ALU.mult)
            link(last)
            dve.sem_inc(S["wab"], 1)
            ps, done = filled(dve, "gcum")
            ps2, done2 = filled(dve, "gtot")
            link(dve.tensor_copy(GA[:, 2, :], ps2[0:R, 0:NG]))
            dve.sem_inc(done2, 1)
            tot, pre = (GA[:, i, :].rearrange("r (p j a) -> r p j a", p=NP, a=2) for i in (2, 3))
            link(dve.memset(GA[:, 3, :], 0.0))
            for j in range(1, NJ):
                link(dve.tensor_tensor(pre[:, :, j, :], pre[:, :, j - 1, :], tot[:, :, j - 1, :], ALU.add))
            link(dve.tensor_tensor(GA[:, 4, :], ps[0:R, 0:NG], GA[:, 3, :], ALU.add))
            dve.sem_inc(done, 1)
            dve.tensor_scalar(GA[:, 4, :], GA[:, 4, :], 1.0, None, ALU.max).then_inc(S["gc"], 1)
            for p in range(NP):
                dve.wait_ge(S["sines"], 2 * (p + 1))
                for x, dim in ((TC[:, 12 * p:12 * p + 12], "r g h p -> r (g h p)"),
                               (TK[:, NJ * p:NJ * p + NJ], "r j k a p -> r (j k a p)")):
                    x = x.rearrange(dim)
                    dve.scalar_tensor_tensor(x, x, -1.0, x, ALU.mult, ALU.max).then_inc(S["absd"], 1)
            for p in range(NP):
                g = slice(12 * p, 12 * p + 12)
                dve.wait_ge(S["cosines"], 2 * (p + 1))
                cc, sc = (x[:, g].rearrange("r g h p -> r (g h) p") for x in (TC, SC))
                wa, wb = (over(WA[:, i, 48 * p:48 * p + 48], 48, PP) for i in range(2))
                p0, p1 = (PT[:, i].rearrange("r g h p -> r (g h) p") for i in (0, 1))
                dve.tensor_tensor(p0, cc, wa, ALU.mult)
                link(dve.tensor_tensor(p1, sc, wb, ALU.mult))
                dve.sem_inc(S["prod"], 1)
                link(dve.tensor_tensor(p0, p0, p1, ALU.subtract))
                dve.reduce_sum(UV[:, 0], PT[:, 0].rearrange("r g h p -> r g p h"), AX)
                dve.wait_ge(S["vsum"], p + 1)
                link(dve.reduce_sum(UV[:, 1], PT[:, 2].rearrange("r g h p -> r g p h"), AX))
                dve.sem_inc(S["uv"], 1)
                u, w = (UV[:, i].rearrange("r (j a) p -> r j a p", a=2) for i in (0, 1))
                t0, t1 = (UT[:, i].rearrange("r (j a) p -> r j a p", a=2) for i in (0, 1))
                cp, sp_ = (trig[:, i, 0:NJ * PP].rearrange("r (j p) -> r j p", p=PP).unsqueeze(2)
                           .to_broadcast([R, NJ, 2, PP]) for i in (0, 1))
                qc, qs = (QQ[:, g, 32 * i:32 * i + 32].rearrange("r (j a) p -> r j a p", a=2) for i in (0, 1))
                dve.tensor_tensor(t0, u, cp, ALU.mult)
                link(dve.tensor_tensor(t1, w, sp_, ALU.mult))
                link(dve.tensor_tensor(qc, t0, t1, ALU.subtract))
                dve.tensor_tensor(t0, u, sp_, ALU.mult)
                link(dve.tensor_tensor(t1, w, cp, ALU.mult))
                dve.tensor_tensor(qs, t0, t1, ALU.add).then_inc(S["qf_ready"], 1)

            dve.wait_ge(S["uv"], NP)
            mask = triu[0:R, 0:R].unsqueeze(1).to_broadcast([R, 2, R])
            for x in range(NT):
                j, p = x // NP, x % NP
                for k2 in range(2):
                    ps, done = filled(dve, ("sm", x, k2))
                    if x >= 4 and k2 == 0:
                        k = jobs[("ret", x - 4)]
                        dve.wait_ge(full[k % 8], k // 8 + 1)
                    dve.tensor_tensor(SM[:, x % 4, k2], ps[0:R, 0:2 * R].rearrange("r (a c) -> r a c", a=2), mask,
                                      ALU.mult).then_inc(done, 1)
                if j < NJ - 1:
                    ps, done = filled(dve, ("state", x))
                    for c in range(2):
                        r = slice(64 * c, 64 * c + 64)
                        delta = ps[r, 0:256].rearrange("r (a c d) -> r a c d", a=2, c=2)[:, :, c, :]
                        if j == 0:
                            ins = dve.tensor_copy(ST[r, 1, p], delta)
                        else:
                            ins = dve.tensor_tensor(ST[r, j + 1, p], ST[r, j, p], delta, ALU.add)
                        ins.then_inc(S["state"], 1)
                    dve.wait_ge(S["state"], 2 * (x + 1))
                    dve.sem_inc(done, 1)
            for x in range(NT - 8, NT):
                emptied(dve, ("ret", x))
            co_ = lambda p: CO[:, NJ * p:NJ * p + NJ, :].rearrange("r j (a d) -> r (j a) d", a=2)
            layer_norm(2, co_, co_)
            for p in range(NP):
                for h in range(2):
                    ps, done = filled(dve, ("o1", p, h))
                    dve.wait_ge(S["h_pre"], p + 1)
                    v = H[:, p, 3 * h:3 * h + 3].rearrange("r j a d -> r (j a d)")
                    k = jobs[("o1", p, h)]
                    dve.tensor_tensor(v, v, ps[0:R, 0:3 * 128], ALU.add).then_inc(done, 1)
                    dve.wait_ge(free[k % 8], k // 8 + 1)

            layer_norm(3, hp_, xp_)
            ps, done = filled(dve, "logits1")
            link(dve.tensor_tensor(GL, ps[0:R, 0:NG * E1].rearrange("r (g e) -> r g e", e=E1),
                                   rows(bias[0:R, RB2:RB2 + E1], NG), ALU.add))
            dve.sem_inc(done, 1)
            m1, i1, d2, x2, ww, w1_, m2, t2 = (g1[:, i, :] for i in range(8))
            i6 = rows(iota8[:, 0:E1], NG)
            link(dve.reduce_max(m1, GL, AX))
            dve.tensor_tensor(GE, GL, over(m1, NG, E1), ALU.subtract).then_inc(S["route1"], 1)
            link(dve.tensor_tensor(GC, GL, over(m1, NG, E1), ALU.is_equal))
            link(dve.tensor_tensor(GC, GC, i6, ALU.mult))
            link(dve.tensor_reduce(i1, GC, AX, ALU.min))
            link(dve.tensor_tensor(GO, i6, over(i1, NG, E1), ALU.is_equal))
            link(dve.scalar_tensor_tensor(GC, GO, -3.0e38, GL, ALU.mult, ALU.add))
            link(dve.reduce_max(m2, GC, AX))
            dve.tensor_tensor(d2, m2, m1, ALU.subtract).then_inc(S["route1"], 1)
            link(dve.tensor_tensor(GC, GC, over(m2, NG, E1), ALU.is_equal))
            link(dve.tensor_tensor(GC, GC, i6, ALU.mult))
            link(dve.tensor_reduce(i1, GC, AX, ALU.min))
            link(dve.tensor_tensor(GW, i6, over(i1, NG, E1), ALU.is_equal))
            dve.wait_ge(S["route1_ex"], 2)
            link(dve.reduce_sum(t2, GE, AX))
            link(dve.reciprocal(t2, t2))
            link(dve.tensor_scalar(x2, x2, 1.0, None, ALU.subtract))
            dve.tensor_tensor(ww, x2, t2, ALU.mult).then_inc(S["route1"], 1)
            dve.wait_ge(S["route1_ex"], 3)
            link(dve.tensor_scalar(t2, w1_, 1.0, None, ALU.add))
            link(dve.reciprocal(t2, t2))
            link(dve.tensor_tensor(w1_, w1_, t2, ALU.mult))
            dve.tensor_tensor(GO, GO, over(t2, NG, E1), ALU.mult)
            link(dve.tensor_tensor(GW, GW, over(w1_, NG, E1), ALU.mult))
            link(dve.tensor_tensor(GW, GW, GO, ALU.add))
            x = 0
            for a in range(2):
                for p in range(NP):
                    for j in range(NJ):
                        ps, done = filled(dve, ("l3", a, p, j))
                        k = jobs[("l3", a, p, j)]
                        yo = YO[:, x % 2]
                        dve.tensor_tensor(yo, ps[0:R, 0:384].rearrange("r (e d) -> r e d", e=E1),
                                          bias[0:R, EB3:EB3 + 384].rearrange("r (e d) -> r e d", e=E1), ALU.add)\
                           .then_inc(done, 1)
                        dve.wait_ge(free[k % 8], k // 8 + 1)
                        g = (p * NJ + j) * 2 + a
                        link(dve.tensor_tensor(yo, yo, over(GW[:, g, :], E1, D), ALU.mult))
                        link(dve.reduce_sum(YR[:, x % 2, :], yo.rearrange("r e d -> r d e"), AX))
                        dve.tensor_tensor(H[:, p, j, a, :], H[:, p, j, a, :], YR[:, x % 2, :], ALU.add)\
                           .then_inc(S["h4"], 1)
                        x += 1


_INS = ['x', 'L0_tok_conv_w', 'L0_tok_conv_b', 'L0_tok_bn_gamma', 'L0_tok_bn_beta', 'L0_tok_bn_mean',
        'L0_tok_bn_var', 'L0_tok_out_w', 'L0_tok_out_b', 'L0_attn_Q', 'L0_attn_K', 'L0_attn_VO',
        'L0_ffn_gate_w', 'L0_ffn_gate_b', 'L0_ffn_w1', 'L0_ffn_b1', 'L0_ffn_w2', 'L0_ffn_b2',
        'L1_attn_pos_phases', 'L1_attn_window_deltas', 'L1_attn_mc_w', 'L1_attn_mc_b', 'L1_attn_hop_w1',
        'L1_attn_hop_b1', 'L1_attn_hop_w2', 'L1_attn_hop_b2', 'L1_attn_cpe_w', 'L1_attn_cpe_b', 'L1_attn_ve_w',
        'L1_attn_ve_b', 'L1_attn_kce_w', 'L1_attn_kce_b', 'L1_attn_ksk_w1', 'L1_attn_ksk_b1', 'L1_attn_ksk_w2',
        'L1_attn_ksk_b2', 'L1_attn_sg_w1', 'L1_attn_sg_b1', 'L1_attn_sg_w2', 'L1_attn_sg_b2', 'L1_attn_ln_g',
        'L1_attn_ln_b', 'L1_attn_out_w', 'L1_attn_out_b', 'L1_ffn_router_w1', 'L1_ffn_router_b1',
        'L1_ffn_router_w2', 'L1_ffn_router_b2', 'L1_ffn_expert_w1', 'L1_ffn_expert_b1', 'L1_ffn_expert_w2',
        'L1_ffn_expert_b2', 'L1_ffn_expert_w3', 'L1_ffn_expert_b3']


def kernel(**inputs):
    import concourse.bacc as bacc
    from concourse.bass_utils import run_bass_kernel_spmd

    nc = bacc.Bacc("TRN2", target_bir_lowering=False, num_devices=1)
    arrays, args = {}, {}
    for name in _INS:
        a = np.ascontiguousarray(inputs[name])
        arrays[f"in_{name}"] = a
        args[name] = nc.dram_tensor(f"in_{name}", a.shape, mybir.dt.from_np(a.dtype), kind="ExternalInput").ap()
    out = nc.dram_tensor("out_0", (B, L, D), F32, kind="ExternalOutput").ap()
    build(nc, args, out)
    r = run_bass_kernel_spmd(nc, [arrays], core_ids=[0])
    return r.results[0]["out_0"]
```

```python
from contextlib import ExitStack

import concourse.bass as bass
import numpy as np
from concourse import mybir

F32 = mybir.dt.float32
BF16 = mybir.dt.bfloat16
U32 = mybir.dt.uint32
ALU = mybir.AluOpType
ACT = mybir.ActivationFunctionType
AX = mybir.AxisListType.X

B, CIN, L, D = 8, 4, 750, 64
NP, NJ, R = 4, 6, 125
NT, NG = NP * NJ, NP * NJ * 2
HALF = L // 2
NB, KT = 9, 3
NS, SEG = 3, 250
HEADS, QR = 8, 32
E0, F0 = 8, 256
CAP = -(-(5 * B * L) // (4 * E0))
CH = CAP // 2
ROWS = 1000
PH, PP, WN = 4, 32, 5
E1 = 6
EPS = 1e-5
PI_IN = 3.1415925
PI = float(np.float32(np.pi))
MAGIC = 12582912.0
C1 = 6.28125
C2 = 0.0019350051879882812
C3 = 2 * np.pi - C1 - C2
RS = 1.0 / np.sqrt(float(PP))

GB, CVB, KSB, GTB, AOB, LNG, LNB, OB, RB2, EB3, WD = (
    0, 8, 264, 392, 394, 658, 722, 786, 850, 856, 1240)
NBIAS = 1245


def build(nc, t, out):
    with ExitStack() as ctx:
        ctx.enter_context(nc.allow_non_contiguous_dma(reason="small weights are laid out on their way in"))
        def sb(name, shape, dt=F32):
            return ctx.enter_context(nc.sbuf_tensor(name, shape, dt))[tuple(slice(None) for _ in shape)]

        psum = ctx.enter_context(nc.psum_tensor("psum", [128, 8, 512], F32))
        bank = [psum[:, i, :] for i in range(8)]
        xbuf = nc.dram_tensor("expert_in", [E0 * ROWS, D], F32, kind="Internal").ap()
        ybuf = nc.dram_tensor("expert_out", [E0 * ROWS, D], F32, kind="Internal").ap()

        H = sb("H", [R, NP, NJ, 2, D])
        XN = sb("XN", [R, NP, NJ, 2, D])
        XT = sb("XT", [128, NP * L])
        ident = sb("ident", [128, 128])
        identb = sb("identb", [128, 128], BF16)
        triu = sb("triu", [128, 128])
        ones = sb("ones", [128, 128])
        mhalf = sb("mhalf", [128, 64])
        zero1 = sb("zero1", [128, 1])
        lnst = sb("lnst", [R, 4, NP, 2 * NJ])
        bias = sb("bias", [128, NBIAS])
        iota8 = sb("iota8", [R, 8])
        trig = sb("trig", [R, 2, NJ * PP + WN])
        halfpi = sb("halfpi", [128, 1])

        WCOLS = [("gw", 16), ("hop1", 128), ("hop2", 264), ("wta", 320), ("ksk1", 128), ("ksm", 128), ("sg1", 64), ("ksk2", 64), ("sg2", 2), ("outw", 128),
                 ("rw1", 64), ("rw2", 12), ("b1", 16), ("b2", 4), ("e1b", 3), ("e2b", 3), ("kb", 1), ("sgb1", 1),
                 ("hopb", 1), ("rb1", 1)]
        wall = sb("wall", [128, sum(n for _, n in WCOLS)])
        W, at = {}, 0
        for name, n in WCOLS:
            W[name] = wall[:, at:at + n]
            at += n
        qkp = sb("qkp", [128, 2, 2, HEADS * QR])
        vox = sb("vox", [128, 4, 130])
        slot_in = sb("slot_in", [R, NG], U32)
        slot_out = sb("slot_out", [R, NG], U32)
        prob = sb("prob", [R, NG])
        pk = sb("pk", [R, NG])

        ASIZE = 37660
        arena = sb("arena", [128, ASIZE])

        def view(at, shape, dt=F32, parts=128):
            n = int(np.prod(shape))
            w = n if dt != BF16 else (n + 1) // 2
            assert at + w <= ASIZE, (at, shape)
            v = arena[0:parts, at:at + w]
            if dt != F32:
                v = v.bitcast(dt)
            if len(shape) > 1:
                dims = [f"d{i}" for i in range(len(shape))]
                v = v.rearrange(f"p ({' '.join(dims)}) -> p {' '.join(dims)}", **dict(zip(dims[1:], shape[1:])))
            return v, at + w

        Fw, at = view(0, [NB * KT, 160], parts=96)
        Wout, at = view(at, [NS * B, D], parts=96)
        P4, at = view(at, [256], parts=4)
        W96, at = view(at, [256], parts=96)
        xc, at = view(at, [SEG], parts=96)
        xs, at = view(at, [SEG], parts=96)
        xr, at = view(at, [SEG], parts=96)
        bmask, at = view(at, [B], parts=96)
        m24, at = view(at, [NS * B], parts=96)
        R4, at = view(at, [96], parts=4)
        bn, at = view(at, [3, NB], parts=96)
        ppt, at = view(at, [NJ * R], parts=PP)
        outb, at = view(at, [D], parts=R)
        phases, at = view(at, [NJ * PP + WN], parts=R)
        ppx, at = view(at, [NJ, PP], parts=R)
        qload, at = view(at, [2, 2, 192])
        voload, at = view(at, [2, 4, D])
        early = [("hop1b", 128), ("kskb", 128), ("kcet", 128), ("kce", 64), ("kb1", 1), ("kceb", 1)]
        wearly, at = view(at, [sum(n for _, n in early)])
        col = 0
        for name, n in early:
            W[name] = wearly[:, col:col + n]
            col += n
        zeros = XN[:, 0].rearrange("r j a d -> r (j a d)")[:, 0:512]
        PAR, OW = NB * CIN * KT, NB * CIN * KT + 5 * NB
        SQ, at_sq = view(ASIZE - 2 * 768, [2, 768], parts=R)
        assert at <= ASIZE - 2 * 768
        PPF = sb("PPF", [128, L])

        QA, at = view(0, [2, HEADS, L], BF16)
        QB, at = view(at, [2, HEADS, L], BF16)
        KA, at = view(at, [2, HEADS, L], BF16)
        KB, at = view(at, [2, HEADS, L], BF16)
        SP, at = view(at, [2, 3, L], BF16)
        RR, at = view(at, [2, HALF])
        CT, at = view(at, [2, 4, L])
        PR, at = view(at, [4, L], parts=R)
        MX, at = view(at, [2, 24], parts=R)
        M1, at = view(at, [2, 12], parts=R)
        MR, at = view(at, [2, 12], parts=R)
        NM, at = view(at, [2, 36], BF16, parts=R)
        MT, at = view(at, [2, 126], BF16, parts=36)
        RD, at = view(at, [2, 4], parts=R)
        OT, at = view(at, [8, D], parts=R)
        OR, at = view(at, [D], parts=R)
        XSQ, at = view(at, [NJ, D], parts=R)
        lnb, at = view(at, [4, NJ], parts=R)
        LG, at = view(at, [NJ, E0], parts=R)
        LD, at = view(at, [NJ, E0], parts=R)
        EQ, at = view(at, [NJ, E0], parts=R)
        OH, at = view(at, [NJ, E0], parts=R)
        SO, at = view(at, [NJ + 1, E0], parts=R)
        PX, at = view(at, [NJ, E0], parts=R)
        r1, at = view(at, [9, NJ], parts=R)

        w1p, at = view(0, [E0, F0])
        w2e, at = view(at, [E0, 2, D])
        XB, at = view(at, [4, 8, 128], parts=R)
        XBT, at = view(at, [4, ROWS])
        HM, at = view(at, [2, 2, 2, CAP])
        YT, at = view(at, [4, ROWS])
        YG, at = view(28860, [NG, D], parts=R)
        big, at = view(at, [2, 768], parts=R)
        msk, at = view(at, [2, 768], parts=R)
        mski = [msk[:, i, :].bitcast(U32) for i in range(2)]
        assert at <= ASIZE - 2 * 768

        HG, at = view(0, [NP * L])
        KG, at = view(at, [NP * L])
        SG, at = view(at, [NP * L])
        CX, at = view(at, [NP * L])
        CV, at = view(at, [NT, 2, 2, D], parts=R)
        TC, at = view(at, [NG, PH, PP], parts=R)
        TK, at = view(at, [NT, 2, 2, PP], parts=R)
        SC, _ = view(0, [NG, PH, PP], parts=R)
        SK, _ = view(6144, [NT, 2, 2, PP], parts=R)
        QF, _ = view(9216, [8, 2 * R])
        QQ = TC.rearrange("r g h p -> r g (h p)")
        FF = SC.rearrange("r g h p -> r g (h p)")
        CO = TK.rearrange("r n k a p -> r n (k a p)")
        t_end = at
        PT, at = view(t_end, [2, 4, 4, PH, PP], parts=R)
        UV, at = view(at, [2, 4, PP], parts=R)
        UT, at = view(at, [2, 4, PP], parts=R)
        SM, at = view(at, [4, 2, 2, R], parts=R)
        ST, at = view(at, [2, NJ, 2, D])
        WE, at_ = view(9216, [NG * PH, WN], parts=R)
        WX, at_ = view(at_, [NG * PH, WN], parts=R)
        hdl, at_ = view(9216 + 2000, [WN], parts=R)
        WA, at_ = view(at_, [3, NG * PH], parts=R)
        assert at_ <= 4 * NP * L
        GA, at = view(at, [6, NG], parts=R)
        WS, at = view(at, [NG * PH], parts=R)
        assert at <= ASIZE - 2 * 768, at
        pos1, _ = view(t_end, [L])
        HT, _ = view(t_end + L, [2, HALF])

        e1w, at = view(0, [2, 3, 128])
        e2w, at = view(at, [3, 128])
        e3w, at = view(at, [3, 128])
        RH, at = view(at, [NP * L])
        H1, at = view(at, [4, HALF])
        H2, at = view(at, [3, NP * L])
        GL, at = view(at, [NG, E1], parts=R)
        GE, at = view(at, [NG, E1], parts=R)
        GO, at = view(at, [NG, E1], parts=R)
        GC, at = view(at, [NG, E1], parts=R)
        GW, at = view(at, [NG, E1], parts=R)
        g1, at = view(at, [8, NG], parts=R)
        YO, at = view(at, [2, 6, D], parts=R)
        YR, at = view(at, [2, D], parts=R)
        assert at <= ASIZE - 2 * 768, at

        S = {}

        def sem(*names):
            for n in names:
                S[n] = ctx.enter_context(nc.semaphore(n))

        sem(*[f"bank_full{i}" for i in range(8)], *[f"bank_free{i}" for i in range(8)])
        sem(*[f"{what}{k}" for k in range(4) for what in ("centred", "squared", "variance", "rstd", "normed")])
        sem("dve_chain", "act_chain", "pool_chain")
        sem("zeroed", "dma_conv", "dma_weights", "consts", "w96", "conv_w", "bn_var", "bn_rstd", 
            "conv_x", "vo_ready", "xbuf_zero",
            "ppt", "ppf", "trig_r", "trig_done")
        sem("ring_full", "ring_free", "split1", "resid", "split2", "split3", "qk_dma0", "qk_dma1", "kb_ones", "v_ready",
            "mx_half", "mx_neg", "shift_in", "shift_out", "shift_dma", "st_done", "exp_done", "pv_done", "ctx_out",
            "att_h", "lnb_sum", "lnb_x", "lnb_ssq", "lnb_done", "onehot_sum", "pos_ready", "big_set", "dma_prep")
        sem("late_zero", "w_late", "big", "route_ld", "route_ex", "onehot", "slots", "scattered", "xb_loaded",
            "y_stored", "gathered0", "gathered1", "gathered2", "gathered3",
            "pos", "cx", "hop_act", "tanh", "width", "gate", "warg", "wexp", "wab", "gc", "rg", "sines", "absd",
            "cosines", "prod", "vsum", "uv", "qf_ready", "ff", "state", "h_pre", "lnx",
            "route1", "route1_ex", "h4", "stored")
        gathered = [S["gathered0"], S["gathered1"], S["gathered2"], S["gathered3"]]
        full = [S[f"bank_full{i}"] for i in range(8)]
        free = [S[f"bank_free{i}"] for i in range(8)]

        jobs = {}

        def take(pe, name):
            k = len(jobs)
            jobs[name] = k
            if k >= 8:
                pe.wait_ge(free[k % 8], k // 8)
            return bank[k % 8], full[k % 8]

        def filled(eng, name):
            k = jobs[name]
            eng.wait_ge(full[k % 8], k // 8 + 1)
            return bank[k % 8], free[k % 8]

        def emptied(eng, name):
            k = jobs[name]
            eng.wait_ge(free[k % 8], k // 8 + 1)

        def pairs(buf, p):
            return buf[:, p].rearrange("r j a d -> r (j a) d")

        def over(ap, n, width):
            return ap.unsqueeze(2).to_broadcast([ap.shape[0], n, width])

        def rows(ap, n):
            return ap.unsqueeze(1).to_broadcast([ap.shape[0], n, ap.shape[1]])

        taps = []
        for i in range(NB):
            mm = [(2, 0, 0, SEG, 0)]
            for tap, shift in ((1, 2 ** i), (0, 2 ** (i + 1))):
                q, r = divmod(shift, SEG)
                if q < NS:
                    mm.append((tap, q, r, SEG, 0))
                if q + 1 < NS and r:
                    mm.append((tap, q + 1, 0, r, SEG - r))
            taps.append(mm)

        NU = 4 * B
        mx, im, pos, sums, kept, sl, sx, tx, sy = (r1[:, i, :] for i in range(9))
        front = [("gathered", 0), ("centre", 0), ("gathered", 1), ("centre", 1)]
        for p in range(NP):
            front += [("variance", p), ("normalize", p), ("transpose", p), ("mean", p), ("hidden", p)]
            if p:
                front.append(("tokens", p - 1))
            if p + 2 < NP:
                front += [("gathered", p + 2), ("centre", p + 2)]
        front.append(("tokens", NP - 1))
        NC = NT // 2
        back = [("chunk", 0), ("chunk", 1)]
        for x in range(NT + 13):
            if x < NT and x % 2 == 0 and x // 2 + 2 < NC:
                back.append(("chunk", x // 2 + 2))
            if x < NT:
                back.append(("features", x))
            if 1 <= x <= NT:
                back.append(("masked", x - 1))
            if 2 <= x < NT + 2:
                back.append(("retrieved", x - 2))
            for p in range(NP):
                k = x - NJ * (p + 1) - 2
                if 0 <= k <= 10 and k not in (3, 9):
                    back.append((("centre", "variance", "normalize", "", "transpose", "product",
                                  "centre", "variance", "normalize", "", "transpose")[k], 2 + k // 6, p))
            if x == 9:
                back.append(("room", 0))
        ffn_order = [("h1", 0), ("h1", 1), ("y", 0), ("h1", 2), ("y", 1), ("yb", 0), ("h1", 3), ("y", 2), ("yb", 1),
                     ("y", 3), ("yb", 2), ("yb", 3)]
        units1 = [(a, p, th, ep) for a in range(2) for p in range(NP) for th in range(2) for ep in range(3)]

        lns = [(1, 2), (1, 2 + NP)]
        for b in range(B):
            if b == 1:
                lns += [(1, 3), (1, 3 + NP)]
            if b:
                lns.append((2, b - 1))
        lns.append((2, B - 1))
        ln_at = {x: k for k, x in enumerate(lns)}

        def ring_jobs(n, c):
            found = []
            if n + 2 < NU:
                found += [("score", n + 2, 4 * c + i) for i in range(4)]
            if c == 1 and n + 1 < NU:
                found.append(("shift", n + 1))
            b, hp = divmod(n, 4)
            if hp < 2 and b + 1 < B and c >= 2:
                found.append(("proj", b + 1, hp, (c - 2) // 2, c % 2))
            k = 6 * hp + c - 2
            if b > 0 and 0 <= k < 12:
                found.append(("out", b - 1, k // 2, k % 2))
            if b < 2 and hp == 2 and c < 2:
                found.append(("xt", 1, b + 2, c))
            if b > 0 and hp == 3:
                found += {0: [("xt", 2, b - 1, 0)], 1: [("xt", 2, b - 1, 1)], 2: [("logits", b - 1)],
                          4: [("pos", b - 1)]}.get(c, [])
            return found

        def side_jobs(n, c):
            b, hp = divmod(n, 4)
            found = []
            if b < 2 and hp < 2 and c in (2, 4):
                found.append(("ln_mean" if c == 2 else "ln_std", 1, b + 2 + NP * hp))
            if b > 0:
                if hp == 2 and c in (3, 4):
                    found.append(("ln_mean" if c == 3 else "ln_std", 2, b - 1))
                if hp == 3 and c in (2, 3):
                    found.append(("choose" if c == 2 else "weigh", b - 1))
            if b > 1:
                if hp == 0 and c == 2:
                    found.append(("slots", b - 2))
                if hp < 2 and c >= 3:
                    found.append(("scatter", b - 2, 3 * hp + c - 3))
            return found

        before = [("proj", 0, g, qk, th) for g in range(2) for qk in range(2) for th in range(2)]
        before += [("score", n, i) for n in range(1) for i in range(24)] + [("shift", 0)]
        before += [("score", 1, i) for i in range(24)]
        b = B - 1
        after = [("slots", b - 1)] + [("scatter", b - 1, j) for j in range(NJ)]
        after += [("out", b, j, h) for j in range(NJ) for h in range(2)]
        after += [("ln_mean", 2, b), ("ln_std", 2, b), ("xt", 2, b, 0), ("xt", 2, b, 1), ("logits", b), ("choose", b),
                  ("weigh", b), ("pos", b), ("slots", b)] + [("scatter", b, j) for j in range(NJ)]
        order = before + [x for n in range(NU) for c in range(6) for x in ring_jobs(n, c) + side_jobs(n, c)] + after
        on_ring = ("proj", "score", "shift", "out", "xt", "logits", "pos")
        ring_at = {x: k for k, x in enumerate(y for y in order if y[0] in on_ring)}
        nproj = {x: k for k, x in enumerate(y for y in order if y[0] == "proj")}
        ring_bank = [bank[0], bank[1]]
        st_bank = [[bank[2], bank[3]], [bank[4], bank[5]]]
        ctx_bank = [bank[6], bank[7]]

        wd = []
        prep = []
        for qk, name in enumerate(("L0_attn_Q", "L0_attn_K")):
            prep.append((qload[:, qk, :, 64:128], t[name].rearrange("(g h) r d -> (h r) g d", g=2)))
        for h2 in range(2):
            rowsl = slice(64 * h2, 64 * h2 + 64)
            vo = t["L0_attn_VO"].rearrange("(hp h) d e -> h d hp e", h=2)[h2]
            prep.append((voload[rowsl, 0, :, :], vo))
            prep.append((voload[rowsl, 1, :, :], t["L0_attn_VO"].rearrange("(hp h) d e -> h d hp e", h=2)[h2, 63]
                       .partition_broadcast(64)))
        for a in range(2):
            r = slice(64 * a, 64 * a + 64)
            wd += [(W["gw"][r, 8 * a:8 * a + 8], t["L0_ffn_gate_w"]),
                   (W["hop1"][r, 64 * a:64 * a + 64], t["L1_attn_hop_w1"][0:64]),
                   (W["hop2"][r, 132 * a:132 * a + 132], t["L1_attn_hop_w2"]),
                   (W["wta"][r, 128 * a:128 * a + 64], t["L1_attn_mc_w"]),
                   (W["wta"][r, 128 * a + 64:128 * a + 128], t["L1_attn_ve_w"]),
                   (W["wta"][r, 256 + 32 * a:288 + 32 * a], t["L1_attn_cpe_w"]),
                   (W["ksk1"][r, 64 * a:64 * a + 64], t["L1_attn_ksk_w1"][0:64]),
                   (W["sg1"][r, 32 * a:32 * a + 32], t["L1_attn_sg_w1"]),
                   (W["ksk2"][r, 32 * a:32 * a + 32], t["L1_attn_ksk_w2"]),
                   (W["sg2"][32 * a:32 * a + 32, a:a + 1], t["L1_attn_sg_w2"]),
                   (W["outw"][r, 64 * a:64 * a + 64], t["L1_attn_out_w"]),
                   (W["rw1"][r, 32 * a:32 * a + 32], t["L1_ffn_router_w1"]),
                   (W["rw2"][32 * a:32 * a + 32, 6 * a:6 * a + 6], t["L1_ffn_router_w2"]),
                   (W["b2"][r, :], t["L0_ffn_b2"][4 * a:4 * a + 4].rearrange("e d -> d e")),
                   (W["e1b"][r, :], t["L1_ffn_expert_b1"].rearrange("(ep e) h -> e h ep", e=2)[a]),
                   (W["e2b"][r, :], t["L1_ffn_expert_b2"].rearrange("(ep e) h -> e h ep", e=2)[a]),
                   (W["sgb1"][32 * a:32 * a + 32, :], t["L1_attn_sg_b1"].unsqueeze(1)),
                   (W["rb1"][32 * a:32 * a + 32, :], t["L1_ffn_router_b1"].unsqueeze(1))]
            prep += [(W["hop1b"][0:32, 64 * a:64 * a + 64], t["L1_attn_hop_w1"][64:96]),
                     (W["kskb"][0:64, 64 * a:64 * a + 64], t["L1_attn_ksk_w1"][64:128]),
                     (W["kb1"][r, :], t["L1_attn_ksk_b1"].unsqueeze(1)),
                     (W["hopb"][r, :], t["L1_attn_hop_b1"].unsqueeze(1))]
            for at_, name, n in ((CVB + 128 * a, "mc_b", 64), (CVB + 128 * a + 64, "ve_b", 64),
                                 (KSB + 32 * a, "cpe_b", 32), (KSB + 64 + 32 * a, "ksk_b2", 32),
                                 (GTB + a, "sg_b2", 1), (AOB + 132 * a, "hop_b2", 132)):
                wd.append((bias[:, at_:at_ + n], t["L1_attn_" + name].partition_broadcast(128)))
        for at_, name, n in ((GB, "L0_ffn_gate_b", 8), (LNG, "L1_attn_ln_g", 64), (LNB, "L1_attn_ln_b", 64),
                             (OB, "L1_attn_out_b", 64), (RB2, "L1_ffn_router_b2", 6)):
            wd.append((bias[:, at_:at_ + n], t[name].partition_broadcast(128)))
        wd.append((bias[:, EB3:EB3 + 384], t["L1_ffn_expert_b3"].rearrange("e d -> (e d)").partition_broadcast(128)))
        wd.append((W["b1"][:, :], t["L0_ffn_b1"].rearrange("e (h f) -> f (e h)", h=2)))
        prep.append((bias[:, WD:WD + WN], t["L1_attn_window_deltas"].partition_broadcast(128)))
        prep.append((W["kceb"][0:64, :], t["L1_attn_kce_b"].unsqueeze(1)))
        prep.append((W["kce"][0:64, :], t["L1_attn_kce_w"]))
        prep.append((ppx[:, :, :], t["L1_attn_pos_phases"][0:L].rearrange("(j r) p -> r j p", r=R)))

        block = ctx.enter_context(nc.Block())

        @block.tensor
        def _(pe):
            pe.wait_ge(S["dma_conv"], 16 * 11)
            pe.wait_ge(S["consts"], 1)
            ps, done = take(pe, "w96")
            pe.matmul(ps[0:96, 0:OW + D], R4, P4[:, 0:OW + D], start=True, stop=True).then_inc(done, 1)
            pe.wait_ge(S["conv_w"], 1)
            for i in range(NB):
                ps, done = take(pe, ("conv", i))
                if i:
                    pe.wait_ge(S["conv_x"], i)
                for n, (tap, q, lo, hi, src) in enumerate(taps[i]):
                    last = pe.matmul(ps[0:96, lo:hi], Fw[:, i * KT + tap, 64 - 32 * q:160 - 32 * q],
                                     xc[:, src:src + hi - lo], start=(n == 0), stop=(n == len(taps[i]) - 1))
                last.then_inc(done, 1)
                if i == 4:
                    pe.wait_ge(S["dma_prep"], 16 * len(prep))
                    pe.wait_ge(S["consts"], 2)
                    for qk in range(2):
                        for a in range(2):
                            ps, done = take(pe, ("qkp", qk, a))
                            for g in range(2):
                                last = pe.transpose(ps[:, g * 128:(g + 1) * 128],
                                                    qload[:, qk, g, 64 - 64 * a:192 - 64 * a], ident)
                            last.then_inc(done, 1)
                if i == 5:
                    ps, done = take(pe, "kcet")
                    pe.transpose(ps[0:64, 0:64], W["kce"][0:64, :], ident[0:64, 0:64]).then_inc(done, 1)
                    ps, done = take(pe, "kb")
                    pe.matmul(ps[:, 0:1], W["kskb"][0:64, :], W["kceb"][0:64, :], start=True, stop=True).then_inc(done, 1)
                    for h in range(2):
                        ps, done = take(pe, ("ppt", h))
                        for n in range(3):
                            last = pe.transpose(ps[0:PP, n * R:(n + 1) * R], ppx[:, 3 * h + n, :], ident[0:R, 0:R])
                        last.then_inc(done, 1)
                if i == 6:
                    emptied(pe, "kcet")
                    emptied(pe, "kb")
                    ps, done = take(pe, "ksm")
                    pe.matmul(ps[:, 0:64], W["kcet"][0:64, :], W["kskb"][0:64, 0:64], start=True, stop=True)\
                        .then_inc(done, 1)
                    emptied(pe, ("ppt", 0))
                    emptied(pe, ("ppt", 1))
                    for h in range(2):
                        ps, done = take(pe, ("ppf", h))
                        pe.matmul(ps[:, 0:HALF], W["hop1b"][0:PP, :], ppt[:, h * HALF:(h + 1) * HALF],
                                  start=True, stop=True).then_inc(done, 1)
            pe.wait_ge(S["conv_x"], NB)
            for half in range(2):
                for s in range(NS):
                    ps, done = take(pe, ("h0", half, s))
                    pe.matmul(ps[0:R, :], xc[:, half * R:(half + 1) * R], Wout[:, 8 * s:8 * s + 8, :],
                              start=True, stop=True).then_inc(done, 1)

            def transposes(k, src, p, ready):
                pe.wait_ge(ready, p + 1)
                for h in range(2):
                    ps, done = take(pe, ("xt", k, p, h))
                    for n in range(3):
                        last = pe.transpose(ps[:, n * R:(n + 1) * R], src(p, 3 * h + n), ident[0:R, 0:R])
                    last.then_inc(done, 1)

            def xn_tile(p, j):
                return XN[:, p, j].rearrange("r a d -> r (a d)")

            for p in range(2):
                transposes(0, xn_tile, p, S["normed0"])

            for k in range(len(jobs) - 8, len(jobs)):
                pe.wait_ge(free[k % 8], k // 8 + 1)
            
            def ring(job):
                k = ring_at[job]
                if k >= 2:
                    pe.wait_ge(S["ring_free"], k - 1)
                ps = ring_bank[k % 2]
                kind = job[0]
                if kind == "proj":
                    _, b, g, qk, th = job
                    p, a = b % NP, b // NP
                    if ("xt", 1, b, 1) in ring_at:
                        pe.wait_ge(S["ring_free"], ring_at[("xt", 1, b, 1)] + 1)
                    last = pe.matmul(ps[:, 0:HALF], qkp[:, a, qk, g * 128:(g + 1) * 128],
                                     XT[:, p * L + th * HALF:p * L + (th + 1) * HALF], start=True, stop=True)
                elif kind == "score":
                    _, n, i = job
                    b, hp = divmod(n, 4)
                    h2, j, half = i // 12, i // 2 % 6, i % 2
                    if i == 0:
                        pe.wait_ge(S["qk_dma0"] if hp < 2 else S["qk_dma1"], 16 * 12 * (b + 1))
                    h = 2 * hp + h2
                    last = pe.matmul(ps[0:R, 0:HALF], QA[0:96, b % 2, h, j * R:(j + 1) * R],
                                     KA[0:96, b % 2, h, half * HALF:(half + 1) * HALF], start=True, stop=True)
                elif kind == "shift":
                    n = job[1]
                    pe.wait_ge(S["shift_in"], n + 1)
                    last = pe.transpose(ps[0:36, 0:63].bitcast(BF16)[:, 0:R],
                                        NM[:, n % 2, :], identb[0:R, 0:R])
                elif kind == "xt":
                    _, k_, b, h = job
                    p = b % NP
                    pe.wait_ge(S["lnb_done"], ln_at[(k_, b + NP if k_ == 1 else b)] + 1)
                    for i in range(3):
                        last = pe.transpose(ps[:, i * R:(i + 1) * R],
                                            XN[:, p, 3 * h + i].rearrange("r a d -> r (a d)"), ident[0:R, 0:R])
                elif kind == "logits":
                    b = job[1]
                    p, a = b % NP, b // NP
                    pe.wait_ge(S["ring_free"], ring_at[("xt", 2, b, 1)] + 1)
                    for j in range(NJ):
                        c = p * L + j * R
                        last = pe.matmul(ps[0:R, E0 * j:E0 * j + E0], XT[:, c:c + R],
                                         W["gw"][:, E0 * a:E0 * a + E0], start=True, stop=True)
                elif kind == "pos":
                    b = job[1]
                    pe.wait_ge(S["onehot"], b + 1)
                    pe.wait_ge(S["onehot_sum"], b + 1)
                    pe.matmul(ps[0:R, 0:NJ * E0], triu[0:R, 0:R], OH, start=True, stop=False)
                    last = pe.matmul(ps[0:R, 0:NJ * E0], ones[0:R, 0:R], SO[:, 0:NJ, :], start=False, stop=True)
                else:
                    _, b, j, h = job
                    for i in range(2):
                        hp = 2 * h + i
                        if j == 0 and i == 0:
                            pe.wait_ge(S["ctx_out"], 2 * (4 * b + 2 * h + 2))
                        last = pe.matmul(ps[0:R, i * 130:(i + 1) * 130], CT[:, b % 2, hp, j * R:(j + 1) * R],
                                         vox[:, hp, :], start=True, stop=True)
                last.then_inc(S["ring_full"], 1)

            def scores_t(n, c, h2):
                b, hp = divmod(n, 4)
                x = 12 * n + 2 * c + h2
                if x >= 2:
                    pe.wait_ge(S["exp_done"], x - 1)
                if c == 0 and h2 == 0:
                    pe.wait_ge(S["shift_dma"], 48 * (n + 1))
                    if n == 0:
                        pe.wait_ge(S["kb_ones"], 2)
                h = 2 * hp + h2
                for th in range(2):
                    cols = slice(th * HALF, (th + 1) * HALF)
                    ps = st_bank[h2][th][0:R, 0:HALF]
                    pe.matmul(ps, KA[0:96, b % 2, h, c * R:(c + 1) * R], QA[0:96, b % 2, h, cols],
                              start=True, stop=False)
                    last = pe.matmul(ps, KB[0:99, b % 2, h, c * R:(c + 1) * R], QB[0:99, b % 2, h, cols],
                                     start=False, stop=True)
                last.then_inc(S["st_done"], 1)

            def values(n, c, th):
                b = n // 4
                p, a = b % NP, b // NP
                if th == 0:
                    pe.wait_ge(S["exp_done"], 12 * n + 2 * c + 2)
                    if c == 0:
                        pe.wait_ge(S["v_ready"], p + 1)
                if c == 0 and n:
                    pe.wait_ge(S["ctx_out"], 2 * n - 1 + th)
                for h2 in range(2):
                    last = pe.matmul(ctx_bank[th][64 * h2:64 * h2 + 64, 0:HALF], XN[:, p, c, a, :],
                                     PR[:, (2 * c + h2) % 4, th * HALF:(th + 1) * HALF],
                                     start=(c == 0), stop=(c == 5), tile_position=(0, 64 * h2))
                if th == 1:
                    last.then_inc(S["pv_done"], 1)

            for job in before:
                ring(job)
            for n in range(NU):
                for c in range(6):
                    js = ring_jobs(n, c)
                    scores_t(n, c, 0)
                    for job in js[0:1]:
                        ring(job)
                    scores_t(n, c, 1)
                    for job in js[1:2]:
                        ring(job)
                    u = 6 * n + c - 1
                    if u >= 0:
                        values(u // 6, u % 6, 0)
                    for job in js[2:3]:
                        ring(job)
                    if u >= 0:
                        values(u // 6, u % 6, 1)
                    for job in js[3:]:
                        ring(job)
            values(NU - 1, 5, 0)
            values(NU - 1, 5, 1)
            for job in after:
                if job in ring_at:
                    ring(job)

            pe.wait_ge(S["xb_loaded"], 16 * 8)
            for e in range(4):
                for h in range(2):
                    ps, done = take(pe, ("xbt", e, h))
                    for n in range(4):
                        last = pe.transpose(ps[:, n * R:(n + 1) * R], XB[:, e, 4 * h + n, :], ident[0:R, 0:R])
                    last.then_inc(done, 1)
            pe.wait_ge(S["w_late"], 16 * 3)

            def expert_in(e):
                emptied(pe, ("xbt", e, 0))
                emptied(pe, ("xbt", e, 1))
                for a in range(2):
                    for fh in range(2):
                        for nn in range(2):
                            ps, done = take(pe, ("h1", e, a, fh, nn))
                            pe.matmul(ps[:, 0:CH], w1p[:, e + 4 * a, fh * 128:(fh + 1) * 128],
                                      XBT[:, e, nn * CH:(nn + 1) * CH], start=True, stop=True).then_inc(done, 1)

            def expert_out(e):
                for a in range(2):
                    for fh in range(2):
                        for nn in range(2):
                            emptied(pe, ("h1", e, a, fh, nn))
                for nn in range(2):
                    ps, done = take(pe, ("y", e, nn))
                    for fh in range(2):
                        for a in range(2):
                            last = pe.matmul(ps[64 * a:64 * a + 64, 0:CH], w2e[:, e + 4 * a, fh, :],
                                             HM[:, e % 2, a, fh, nn * CH:(nn + 1) * CH],
                                             start=(fh == 0), stop=(fh == 1), tile_position=(0, 64 * a))
                    last.then_inc(done, 1)

            def expert_back(e):
                emptied(pe, ("y", e, 0))
                emptied(pe, ("y", e, 1))
                pe.wait_ge(S["big"], 2)
                for h in range(2):
                    ps, done = take(pe, ("yb", e, h))
                    for n in range(4):
                        last = pe.transpose(ps[0:R, n * 128:(n + 1) * 128],
                                            YT[:, e, (4 * h + n) * R:(4 * h + n + 1) * R], ident)
                    last.then_inc(done, 1)

            expert_in(0)
            for e in range(4):
                if e < 3:
                    expert_in(e + 1)
                expert_out(e)
                if e:
                    expert_back(e - 1)
            expert_back(3)

            def hidden(p):
                for h in range(2):
                    emptied(pe, ("xt", 1, p, h))
                for th in range(2):
                    cols = slice(p * L + th * HALF, p * L + (th + 1) * HALF)
                    for name, w in (("hop", W["hop1"]), ("sg", W["sg1"])):
                        ps, done = take(pe, (name, p, th))
                        pe.matmul(ps[0:w.shape[1], 0:HALF], w, XT[:, cols], start=True, stop=True).then_inc(done, 1)
                    if th == 0:
                        pe.wait_ge(S["cx"], p + 1)
                    ps, done = take(pe, ("ksk", p, th))
                    pe.matmul(ps[:, 0:HALF], W["ksk1"], XT[:, cols], start=True, stop=False)
                    pe.matmul(ps[:, 0:HALF], W["ksm"], CX[:, cols], start=False, stop=True).then_inc(done, 1)

            def tokens(p):
                for th in range(2):
                    emptied(pe, ("ksk", p, th))
                pe.wait_ge(S["hop_act"], 2 * (p + 1))
                for i in range(NJ * p, NJ * p + NJ):
                    cols = slice(i * R, (i + 1) * R)
                    ps, done = take(pe, ("tok", i))
                    pe.matmul(ps[0:R, 0:320], XT[:, cols], W["wta"], start=True, stop=True)
                    pe.matmul(ps[0:R, 320:384], KG[:, cols], W["ksk2"], start=True, stop=True)
                    pe.matmul(ps[0:R, 384:386], SG[0:64, cols], W["sg2"][0:64, :], start=True, stop=True)\
                        .then_inc(done, 1)
                    ps, done = take(pe, ("ao", i))
                    pe.matmul(ps[0:R, 0:264], HG[:, cols], W["hop2"], start=True, stop=True).then_inc(done, 1)

            for kind, p in front:
                if kind == "transpose":
                    transposes(1, xn_tile, p, S["normed1"])
                elif kind == "hidden":
                    hidden(p)
                elif kind == "tokens":
                    tokens(p)
            pe.wait_ge(S["gate"], 1)
            for name, m in (("gcum", triu), ("gtot", ones)):
                ps, done = take(pe, name)
                pe.matmul(ps[0:R, 0:NG], m[0:R, 0:R], GA[:, 0, :], start=True, stop=True).then_inc(done, 1)

            def features(x):
                p, j = divmod(x, NJ)
                pe.wait_ge(S["qf_ready"], x // 2 + 1)
                pe.wait_ge(S["ff"], x // 2 + 1)
                for a in range(2):
                    ps, done = take(pe, ("qf", x, a))
                    pe.transpose(ps[:, 0:R], QQ[:, 2 * x + a, :], ident[0:R, 0:R])
                    pe.transpose(ps[:, R:2 * R], FF[:, 2 * x + a, :], ident[0:R, 0:R]).then_inc(done, 1)

            def masked(x):
                p, j = divmod(x, NJ)
                g = 2 * x
                for k in range(2):
                    ps, done = take(pe, ("sm", x, k))
                    for a in range(2):
                        if k == 0:
                            emptied(pe, ("qf", x, a))
                        q = QF[64 * k:64 * k + 64, (2 * x + a) % 8, :]
                        last = pe.matmul(ps[0:R, a * R:(a + 1) * R], q[:, R:2 * R], q[:, 0:R], start=True, stop=True)
                    last.then_inc(done, 1)
                if j < NJ - 1:
                    ps, done = take(pe, ("state", x))
                    for a in range(2):
                        last = pe.matmul(ps[:, a * 128:(a + 1) * 128], FF[:, g + a, :],
                                         CV[:, g // 2, a].rearrange("r c d -> r (c d)"), start=True, stop=True)
                    last.then_inc(done, 1)

            def retrieved(x):
                p, j = divmod(x, NJ)
                g = 2 * x
                emptied(pe, ("sm", x, 0))
                emptied(pe, ("sm", x, 1))
                if j:
                    pe.wait_ge(S["state"], 2 * (p * (NJ - 1) + j))
                ps, done = take(pe, ("ret", x))
                for a in range(2):
                    o = ps[0:R, a * D:(a + 1) * D]
                    pe.matmul(o, SM[:, x % 4, 0, a, :], CV[:, g // 2, a, 0, :], start=True, stop=False)
                    last = pe.matmul(o, SM[:, x % 4, 1, a, :], CV[:, g // 2, a, 1, :], start=False, stop=(j == 0))
                    if j:
                        last = pe.matmul(o, QF[:, (2 * x + a) % 8, 0:R], ST[:, p % 2, j, a, :], start=False, stop=True)
                last.then_inc(done, 1)

            def product(p):
                for h in range(2):
                    emptied(pe, ("xt", 2, p, h))
                for h in range(2):
                    ps, done = take(pe, ("product", p, h))
                    for n in range(3):
                        c = p * L + (3 * h + n) * R
                        last = pe.matmul(ps[0:R, n * 128:(n + 1) * 128], XT[:, c:c + R], W["outw"],
                                         start=True, stop=True)
                    last.then_inc(done, 1)

            for event in back:
                kind, x = event[0:2]
                if kind == "features":
                    features(x)
                elif kind == "masked":
                    masked(x)
                elif kind == "retrieved":
                    retrieved(x)
                elif kind == "transpose" and x == 2:
                    transposes(2, lambda p, j: CO[:, p * NJ + j, :], event[2], S["lnx"])
                elif kind == "transpose":
                    transposes(3, xn_tile, event[2], S["normed3"])
                elif kind == "product":
                    product(event[2])

            pe.wait_ge(S["w_late"], 16 * 9)
            for p in range(NP):
                emptied(pe, ("xt", 3, p, 0))
                emptied(pe, ("xt", 3, p, 1))
                for th in range(2):
                    cols = slice(p * L + th * HALF, p * L + (th + 1) * HALF)
                    ps, done = take(pe, ("rh", p, th))
                    pe.matmul(ps[0:64, 0:HALF], W["rw1"], XT[:, cols], start=True, stop=True).then_inc(done, 1)
            for p in range(NP):
                emptied(pe, ("rh", p, 0))
                emptied(pe, ("rh", p, 1))
            ps, done = take(pe, "logits1")
            for i in range(NT):
                last = pe.matmul(ps[0:R, 12 * i:12 * i + 12], RH[0:64, i * R:(i + 1) * R], W["rw2"][0:64, :],
                                 start=True, stop=True)
            last.then_inc(done, 1)
            units = units1

            def layer1(x):
                a, p, th, ep = units[x]
                ps, done = take(pe, ("l1", x))
                pe.matmul(ps[:, 0:HALF], e1w[:, a, ep, :], XT[:, p * L + th * HALF:p * L + (th + 1) * HALF],
                          start=True, stop=True).then_inc(done, 1)

            def layer2(x):
                a, p, th, ep = units[x]
                emptied(pe, ("l1", x))
                ps, done = take(pe, ("l2", x))
                pe.matmul(ps[:, 0:HALF], e2w[:, ep, :], H1[:, x % 4, :], start=True, stop=True).then_inc(done, 1)

            def layer3(a, p, th):
                x0 = 3 * ((a * NP + p) * 2 + th)
                for ep in range(3):
                    emptied(pe, ("l2", x0 + ep))
                for n in range(3):
                    j = 3 * th + n
                    ps, done = take(pe, ("l3", a, p, j))
                    for ep in range(3):
                        last = pe.matmul(ps[0:R, ep * 128:(ep + 1) * 128],
                                         H2[:, ep, p * L + j * R:p * L + (j + 1) * R], e3w[:, ep, :],
                                         start=True, stop=True)
                    last.then_inc(done, 1)

            NX = len(units)
            for x in range(NX + 1):
                if x < NX:
                    layer1(x)
                if x:
                    layer2(x - 1)
                    if x >= 6 and x % 3 == 0:
                        layer3(*units[x - 6][0:3])
            layer3(*units[NX - 3][0:3])

        @block.sync
        def _(sp):
            for s in range(NS):
                sp.dma_start(xc[32 * s:32 * s + 32, :],
                             t["x"].rearrange("b c (s l) -> s (b c) l", s=NS)[s]).then_inc(S["dma_conv"], 16)
            sp.dma_start(P4[:, 0:PAR].rearrange("c (i o k) -> c i o k", i=NB, o=CIN),
                         t["L0_tok_conv_w"].rearrange("i o c k -> c i o k")).then_inc(S["dma_conv"], 16)
            for n, name in enumerate(("conv_b", "bn_gamma", "bn_beta", "bn_mean", "bn_var")):
                sp.dma_start(P4[:, PAR + n * NB:PAR + (n + 1) * NB],
                             t["L0_tok_" + name].rearrange("i c -> c i")).then_inc(S["dma_conv"], 16)
            sp.dma_start(P4[:, OW:OW + D], t["L0_tok_out_w"].rearrange("v c o -> c (v o)")).then_inc(S["dma_conv"], 16)
            sp.dma_start(outb[:, :], t["L0_tok_out_b"].partition_broadcast(R)).then_inc(S["dma_conv"], 16)
            sp.wait_ge(S["zeroed"], 1)
            for e in range(E0):
                sp.dma_start(xbuf[e * ROWS:(e + 1) * ROWS].rearrange("(r c) d -> r (c d)", r=R), zeros)\
                    .then_inc(S["xbuf_zero"], 16)
            sp.wait_ge(S["zeroed"], 2)
            for dst, src in prep:
                sp.dma_start(dst, src).then_inc(S["dma_prep"], 16)
            for dst, src in wd:
                sp.dma_start(dst, src).then_inc(S["dma_weights"], 16)

            for job in order:
                if job[0] == "proj" and job[4] == 1:
                    _, b, g, qk, th = job
                    dma = S["qk_dma0"] if g == 0 else S["qk_dma1"]
                    sp.wait_ge(S["split3"], nproj[job] + 1)
                    if b >= 2:
                        sp.wait_ge(S["st_done"], 48 * (b - 1))
                    for arr, terms in (((QA, (0, 0, 1)), (QB, (0, 2, 1))), ((KA, (0, 1, 0)), (KB, (2, 0, 1))))[qk]:
                        for s, term in enumerate(terms):
                            sp.dma_start(arr[32 * s:32 * s + 32, b % 2, 4 * g:4 * g + 4, :],
                                         SP[:, qk, term, :]).then_inc(dma, 16)
                if job[0] == "shift":
                    n = job[1]
                    b, hp = divmod(n, 4)
                    sp.wait_ge(S["ring_free"], ring_at[job] + 1)
                    for term in range(3):
                        dst = QB[96 + term:97 + term, b % 2, 2 * hp:2 * hp + 2, :]
                        sp.dma_start(dst.rearrange("o h (j r) -> o (h j) r", r=R), MT[12 * term:12 * term + 12, n % 2, 0:R])\
                            .then_inc(S["shift_dma"], 16)

            sp.wait_ge(S["late_zero"], 1)
            sp.dma_start(w1p[0:64, 0:4, :], t["L0_ffn_w1"][0:4].rearrange("e d f -> d e f")).then_inc(S["w_late"], 16)
            sp.dma_start(w1p[64:128, 4:8, :], t["L0_ffn_w1"][4:8].rearrange("e d f -> d e f")).then_inc(S["w_late"], 16)
            sp.dma_start(w2e.rearrange("f e h d -> f (e h) d"),
                         t["L0_ffn_w2"].rearrange("e (h f) d -> f (e h) d", h=2)).then_inc(S["w_late"], 16)
            sp.wait_ge(S["scattered"], 16 * NG)
            for e in range(4):
                for a in range(2):
                    r0 = (e + 4 * a) * ROWS
                    sp.dma_start(XB[:, e, :, a * D:(a + 1) * D],
                                 xbuf[r0:r0 + ROWS].rearrange("(c r) d -> r c d", r=R)).then_inc(S["xb_loaded"], 16)
            for e in range(4):
                emptied(sp, ("yb", e, 0))
                emptied(sp, ("yb", e, 1))
                for a in range(2):
                    r0 = (e + 4 * a) * ROWS
                    sp.dma_start(ybuf[r0:r0 + ROWS].rearrange("(c r) d -> r c d", r=R),
                                 XB[:, e, :, a * D:(a + 1) * D]).then_inc(S["y_stored"], 16)
            sp.wait_ge(S["late_zero"], 2)
            for a in range(2):
                r = slice(64 * a, 64 * a + 64)
                w1, w2, w3 = (t["L1_ffn_expert_w" + str(n)].rearrange("(ep e) d h -> e d ep h", e=2)
                              for n in (1, 2, 3))
                sp.dma_start(e1w[r, a].rearrange("d ep (e h) -> d (ep e) h", e=2),
                             t["L1_ffn_expert_w1"].rearrange("e d h -> d e h")).then_inc(S["w_late"], 16)
                sp.dma_start(e2w[r, :, 64 * a:64 * a + 64], w2[a]).then_inc(S["w_late"], 16)
                sp.dma_start(e3w[r, :, 64 * a:64 * a + 64], w3[a]).then_inc(S["w_late"], 16)
            for a in range(2):
                for p in range(NP):
                    sp.wait_ge(S["h4"], NJ * (a * NP + p + 1))
                    sp.dma_start(out[p + 4 * a].rearrange("(j r) d -> r j d", r=R), H[:, p, :, a, :])\
                        .then_inc(S["stored"], 16)
            sp.wait_ge(S["stored"], 16 * B)

        @block.gpsimd
        def _(pool):
            n_ = [0]

            def link(ins):
                n_[0] += 1
                ins.then_inc(S["pool_chain"], 1)
                pool.wait_ge(S["pool_chain"], n_[0])

            pool.memset(R4, 0.0)
            pool.memset(bmask, 1.0)
            link(pool.memset(m24, 1.0))
            v = R4.rearrange("c (g k) -> c g k", k=CIN)
            pool.affine_select(out=v, in_=v, compare_op=ALU.not_equal, fill=1.0, base=0,
                               pattern=[[0, NS * B], [-1, CIN]], channel_multiplier=1).then_inc(S["consts"], 1)
            masks = [bmask[32 * s:32 * s + 32, :] for s in range(NS)] + [m24]
            for v in masks:
                link(pool.affine_select(out=v, in_=v, compare_op=ALU.is_ge, fill=0.0, base=0,
                                        pattern=[[-CIN, v.shape[1]]], channel_multiplier=1))
                link(pool.affine_select(out=v, in_=v, compare_op=ALU.is_ge, fill=0.0, base=CIN - 1,
                                        pattern=[[CIN, v.shape[1]]], channel_multiplier=-1))
            pool.memset(Fw, 0.0)
            pool.memset(ident[:, :], 0.0)
            pool.memset(triu[:, :], 1.0)
            pool.memset(ones[:, :], 1.0)
            pool.memset(mhalf[:, :], -0.5)
            link(pool.memset(halfpi[:, :], PI / 2))
            pool.affine_select(out=ident[:, :], in_=ident[:, :], compare_op=ALU.not_equal, fill=1.0, base=0,
                               pattern=[[-1, 128]], channel_multiplier=1).then_inc(S["consts"], 1)
            pool.affine_select(out=triu[:, :], in_=triu[:, :], compare_op=ALU.is_ge, fill=0.0, base=0,
                               pattern=[[1, 128]], channel_multiplier=-1)
            pool.memset(zero1[:, :], 0.0)
            pool.memset(wearly, 0.0)
            pool.memset(zeros, 0.0).then_inc(S["zeroed"], 1)
            pool.memset(qload, 0.0)
            pool.memset(wall[:, :], 0.0)
            pool.memset(vox[:, :, :], 0.0).then_inc(S["zeroed"], 1)
            pool.wait_ge(S["consts"], 2)
            pool.tensor_copy(identb[:, :], ident[:, :]).then_inc(S["consts"], 1)
            pool.iota(out=iota8[:, :], pattern=[[1, E0]], base=-E0, channel_multiplier=0,
                      allow_small_or_imprecise_dtypes=True).then_inc(S["consts"], 1)
            pool.wait_ge(S["bn_var"], 1)
            pool.tensor_tensor(bn[:, 1, :], bn[:, 0, :], mhalf[0:96, 0:NB], ALU.pow).then_inc(S["bn_rstd"], 1)
            pool.wait_ge(S["vo_ready"], 1)
            for h2 in range(2):
                v = vox[:, :, 65 * h2 + 64:65 * h2 + 65]
                ins = pool.affine_select(out=v, in_=v, compare_op=ALU.not_equal, fill=1.0, base=-(63 + 64 * h2),
                                         pattern=[[0, 4], [0, 1]], channel_multiplier=1)
            ins.then_inc(S["vo_ready"], 1)

            def rstd(k, p):
                pool.wait_ge(S[f"variance{k}"], p + 1)
                pool.tensor_tensor(lnst[:, 3, p, :], lnst[:, 2, p, :], mhalf[0:R, 0:2 * NJ], ALU.pow)\
                    .then_inc(S[f"rstd{k}"], 1)

            rstd(0, 0)
            rstd(0, 1)

            pool.wait_ge(S["rstd0"], 2)
            for a in range(2):
                pool.memset(KB[96:99, a], 1.0).then_inc(S["kb_ones"], 1)
                pool.wait_ge(S["kb_ones"], a + 1)

            def values_ready(p):
                pool.memset(XN[:, p, :, :, D - 1:D], 1.0).then_inc(S["v_ready"], 1)

            link(pool.memset(SO[:, NJ, :], 0.0))
            for p in range(2):
                for h in range(2):
                    pool.wait_ge(full[jobs[("xt", 0, p, h)] % 8], jobs[("xt", 0, p, h)] // 8 + 1)
                values_ready(p)
            for job in order:
                kind = job[0]
                if kind == "proj":
                    _, b, g, qk, th = job
                    q = nproj[job]
                    cols = slice(th * HALF, (th + 1) * HALF)
                    pool.wait_ge(S["ring_free"], ring_at[job] + 1)
                    link(pool.tensor_copy(SP[:, qk, 1, cols], RR[:, q % 2, :]))
                    pool.tensor_tensor(SP[:, qk, 2, cols], RR[:, q % 2, :], SP[:, qk, 1, cols], ALU.subtract)\
                        .then_inc(S["split3"], 1)
                elif kind == "score" and job[2] == 23:
                    n = job[1]
                    pool.wait_ge(S["mx_neg"], n + 1)
                    if n >= 2:
                        pool.wait_ge(S["ring_full"], ring_at[("shift", n - 2)] + 1)
                    m, nm = M1[:, n % 2, :], NM[:, n % 2, :]
                    link(pool.tensor_scalar(nm[:, 0:12], m, -1.0, None, ALU.mult))
                    link(pool.tensor_tensor(MR[:, 0, :], m, nm[:, 0:12], ALU.add))
                    link(pool.tensor_scalar(nm[:, 12:24], MR[:, 0, :], -1.0, None, ALU.mult))
                    link(pool.tensor_tensor(MR[:, 1, :], MR[:, 0, :], nm[:, 12:24], ALU.add))
                    pool.tensor_scalar(nm[:, 24:36], MR[:, 1, :], -1.0, None, ALU.mult).then_inc(S["shift_in"], 1)
                elif kind == "xt" and job[1] == 1 and job[3] == 1:
                    pool.wait_ge(S["ring_full"], ring_at[job] + 1)
                    values_ready(job[2])
                elif kind == "ln_mean":
                    k, b = ln_at[job[1:3]], job[2]
                    p, a = b % NP, b // NP
                    pool.wait_ge(S["lnb_sum"], k + 1)
                    x = XN[:, p, :, a, :]
                    link(pool.tensor_scalar(lnb[:, 1, :], lnb[:, 0, :], -1.0 / D, None, ALU.mult))
                    link(pool.tensor_tensor(x, H[:, p, :, a, :], over(lnb[:, 1, :], NJ, D), ALU.add))
                    pool.tensor_tensor(XSQ, x, x, ALU.mult).then_inc(S["lnb_x"], 1)
                elif kind == "ln_std":
                    k, b = ln_at[job[1:3]], job[2]
                    p, a = b % NP, b // NP
                    pool.wait_ge(S["lnb_ssq"], k + 1)
                    x = XN[:, p, :, a, :]
                    link(pool.tensor_scalar(lnb[:, 3, :], lnb[:, 2, :], 1.0 / D, EPS, ALU.mult, ALU.add))
                    link(pool.tensor_tensor(lnb[:, 3, :], lnb[:, 3, :], mhalf[0:R, 0:NJ], ALU.pow))
                    pool.tensor_tensor(x, x, over(lnb[:, 3, :], NJ, D), ALU.mult).then_inc(S["lnb_done"], 1)
                elif kind == "choose":
                    b = job[1]
                    pool.wait_ge(S["onehot"], b + 1)
                    link(pool.tensor_copy(SO[:, 0, :], SO[:, NJ, :]))
                    for j in range(NJ):
                        ins = pool.tensor_tensor(SO[:, j + 1, :], SO[:, j, :], OH[:, j, :], ALU.add)
                        if j < NJ - 1:
                            link(ins)
                    ins.then_inc(S["onehot_sum"], 1)
                elif kind == "slots":
                    b = job[1]
                    tiles = slice(NJ * b, NJ * b + NJ)
                    pool.wait_ge(S["pos_ready"], b + 1)
                    link(pool.tensor_scalar(kept, pos, float(CAP), None, ALU.is_le))
                    link(pool.tensor_tensor(pk[:, tiles], prob[:, tiles], kept, ALU.mult))
                    link(pool.tensor_scalar(sl, im, float(ROWS), float(E0 * ROWS), ALU.mult, ALU.add))
                    link(pool.tensor_scalar(tx, kept, -65536.0, 65535.0, ALU.mult, ALU.add))
                    link(pool.tensor_tensor(sx, sl, pos, ALU.add))
                    link(pool.tensor_tensor(sx, sx, tx, ALU.add))
                    link(pool.tensor_copy(slot_in[:, tiles], sx))
                    link(pool.tensor_scalar(sy, pos, float(CAP), -1.0, ALU.min, ALU.add))
                    link(pool.tensor_tensor(sy, sy, sl, ALU.add))
                    link(pool.tensor_copy(slot_out[:, tiles], sy))
                    if b == 0:
                        pool.wait_ge(S["xbuf_zero"], 16 * E0)
                elif kind == "scatter":
                    _, b, j = job
                    p, a = b % NP, b // NP
                    g = b * NJ + j
                    pool.indirect_dma_start(out=xbuf, out_offset=bass.IndirectOffsetOnAxis(ap=slot_in[:, g:g + 1],
                                                                                           axis=0),
                                            in_=XN[:, p, j, a, :], in_offset=None, bounds_check=E0 * ROWS - 1,
                                            oob_is_err=False).then_inc(S["scattered"], 16)
                if job == after[NJ]:
                    pool.wait_ge(S["st_done"], 12 * NU)
                    pool.memset(w1p, 0.0).then_inc(S["late_zero"], 1)
                    pool.wait_ge(S["late_zero"], 1)

            pool.memset(big[:, 0, :], 1.0e4)
            pool.memset(big[:, 1, :], -1.0e4).then_inc(S["big"], 1)
            pool.memset(YT[:, :, CAP:ROWS], 0.0).then_inc(S["big"], 1)
            pool.wait_ge(S["y_stored"], 16 * 8)

            def gather(p):
                for j in range(NJ):
                    for a in range(2):
                        g, i = a * NT + p * NJ + j, (p * NJ + j) * 2 + a
                        pool.indirect_dma_start(
                            out=YG[:, i, :], out_offset=None, in_=ybuf,
                            in_offset=bass.IndirectOffsetOnAxis(ap=slot_out[:, g:g + 1], axis=0),
                            bounds_check=E0 * ROWS - 1, oob_is_err=False).then_inc(gathered[p], 16)

            def residual(p):
                pool.wait_ge(S["normed1"], p + 1)
                link(pool.tensor_tensor(pairs(H, p), pairs(H, p), pairs(XN, p), ALU.add))
                pool.tensor_tensor(pairs(H, p), pairs(H, p), rows(bias[0:R, OB:OB + D], 2 * NJ), ALU.add)\
                    .then_inc(S["h_pre"], 1)

            gather(0)
            pool.iota(out=pos1, pattern=[[1, L]], base=1, channel_multiplier=0,
                      allow_small_or_imprecise_dtypes=True).then_inc(S["pos"], 1)
            gather(1)
            for kind, p in front:
                if kind == "variance":
                    rstd(1, p)
                elif kind == "gathered" and p >= 2:
                    gather(p)
            for p in range(NP):
                residual(p)
            pool.wait_ge(S["gc"], 1)
            link(pool.tensor_tensor(GA[:, 5, :], GA[:, 4, :], mhalf[0:R, 0:NG], ALU.pow))
            link(pool.tensor_scalar(GA[:, 5, :], GA[:, 5, :], RS, None, ALU.mult))

            def chunk(q):
                p = q // 3
                g = slice(4 * q, 4 * q + 4)
                tiles = slice(2 * q, 2 * q + 2)
                pool.wait_ge(S["cosines"], 2 * (p + 1))
                pool.wait_ge(S["wab"], 1)
                if q >= 2:
                    pool.wait_ge(S["uv"], q - 1)
                cc, sc = (x[:, g].rearrange("r g h p -> r (g h) p") for x in (TC, SC))
                wa, wb = (over(WA[:, i, 16 * q:16 * q + 16], 16, PP) for i in range(2))
                p2, p3 = (PT[:, q % 2, i].rearrange("r g h p -> r (g h) p") for i in (2, 3))
                pool.tensor_tensor(p2, sc, wa, ALU.mult)
                link(pool.tensor_tensor(p3, cc, wb, ALU.mult))
                pool.tensor_tensor(p2, p2, p3, ALU.add).then_inc(S["vsum"], 1)
                pool.wait_ge(S["prod"], q + 1)
                pool.wait_ge(S["vsum"], q + 1)
                for i, x in ((0, TK), (1, SK)):
                    kk, ss = (x[:, tiles, w] for w in (0, 1))
                    fs, fq = (v[:, g, 64 + 32 * i:96 + 32 * i].rearrange("r (j a) p -> r j a p", a=2)
                              for v in (FF, QQ))
                    pool.tensor_copy(fs, ss)
                    pool.tensor_tensor(fq, kk, over(GA[:, 5, g], 4, PP).rearrange("r (j a) p -> r j a p", a=2),
                                       ALU.mult)
                    j = 2 * (q % 3)
                    pool.tensor_copy(FF[:, g, 32 * i:32 * i + 32].rearrange("r (j a) p -> r j a p", a=2),
                                     trig[:, i, j * PP:(j + 2) * PP].rearrange("r (j p) -> r j p", p=PP).unsqueeze(2)
                                     .to_broadcast([R, 2, 2, PP]))
                v = CV[:, tiles, :, 1, :].rearrange("r j a d -> r (j a) d")
                pool.tensor_tensor(v, v, over(GA[:, 0, g], 4, D), ALU.mult).then_inc(S["ff"], 1)

            for event in back:
                kind, x = event[0:2]
                if kind == "chunk":
                    chunk(x)
                elif kind == "variance":
                    rstd(x, event[2])
                elif kind == "normalize" and x == 2:
                    p = event[2]
                    v = CO[:, NJ * p:NJ * p + NJ, :].rearrange("r j (a d) -> r (j a) d", a=2)
                    pool.wait_ge(S["normed2"], p + 1)
                    link(pool.tensor_tensor(v, v, rows(bias[0:R, LNG:LNG + D], 12), ALU.mult))
                    pool.tensor_tensor(v, v, rows(bias[0:R, LNB:LNB + D], 12), ALU.add).then_inc(S["lnx"], 1)
                elif kind == "room":
                    k = jobs[("ret", NJ - 1)]
                    pool.wait_ge(full[k % 8], k // 8 + 1)
                    pool.memset(e1w, 0.0)
                    pool.memset(e2w, 0.0)
                    pool.memset(e3w, 0.0).then_inc(S["late_zero"], 1)

        @block.scalar
        def _(act):
            for i in range(NB):
                ps, done = filled(act, ("conv", i))
                if i == 0:
                    act.wait_ge(S["w96"], 1)
                act.activation(xr, ps[0:96, 0:SEG], ACT.Relu, bias=W96[:, PAR + i:PAR + i + 1]).then_inc(done, 1)
                if i == 4:
                    for qk in range(2):
                        for a in range(2):
                            ps, done = filled(act, ("qkp", qk, a))
                            act.wait_ge(S["zeroed"], 2)
                            act.activation(qkp[:, a, qk, :].rearrange("p (g r h) -> p g h r", g=2, h=4),
                                           ps[:, 0:256].rearrange("p (g h r) -> p g h r", g=2, h=4), ACT.Copy)\
                               .then_inc(done, 1)
                if i == 5:
                    ps, done = filled(act, "kcet")
                    act.activation(W["kcet"][0:64, 0:64], ps[0:64, 0:64], ACT.Copy)
                    act.activation(W["kcet"][0:64, 64:128], ps[0:64, 0:64], ACT.Copy).then_inc(done, 1)
                    ps2, done2 = filled(act, "kb")
                    act.activation(W["kb"], ps2[:, 0:1], ACT.Identity, bias=W["kb1"]).then_inc(done2, 1)
                    for h in range(2):
                        ps, done = filled(act, ("ppt", h))
                        act.activation(ppt[:, h * HALF:(h + 1) * HALF], ps[0:PP, 0:HALF], ACT.Copy)\
                           .then_inc(done, 1)
                if i == 6:
                    ps, done = filled(act, "ksm")
                    for a in range(2):
                        r = slice(64 * a, 64 * a + 64)
                        last = act.activation(W["ksm"][r, 64 * a:64 * a + 64], ps[r, 0:64], ACT.Copy)
                    last.then_inc(done, 1)
                    for h in range(2):
                        ps, done = filled(act, ("ppf", h))
                        act.activation(PPF[:, h * HALF:(h + 1) * HALF], ps[:, 0:HALF], ACT.Identity, bias=W["hopb"])\
                           .then_inc(done, 1)
            act.wait_ge(S["trig_r"], 1)
            act.activation(trig[:, 1, :], phases, ACT.Sin).then_inc(S["trig_done"], 1)
            act.activation(trig[:, 0, :], trig[:, 0, :], ACT.Sin, bias=halfpi[0:R, :], scale=-1.0)\
               .then_inc(S["trig_done"], 1)

            def squares(k, p, src):
                act.wait_ge(S[f"centred{k}"], p + 1)
                i = p % 2 if k < 2 else k - 2
                if p >= (2 if k < 2 else 1):
                    act.wait_ge(S[f"variance{k}"], p - 1 if k < 2 else p)
                act.activation(SQ[:, i, :], src, ACT.Square).then_inc(S[f"squared{k}"], 1)

            def xn_flat(p):
                return XN[:, p].rearrange("r j a d -> r (j a d)")

            def to_xt(k, p):
                for h in range(2):
                    ps, done = filled(act, ("xt", k, p, h))
                    act.activation(XT[:, p * L + h * HALF:p * L + (h + 1) * HALF], ps[:, 0:HALF], ACT.Copy)\
                       .then_inc(done, 1)

            squares(0, 0, xn_flat(0))
            squares(0, 1, xn_flat(1))
            to_xt(0, 0)
            to_xt(0, 1)

            def split1(job):
                _, b, g, qk, th = job
                k = ring_at[job]
                act.wait_ge(S["ring_full"], k + 1)
                group = 2 * b + g
                if group and qk == 0 and th == 0:
                    prev = group - 1
                    act.wait_ge((S["qk_dma0"], S["qk_dma1"])[prev % 2], 16 * 12 * (prev // 2 + 1))
                act.activation(SP[:, qk, 0, th * HALF:(th + 1) * HALF], ring_bank[k % 2][:, 0:HALF], ACT.Copy,
                               scale=(0.125 if qk == 0 else 1.0)).then_inc(S["split1"], 1)

            def exp_(n, c, h2):
                x = 12 * n + 2 * c + h2
                act.wait_ge(S["st_done"], x + 1)
                if x >= 4:
                    act.wait_ge(S["pv_done"], x // 2 - 1)
                act.activation(PR[:, x % 4, :].rearrange("r (h c) -> r h c", h=2),
                               psum[0:R, 2 + 2 * h2:4 + 2 * h2, 0:HALF], ACT.Exp).then_inc(S["exp_done"], 1)

            def ctx_out(n):
                b, hp = divmod(n, 4)
                act.wait_ge(S["pv_done"], 6 * (n + 1))
                if b >= 2:
                    act.wait_ge(S["ring_full"], ring_at[("out", b - 2, NJ - 1, 1)] + 1)
                for th in range(2):
                    act.activation(CT[:, b % 2, hp, th * HALF:(th + 1) * HALF], ctx_bank[th][:, 0:HALF], ACT.Copy)\
                       .then_inc(S["ctx_out"], 1)

            def weigh(b):
                act.wait_ge(S["route_ld"], b + 1)
                act.activation(LD, LD, ACT.Exp).then_inc(S["route_ex"], 1)

            for job in before:
                if job[0] == "proj":
                    split1(job)
            for n in range(NU):
                for c in range(6):
                    exp_(n, c, 0)
                    exp_(n, c, 1)
                    if c == 0 and n:
                        ctx_out(n - 1)
                    for job in ring_jobs(n, c) + side_jobs(n, c):
                        if job[0] == "proj":
                            split1(job)
                        elif job[0] == "weigh":
                            weigh(job[1])
            ctx_out(NU - 1)
            weigh(B - 1)

            def copy_out(name, dst):
                ps, done = filled(act, name)
                k = jobs[name]
                act.activation(dst, ps[0:dst.shape[0], 0:dst.shape[1]], ACT.Copy).then_inc(done, 1)

            for e in range(4):
                copy_out(("xbt", e, 0), XBT[:, e, 0:4 * R])
            for kind, e in ffn_order:
                if kind == "h1":
                    for a in range(2):
                        for nn in range(2):
                            name = ("h1", e, a, 0, nn)
                            ps, done = filled(act, name)
                            act.activation(HM[:, e % 2, a, 0, nn * CH:(nn + 1) * CH], ps[:, 0:CH], ACT.Relu,
                                           bias=W["b1"][:, 2 * (e + 4 * a):2 * (e + 4 * a) + 1]).then_inc(done, 1)
                elif kind == "y":
                    for nn in range(2):
                        ps, done = filled(act, ("y", e, nn))
                        act.activation(YT[:, e, nn * CH:(nn + 1) * CH], ps[:, 0:CH], ACT.Identity,
                                       bias=W["b2"][:, e:e + 1]).then_inc(done, 1)
                else:
                    copy_out(("yb", e, 0), XB[:, e, 0:4, :].rearrange("r c d -> r (c d)"))

            for kind, p in front:
                if kind == "centre":
                    squares(1, p, xn_flat(p))
                elif kind == "transpose":
                    to_xt(1, p)
                elif kind == "hidden":
                    for th in range(2):
                        cols = slice(p * L + th * HALF, p * L + (th + 1) * HALF)
                        emptied(act, ("hop", p, th))
                        act.activation(HG[:, cols], HT[:, th, :], ACT.Gelu).then_inc(S["hop_act"], 1)
                        for name, dst, b_, w in (("sg", SG, W["sgb1"], 64), ("ksk", KG, W["kb"], 128)):
                            ps, done = filled(act, (name, p, th))
                            act.activation(dst[0:w, cols], ps[0:w, 0:HALF], ACT.Gelu, bias=b_[0:w, :])\
                               .then_inc(done, 1)
            for p in range(NP):
                for i in range(NJ * p, NJ * p + NJ):
                    emptied(act, ("ao", i))
                for x, dim in ((TC[:, 12 * p:12 * p + 12], "r g h p -> r (g h p)"),
                               (TK[:, NJ * p:NJ * p + NJ], "r j k a p -> r (j k a p)")):
                    x = x.rearrange(dim)
                    act.activation(x, x, ACT.Tanh).then_inc(S["tanh"], 1)
            act.activation(WS, WS, ACT.Sigmoid).then_inc(S["width"], 1)
            act.activation(GA[:, 0, :], GA[:, 1, :], ACT.Sigmoid).then_inc(S["gate"], 1)
            act.wait_ge(S["warg"], 1)
            act.activation(WE, WE, ACT.Exp).then_inc(S["wexp"], 1)
            act.wait_ge(S["tanh"], 2 * NP)
            for p in range(NP):
                for x, y, dim in ((TC[:, 12 * p:12 * p + 12], SC[:, 12 * p:12 * p + 12], "r g h p -> r (g h p)"),
                                  (TK[:, NJ * p:NJ * p + NJ], SK[:, NJ * p:NJ * p + NJ], "r j k a p -> r (j k a p)")):
                    act.activation(y.rearrange(dim), x.rearrange(dim), ACT.Sin, scale=PI_IN).then_inc(S["sines"], 1)
            for p in range(NP):
                act.wait_ge(S["absd"], 2 * (p + 1))
                for x, dim in ((TC[:, 12 * p:12 * p + 12], "r g h p -> r (g h p)"),
                               (TK[:, NJ * p:NJ * p + NJ], "r j k a p -> r (j k a p)")):
                    x = x.rearrange(dim)
                    act.activation(x, x, ACT.Sin, bias=halfpi[0:R, :], scale=-PI).then_inc(S["cosines"], 1)

            def feature_tiles(x):
                for a in range(2):
                    ps, done = filled(act, ("qf", x, a))
                    if x >= 4:
                        k = jobs[("ret", x - 4)]
                        act.wait_ge(full[k % 8], k // 8 + 1)
                    act.activation(QF[:, (2 * x + a) % 8, :], ps[:, 0:2 * R], ACT.Copy).then_inc(done, 1)

            def retrieved_out(x):
                ps, done = filled(act, ("ret", x))
                act.wait_ge(S["ff"], x // 2 + 1)
                act.activation(CO[:, x, :], ps[0:R, 0:128], ACT.Copy).then_inc(done, 1)

            for event in back:
                kind, x = event[0:2]
                if kind == "features":
                    feature_tiles(x)
                elif kind == "retrieved":
                    retrieved_out(x)
                elif kind == "centre":
                    p = event[2]
                    src = xn_flat(p) if x == 3 else CO[:, NJ * p:NJ * p + NJ, :].rearrange("r j d -> r (j d)")
                    squares(x, p, src)
                elif kind == "transpose":
                    to_xt(x, event[2])

            for p in range(NP):
                for th in range(2):
                    name = ("rh", p, th)
                    ps, done = filled(act, name)
                    act.activation(RH[0:64, p * L + th * HALF:p * L + (th + 1) * HALF], ps[0:64, 0:HALF], ACT.Relu,
                                   bias=W["rb1"][0:64, :]).then_inc(done, 1)
            act.wait_ge(S["route1"], 1)
            act.activation(GE, GE, ACT.Exp).then_inc(S["route1_ex"], 1)
            act.wait_ge(S["route1"], 2)
            act.activation(g1[:, 3, :], g1[:, 2, :], ACT.Exp).then_inc(S["route1_ex"], 1)
            act.wait_ge(S["route1"], 3)
            act.activation(g1[:, 5, :], g1[:, 4, :], ACT.Exp).then_inc(S["route1_ex"], 1)

            def hidden_out(layer, x):
                a, p, th, ep = units1[x]
                name = (f"l{layer}", x)
                dst = H1[:, x % 4, :] if layer == 1 else H2[:, ep, p * L + th * HALF:p * L + (th + 1) * HALF]
                b_ = (W["e1b"] if layer == 1 else W["e2b"])[:, ep:ep + 1]
                ps, done = filled(act, name)
                act.activation(dst, ps[:, 0:HALF], ACT.Relu, bias=b_).then_inc(done, 1)

            for x in range(len(units1) + 1):
                if x < len(units1):
                    hidden_out(1, x)
                if x:
                    hidden_out(2, x - 1)

        @block.vector
        def _(dve):
            n_ = [0]

            def link(ins):
                n_[0] += 1
                ins.then_inc(S["dve_chain"], 1)
                dve.wait_ge(S["dve_chain"], n_[0])

            ps, done96 = filled(dve, "w96")
            link(dve.tensor_copy(W96[:, 0:OW + D], ps[0:96, 0:OW + D]))
            dve.tensor_scalar(bn[:, 0, :], W96[:, PAR + 4 * NB:PAR + 5 * NB], EPS, None, ALU.add)\
               .then_inc(S["bn_var"], 1)
            dve.wait_ge(S["consts"], 2)
            wk = W96[:, 0:PAR].rearrange("p (i o k) -> p i o k", i=NB, o=CIN)
            fk = Fw.rearrange("p (i k) c -> p i k c", k=KT)
            for s in range(NS):
                r = slice(32 * s, 32 * s + 32)
                for tap in range(KT):
                    last = dve.tensor_tensor(
                        fk[r, :, tap, 64 + 32 * s:96 + 32 * s].rearrange("p i (b o) -> p i b o", b=B),
                        wk[r, :, :, tap].unsqueeze(2).to_broadcast([32, NB, B, CIN]),
                        bmask[r].unsqueeze(1).unsqueeze(3).to_broadcast([32, NB, B, CIN]), ALU.mult)
            last.then_inc(S["conv_w"], 1)
            dve.wait_ge(S["bn_rstd"], 1)
            link(dve.tensor_tensor(bn[:, 1, :], bn[:, 1, :], W96[:, PAR + NB:PAR + 2 * NB], ALU.mult))
            link(dve.tensor_tensor(bn[:, 0, :], bn[:, 1, :], W96[:, PAR + 3 * NB:PAR + 4 * NB], ALU.mult))
            link(dve.tensor_tensor(bn[:, 2, :], W96[:, PAR + 2 * NB:PAR + 3 * NB], bn[:, 0, :], ALU.subtract))
            dve.sem_inc(S["w96"], 1)
            dve.sem_inc(done96, 1)
            for i in range(NB):
                link(dve.tensor_scalar(xs, xc, bn[:, 2, i:i + 1], None, ALU.add))
                if i == 1:
                    dve.tensor_tensor(Wout, rows(W96[:, OW:OW + D], NS * B), over(m24, NS * B, D), ALU.mult)
                if i == 5:
                    dve.wait_ge(S["dma_prep"], 16 * len(prep))
                    for h2 in range(2):
                        r = slice(64 * h2, 64 * h2 + 64)
                        last = dve.tensor_tensor(vox[r, :, 65 * h2:65 * h2 + D], voload[r, 0], voload[r, 1],
                                                 ALU.subtract)
                    last.then_inc(S["vo_ready"], 1)
                emptied(dve, ("conv", i))
                ins = dve.scalar_tensor_tensor(xc, xr, bn[:, 1, i:i + 1], xs, ALU.mult, ALU.add)
                ins.then_inc(S["conv_x"], 1)
                dve.wait_ge(S["conv_x"], i + 1)
                if i == 6:
                    x0, x1 = phases, trig[:, 0, :]
                    dve.tensor_scalar(x0[:, NJ * PP:], bias[0:R, WD:WD + WN], 0.1, None, ALU.mult)
                    link(dve.tensor_copy(x0[:, 0:NJ * PP], ppx.rearrange("r j p -> r (j p)")))
                    link(dve.tensor_scalar(x1, x0, 1.0 / (2 * np.pi), MAGIC, ALU.mult, ALU.add))
                    link(dve.tensor_scalar(x1, x1, MAGIC, None, ALU.subtract))
                    for c in (C1, C2, C3):
                        link(dve.scalar_tensor_tensor(x0, x1, -c, x0, ALU.mult, ALU.add))
                    link(dve.tensor_scalar(x0, x0, PI_IN, -PI_IN, ALU.min, ALU.max))
                    dve.scalar_tensor_tensor(x1, x0, -1.0, x0, ALU.mult, ALU.max).then_inc(S["trig_r"], 1)
            for half in range(2):
                for s in range(NS):
                    ps, done = filled(dve, ("h0", half, s))
                    for a in range(2):
                        last = dve.tensor_tensor(H[:, :, 2 * s + half, a, :],
                                                 ps[0:R, 256 * a:256 * a + 256].rearrange("r (p d) -> r p d", p=NP),
                                                 rows(outb[:, :], NP), ALU.add)
                    last.then_inc(done, 1)
            k = jobs[("h0", 1, NS - 1)]
            dve.wait_ge(free[k % 8], k // 8 + 1)

            def centre(k, p, src, dst):
                link(dve.reduce_sum(lnst[:, 0, p, :], src, AX))
                link(dve.tensor_scalar(lnst[:, 1, p, :], lnst[:, 0, p, :], -1.0 / D, None, ALU.mult))
                dve.tensor_tensor(dst, src, over(lnst[:, 1, p, :], 2 * NJ, D), ALU.add)\
                   .then_inc(S[f"centred{k}"], 1)

            def variance(k, p):
                dve.wait_ge(S[f"squared{k}"], p + 1)
                i = p % 2 if k < 2 else k - 2
                link(dve.reduce_sum(lnst[:, 0, p, :], SQ[:, i, :].rearrange("r (g d) -> r g d", d=D), AX))
                dve.tensor_scalar(lnst[:, 2, p, :], lnst[:, 0, p, :], 1.0 / D, EPS, ALU.mult, ALU.add)\
                   .then_inc(S[f"variance{k}"], 1)

            def normalize(k, p, dst):
                dve.wait_ge(S[f"rstd{k}"], p + 1)
                dve.tensor_tensor(dst, dst, over(lnst[:, 3, p, :], 2 * NJ, D), ALU.mult)\
                   .then_inc(S[f"normed{k}"], 1)

            dve.wait_ge(S["xbuf_zero"], 16 * E0)
            for p in range(2):
                centre(0, p, pairs(H, p), pairs(XN, p))
            for p in range(2):
                variance(0, p)
            for p in range(2):
                normalize(0, p, pairs(XN, p))

            for job in order:
                if job in ring_at:
                    k = ring_at[job]
                    ps = ring_bank[k % 2]
                    dve.wait_ge(S["ring_full"], k + 1)
                if job[0] == "score":
                    _, n, i = job
                    dve.reduce_max(MX[:, n % 2, i:i + 1], ps[0:R, 0:HALF], AX).then_inc(S["ring_free"], 1)
                    if i == 23:
                        dve.wait_ge(S["ring_free"], k + 1)
                        if n >= 2:
                            dve.wait_ge(S["shift_in"], n - 1)
                        dve.reduce_max(M1[:, n % 2, :], MX[:, n % 2, :].rearrange("r (t h) -> r t h", h=2), AX)\
                           .then_inc(S["mx_neg"], 1)
                elif job[0] == "proj":
                    _, b, g, qk, th = job
                    q = nproj[job]
                    dve.wait_ge(S["split1"], q + 1)
                    if q >= 2:
                        dve.wait_ge(S["split3"], q - 1)
                    dve.scalar_tensor_tensor(RR[:, q % 2, :], ps[:, 0:HALF], 0.125 if qk == 0 else 1.0,
                                             SP[:, qk, 0, th * HALF:(th + 1) * HALF], ALU.mult, ALU.subtract)\
                       .then_inc(S["ring_free"], 1)
                elif job[0] == "shift":
                    n = job[1]
                    if n >= 2:
                        dve.wait_ge(S["shift_dma"], 48 * (n - 1))
                    dve.tensor_copy(MT[:, n % 2, 0:R], ps[0:36, 0:63].bitcast(BF16)[:, 0:R]).then_inc(S["ring_free"], 1)
                elif job[0] == "xt":
                    _, which, b, h = job
                    p, a = b % NP, b // NP
                    r = slice(0, 128) if which == 1 else slice(64 * a, 64 * a + 64)
                    dve.tensor_copy(XT[r, p * L + h * HALF:p * L + (h + 1) * HALF], ps[r, 0:HALF])\
                       .then_inc(S["ring_free"], 1)
                elif job[0] == "logits":
                    dve.tensor_tensor(LG, ps[0:R, 0:NJ * E0].rearrange("r (g e) -> r g e", e=E0),
                                      rows(bias[0:R, GB:GB + E0], NJ), ALU.add).then_inc(S["ring_free"], 1)
                    dve.wait_ge(S["ring_free"], k + 1)
                elif job[0] == "choose":
                    link(dve.reduce_max(mx, LG, AX))
                    dve.tensor_tensor(LD, LG, over(mx, NJ, E0), ALU.subtract).then_inc(S["route_ld"], 1)
                    link(dve.tensor_tensor(EQ, LG, over(mx, NJ, E0), ALU.is_equal))
                    link(dve.tensor_tensor(EQ, EQ, rows(iota8, NJ), ALU.mult))
                    link(dve.tensor_reduce(im, EQ, AX, ALU.min))
                    dve.tensor_tensor(OH, rows(iota8, NJ), over(im, NJ, E0), ALU.is_equal).then_inc(S["onehot"], 1)
                elif job[0] == "pos":
                    b = job[1]
                    link(dve.tensor_tensor(PX, ps[0:R, 0:NJ * E0].rearrange("r (g e) -> r g e", e=E0), OH, ALU.mult))
                    dve.sem_inc(S["ring_free"], 1)
                    dve.wait_ge(S["route_ex"], b + 1)
                    dve.reduce_sum(pos, PX, AX)
                    link(dve.reduce_sum(sums, LD, AX))
                    dve.reciprocal(prob[:, NJ * b:NJ * b + NJ], sums).then_inc(S["pos_ready"], 1)
                elif job[0] == "ln_mean":
                    b = job[2]
                    if job[1] == 2:
                        dve.wait_ge(S["att_h"], NJ * (b + 1))
                    dve.reduce_sum(lnb[:, 0, :], H[:, b % NP, :, b // NP, :], AX).then_inc(S["lnb_sum"], 1)
                elif job[0] == "ln_std":
                    dve.wait_ge(S["lnb_x"], ln_at[job[1:3]] + 1)
                    dve.reduce_sum(lnb[:, 2, :], XSQ, AX).then_inc(S["lnb_ssq"], 1)
                elif job[0] == "out":
                    _, b, j, h = job
                    p, a = b % NP, b // NP
                    v = ps[0:R, 0:260].rearrange("r (h c) -> r h c", c=D + 1)
                    link(dve.reciprocal(RD[:, h, :].unsqueeze(2), v[:, :, D:D + 1]))
                    dve.tensor_tensor(OT[:, 4 * h:4 * h + 4, :], v[:, :, 0:D], over(RD[:, h, :], 4, D), ALU.mult)\
                       .then_inc(S["ring_free"], 1)
                    if h == 1:
                        dve.wait_ge(S["ring_free"], k + 1)
                        link(dve.reduce_sum(OR, OT.rearrange("r h d -> r d h"), AX))
                        dve.tensor_tensor(H[:, p, j, a, :], H[:, p, j, a, :], OR, ALU.add).then_inc(S["att_h"], 1)
            dve.wait_ge(S["att_h"], NJ * B)

            def copy_out(name, dst):
                ps, done = filled(dve, name)
                k = jobs[name]
                dve.tensor_copy(dst, ps[0:dst.shape[0], 0:dst.shape[1]]).then_inc(done, 1)

            for e in range(4):
                copy_out(("xbt", e, 1), XBT[:, e, 4 * R:8 * R])
            for kind, e in ffn_order:
                if kind == "h1":
                    for a in range(2):
                        for nn in range(2):
                            name = ("h1", e, a, 1, nn)
                            ps, done = filled(dve, name)
                            i = 2 * (e + 4 * a) + 1
                            dve.tensor_scalar(HM[:, e % 2, a, 1, nn * CH:(nn + 1) * CH], ps[:, 0:CH],
                                              W["b1"][:, i:i + 1], 0.0, ALU.add, ALU.max).then_inc(done, 1)
                elif kind == "yb":
                    copy_out(("yb", e, 1), XB[:, e, 4:8, :].rearrange("r c d -> r (c d)"))
            dve.wait_ge(S["big"], 2)

            def routed(p):
                dve.wait_ge(gathered[p], 16 * 12)
                y = YG[:, 12 * p:12 * p + 12, :]
                yf = y.rearrange("r g d -> r (g d)")
                w = pk.rearrange("r (a n j) -> r a n j", a=2, n=NP)[:, :, p, :].rearrange("r a j -> r j a")
                y4 = y.rearrange("r (j a) d -> r j a d", a=2)
                link(dve.tensor_tensor(y4, y4, w.unsqueeze(3).to_broadcast([R, NJ, 2, D]), ALU.mult))
                link(dve.tensor_scalar(msk[:, 0, :], yf, 3.4028235e38, None, ALU.is_gt))
                link(dve.copy_predicated(yf, mski[0], big[:, 0, :]))
                link(dve.tensor_scalar(msk[:, 0, :], yf, -3.4028235e38, None, ALU.is_lt))
                link(dve.copy_predicated(yf, mski[0], big[:, 1, :]))
                link(dve.tensor_tensor(msk[:, 1, :], yf, yf, ALU.not_equal))
                link(dve.copy_predicated(yf, mski[1], zero1[0:R, 0:1].to_broadcast([R, 768])))
                link(dve.tensor_tensor(pairs(H, p), pairs(H, p), y, ALU.add))

            def running_mean(p):
                for h in range(2):
                    emptied(dve, ("xt", 1, p, h))
                cols = slice(p * L, (p + 1) * L)
                link(dve.tensor_tensor_scan(CX[:, cols], ones[:, 0:1].to_broadcast([128, L]), XT[:, cols], 0.0,
                                            ALU.mult, ALU.add))
                dve.tensor_tensor(CX[:, cols], CX[:, cols], pos1, ALU.mult).then_inc(S["cx"], 1)

            def hop_hidden(p):
                for th in range(2):
                    ps, done = filled(dve, ("hop", p, th))
                    if p:
                        dve.wait_ge(S["hop_act"], 2 * (p - 1) + th + 1)
                    dve.tensor_tensor(HT[:, th, :], ps[:, 0:HALF], PPF[:, th * HALF:(th + 1) * HALF], ALU.add)\
                       .then_inc(done, 1)

            def tokens_out(p):
                for i in range(NJ * p, NJ * p + NJ):
                    ps, done = filled(dve, ("tok", i))
                    dve.tensor_tensor(CV[:, i].rearrange("r a c d -> r (a c d)"), ps[0:R, 0:256],
                                      bias[0:R, CVB:CVB + 256], ALU.add)
                    dve.tensor_tensor(TK[:, i].rearrange("r k a p -> r (k a p)"), ps[0:R, 256:384],
                                      bias[0:R, KSB:KSB + 128], ALU.add)
                    dve.tensor_tensor(GA[:, 1, 2 * i:2 * i + 2], ps[0:R, 384:386], bias[0:R, GTB:GTB + 2], ALU.add)\
                       .then_inc(done, 1)
                    ps, done = filled(dve, ("ao", i))
                    v = ps[0:R, 0:264].rearrange("r (g c) -> r g c", c=PP + 1)
                    bv = bias[0:R, AOB:AOB + 264].rearrange("r (g c) -> r g c", c=PP + 1)
                    dve.tensor_tensor(TC[:, 2 * i:2 * i + 2].rearrange("r g h p -> r (g h) p"), v[:, :, 0:PP],
                                      bv[:, :, 0:PP], ALU.add)
                    dve.tensor_tensor(WS[:, 8 * i:8 * i + 8].unsqueeze(2), v[:, :, PP:], bv[:, :, PP:], ALU.add)\
                       .then_inc(done, 1)

            for kind, p in front:
                if kind == "gathered":
                    routed(p)
                elif kind == "centre":
                    centre(1, p, pairs(H, p), pairs(XN, p))
                elif kind == "variance":
                    variance(1, p)
                elif kind == "normalize":
                    normalize(1, p, pairs(XN, p))
                elif kind == "mean":
                    if p == 0:
                        dve.wait_ge(S["pos"], 1)
                        link(dve.reciprocal(pos1, pos1))
                    running_mean(p)
                elif kind == "hidden":
                    hop_hidden(p)
                elif kind == "tokens":
                    tokens_out(p)
            G4 = NG * PH
            link(dve.tensor_tensor(hdl, bias[0:R, WD:WD + WN], bias[0:R, WD:WD + WN], ALU.mult))
            link(dve.tensor_scalar(hdl, hdl, -0.5, None, ALU.mult))
            dve.wait_ge(S["width"], 1)
            link(dve.tensor_scalar(WS, WS, 2.0, 0.1, ALU.mult, ALU.add))
            link(dve.tensor_tensor(WS, WS, WS, ALU.mult))
            link(dve.tensor_scalar(WS, WS, 1e-6, None, ALU.add))
            link(dve.reciprocal(WS, WS))
            dve.tensor_tensor(WE, over(WS, G4, WN), rows(hdl, G4), ALU.mult).then_inc(S["warg"], 1)
            dve.wait_ge(S["wexp"], 1)
            for i in range(2):
                link(dve.tensor_tensor(WX, WE, rows(trig[:, i, NJ * PP:], G4), ALU.mult))
                link(dve.reduce_sum(WA[:, i, :], WX, AX))
            link(dve.reduce_sum(WA[:, 2, :], WE, AX))
            link(dve.tensor_scalar(WA[:, 2, :], WA[:, 2, :], 1e-6, None, ALU.add))
            link(dve.reciprocal(WA[:, 2, :], WA[:, 2, :]))
            link(dve.tensor_scalar(WA[:, 2, :], WA[:, 2, :], RS / PH, None, ALU.mult))
            for i in range(2):
                last = dve.tensor_tensor(WA[:, i, :], WA[:, i, :], WA[:, 2, :], ALU.mult)
            link(last)
            dve.sem_inc(S["wab"], 1)
            ps, done = filled(dve, "gcum")
            ps2, done2 = filled(dve, "gtot")
            link(dve.tensor_copy(GA[:, 2, :], ps2[0:R, 0:NG]))
            dve.sem_inc(done2, 1)
            tot, pre = (GA[:, i, :].rearrange("r (p j a) -> r p j a", p=NP, a=2) for i in (2, 3))
            link(dve.memset(GA[:, 3, :], 0.0))
            for j in range(1, NJ):
                link(dve.tensor_tensor(pre[:, :, j, :], pre[:, :, j - 1, :], tot[:, :, j - 1, :], ALU.add))
            link(dve.tensor_tensor(GA[:, 4, :], ps[0:R, 0:NG], GA[:, 3, :], ALU.add))
            dve.sem_inc(done, 1)
            dve.tensor_scalar(GA[:, 4, :], GA[:, 4, :], 1.0, None, ALU.max).then_inc(S["gc"], 1)
            for p in range(NP):
                dve.wait_ge(S["sines"], 2 * (p + 1))
                for x, dim in ((TC[:, 12 * p:12 * p + 12], "r g h p -> r (g h p)"),
                               (TK[:, NJ * p:NJ * p + NJ], "r j k a p -> r (j k a p)")):
                    x = x.rearrange(dim)
                    dve.scalar_tensor_tensor(x, x, -1.0, x, ALU.mult, ALU.max).then_inc(S["absd"], 1)
            def chunk(q):
                p = q // 3
                g = slice(4 * q, 4 * q + 4)
                dve.wait_ge(S["cosines"], 2 * (p + 1))
                cc, sc = (x[:, g].rearrange("r g h p -> r (g h) p") for x in (TC, SC))
                wa, wb = (over(WA[:, i, 16 * q:16 * q + 16], 16, PP) for i in range(2))
                p0, p1 = (PT[:, q % 2, i].rearrange("r g h p -> r (g h) p") for i in (0, 1))
                dve.tensor_tensor(p0, cc, wa, ALU.mult)
                dve.tensor_tensor(p1, sc, wb, ALU.mult).then_inc(S["prod"], 1)
                dve.wait_ge(S["prod"], q + 1)
                link(dve.tensor_tensor(p0, p0, p1, ALU.subtract))
                dve.reduce_sum(UV[:, 0], PT[:, q % 2, 0].rearrange("r g h p -> r g p h"), AX)
                dve.wait_ge(S["vsum"], q + 1)
                dve.reduce_sum(UV[:, 1], PT[:, q % 2, 2].rearrange("r g h p -> r g p h"), AX).then_inc(S["uv"], 1)
                dve.wait_ge(S["uv"], q + 1)
                u, w = (UV[:, i].rearrange("r (j a) p -> r j a p", a=2) for i in (0, 1))
                t0, t1 = (UT[:, i].rearrange("r (j a) p -> r j a p", a=2) for i in (0, 1))
                j = 2 * (q % 3)
                cp, sp_ = (trig[:, i, j * PP:(j + 2) * PP].rearrange("r (j p) -> r j p", p=PP).unsqueeze(2)
                           .to_broadcast([R, 2, 2, PP]) for i in (0, 1))
                qc, qs = (QQ[:, g, 32 * i:32 * i + 32].rearrange("r (j a) p -> r j a p", a=2) for i in (0, 1))
                dve.tensor_tensor(t0, u, cp, ALU.mult)
                link(dve.tensor_tensor(t1, w, sp_, ALU.mult))
                link(dve.tensor_tensor(qc, t0, t1, ALU.subtract))
                dve.tensor_tensor(t0, u, sp_, ALU.mult)
                link(dve.tensor_tensor(t1, w, cp, ALU.mult))
                dve.tensor_tensor(qs, t0, t1, ALU.add).then_inc(S["qf_ready"], 1)

            mask = triu[0:R, 0:R].unsqueeze(1).to_broadcast([R, 2, R])

            def masked(x):
                p, j = divmod(x, NJ)
                for k2 in range(2):
                    ps, done = filled(dve, ("sm", x, k2))
                    if x >= 4 and k2 == 0:
                        k = jobs[("ret", x - 4)]
                        dve.wait_ge(full[k % 8], k // 8 + 1)
                    dve.tensor_tensor(SM[:, x % 4, k2], ps[0:R, 0:2 * R].rearrange("r (a c) -> r a c", a=2), mask,
                                      ALU.mult).then_inc(done, 1)
                if j < NJ - 1:
                    ps, done = filled(dve, ("state", x))
                    for c in range(2):
                        r = slice(64 * c, 64 * c + 64)
                        delta = ps[r, 0:256].rearrange("r (a c d) -> r a c d", a=2, c=2)[:, :, c, :]
                        if j == 0:
                            ins = dve.tensor_copy(ST[r, p % 2, 1], delta)
                        else:
                            ins = dve.tensor_tensor(ST[r, p % 2, j + 1], ST[r, p % 2, j], delta, ALU.add)
                        ins.then_inc(S["state"], 1)
                    dve.wait_ge(S["state"], 2 * (p * (NJ - 1) + j + 1))
                    dve.sem_inc(done, 1)

            for event in back:
                kind, x = event[0:2]
                if kind == "chunk":
                    chunk(x)
                elif kind == "masked":
                    masked(x)
                elif kind == "product":
                    p = event[2]
                    for h in range(2):
                        ps, done = filled(dve, ("product", p, h))
                        dve.wait_ge(S["h_pre"], p + 1)
                        v = H[:, p, 3 * h:3 * h + 3].rearrange("r j a d -> r (j a d)")
                        dve.tensor_tensor(v, v, ps[0:R, 0:3 * 128], ALU.add).then_inc(done, 1)
                elif kind in ("centre", "variance", "normalize"):
                    p = event[2]
                    if x == 2:
                        src = dst = CO[:, NJ * p:NJ * p + NJ, :].rearrange("r j (a d) -> r (j a) d", a=2)
                    else:
                        src, dst = pairs(H, p), pairs(XN, p)
                    if kind == "centre":
                        for i in range(NJ if x == 2 else 0):
                            emptied(dve, ("ret", NJ * p + i))
                        for h in range(2 if x == 3 else 0):
                            emptied(dve, ("product", p, h))
                        centre(x, p, src, dst)
                    elif kind == "variance":
                        variance(x, p)
                    else:
                        normalize(x, p, dst)

            ps, done = filled(dve, "logits1")
            link(dve.tensor_tensor(GL, ps[0:R, 0:NG * E1].rearrange("r (g e) -> r g e", e=E1),
                                   rows(bias[0:R, RB2:RB2 + E1], NG), ALU.add))
            dve.sem_inc(done, 1)
            m1, i1, d2, x2, ww, w1_, m2, t2 = (g1[:, i, :] for i in range(8))
            i6 = rows(iota8[:, 0:E1], NG)
            link(dve.reduce_max(m1, GL, AX))
            dve.tensor_tensor(GE, GL, over(m1, NG, E1), ALU.subtract).then_inc(S["route1"], 1)
            link(dve.tensor_tensor(GC, GL, over(m1, NG, E1), ALU.is_equal))
            link(dve.tensor_tensor(GC, GC, i6, ALU.mult))
            link(dve.tensor_reduce(i1, GC, AX, ALU.min))
            link(dve.tensor_tensor(GO, i6, over(i1, NG, E1), ALU.is_equal))
            link(dve.scalar_tensor_tensor(GC, GO, -3.0e38, GL, ALU.mult, ALU.add))
            link(dve.reduce_max(m2, GC, AX))
            dve.tensor_tensor(d2, m2, m1, ALU.subtract).then_inc(S["route1"], 1)
            link(dve.tensor_tensor(GC, GC, over(m2, NG, E1), ALU.is_equal))
            link(dve.tensor_tensor(GC, GC, i6, ALU.mult))
            link(dve.tensor_reduce(i1, GC, AX, ALU.min))
            link(dve.tensor_tensor(GW, i6, over(i1, NG, E1), ALU.is_equal))
            dve.wait_ge(S["route1_ex"], 2)
            link(dve.reduce_sum(t2, GE, AX))
            link(dve.reciprocal(t2, t2))
            link(dve.tensor_scalar(x2, x2, 1.0, None, ALU.subtract))
            dve.tensor_tensor(ww, x2, t2, ALU.mult).then_inc(S["route1"], 1)
            dve.wait_ge(S["route1_ex"], 3)
            link(dve.tensor_scalar(t2, w1_, 1.0, None, ALU.add))
            link(dve.reciprocal(t2, t2))
            link(dve.tensor_tensor(w1_, w1_, t2, ALU.mult))
            dve.tensor_tensor(GO, GO, over(t2, NG, E1), ALU.mult)
            link(dve.tensor_tensor(GW, GW, over(w1_, NG, E1), ALU.mult))
            link(dve.tensor_tensor(GW, GW, GO, ALU.add))
            x = 0
            for a in range(2):
                for p in range(NP):
                    for j in range(NJ):
                        ps, done = filled(dve, ("l3", a, p, j))
                        k = jobs[("l3", a, p, j)]
                        yo = YO[:, x % 2]
                        dve.tensor_tensor(yo, ps[0:R, 0:384].rearrange("r (e d) -> r e d", e=E1),
                                          bias[0:R, EB3:EB3 + 384].rearrange("r (e d) -> r e d", e=E1), ALU.add)\
                           .then_inc(done, 1)
                        dve.wait_ge(free[k % 8], k // 8 + 1)
                        g = (p * NJ + j) * 2 + a
                        link(dve.tensor_tensor(yo, yo, over(GW[:, g, :], E1, D), ALU.mult))
                        link(dve.reduce_sum(YR[:, x % 2, :], yo.rearrange("r e d -> r d e"), AX))
                        dve.tensor_tensor(H[:, p, j, a, :], H[:, p, j, a, :], YR[:, x % 2, :], ALU.add)\
                           .then_inc(S["h4"], 1)
                        x += 1


_INS = ['x', 'L0_tok_conv_w', 'L0_tok_conv_b', 'L0_tok_bn_gamma', 'L0_tok_bn_beta', 'L0_tok_bn_mean',
        'L0_tok_bn_var', 'L0_tok_out_w', 'L0_tok_out_b', 'L0_attn_Q', 'L0_attn_K', 'L0_attn_VO',
        'L0_ffn_gate_w', 'L0_ffn_gate_b', 'L0_ffn_w1', 'L0_ffn_b1', 'L0_ffn_w2', 'L0_ffn_b2',
        'L1_attn_pos_phases', 'L1_attn_window_deltas', 'L1_attn_mc_w', 'L1_attn_mc_b', 'L1_attn_hop_w1',
        'L1_attn_hop_b1', 'L1_attn_hop_w2', 'L1_attn_hop_b2', 'L1_attn_cpe_w', 'L1_attn_cpe_b', 'L1_attn_ve_w',
        'L1_attn_ve_b', 'L1_attn_kce_w', 'L1_attn_kce_b', 'L1_attn_ksk_w1', 'L1_attn_ksk_b1', 'L1_attn_ksk_w2',
        'L1_attn_ksk_b2', 'L1_attn_sg_w1', 'L1_attn_sg_b1', 'L1_attn_sg_w2', 'L1_attn_sg_b2', 'L1_attn_ln_g',
        'L1_attn_ln_b', 'L1_attn_out_w', 'L1_attn_out_b', 'L1_ffn_router_w1', 'L1_ffn_router_b1',
        'L1_ffn_router_w2', 'L1_ffn_router_b2', 'L1_ffn_expert_w1', 'L1_ffn_expert_b1', 'L1_ffn_expert_w2',
        'L1_ffn_expert_b2', 'L1_ffn_expert_w3', 'L1_ffn_expert_b3']


def kernel(**inputs):
    import concourse.bacc as bacc
    from concourse.bass_utils import run_bass_kernel_spmd

    nc = bacc.Bacc("TRN2", target_bir_lowering=False, num_devices=1)
    arrays, args = {}, {}
    for name in _INS:
        a = np.ascontiguousarray(inputs[name])
        arrays[f"in_{name}"] = a
        args[name] = nc.dram_tensor(f"in_{name}", a.shape, mybir.dt.from_np(a.dtype), kind="ExternalInput").ap()
    out = nc.dram_tensor("out_0", (B, L, D), F32, kind="ExternalOutput").ap()
    build(nc, args, out)
    r = run_bass_kernel_spmd(nc, [arrays], core_ids=[0])
    return r.results[0]["out_0"]
```

```python
from contextlib import ExitStack

import concourse.bass as bass
import numpy as np
from concourse import mybir

F32 = mybir.dt.float32
BF16 = mybir.dt.bfloat16
U32 = mybir.dt.uint32
ALU = mybir.AluOpType
ACT = mybir.ActivationFunctionType
AX = mybir.AxisListType.X

B, CIN, L, D = 8, 4, 750, 64
NP, NJ, R = 4, 6, 125
NT, NG = NP * NJ, NP * NJ * 2
HALF = L // 2
NB, KT = 9, 3
NS, SEG = 3, 250
HEADS, QR = 8, 32
E0, F0 = 8, 256
CAP = -(-(5 * B * L) // (4 * E0))
CH = CAP // 2
ROWS = 1000
PH, PP, WN = 4, 32, 5
E1 = 6
EPS = 1e-5
PI_IN = 3.1415925
PI = float(np.float32(np.pi))
MAGIC = 12582912.0
C1 = 6.28125
C2 = 0.0019350051879882812
C3 = 2 * np.pi - C1 - C2
RS = 1.0 / np.sqrt(float(PP))

GB, CVB, KSB, GTB, AOB, LNG, LNB, OB, RB2, EB3, WD = (
    0, 8, 264, 392, 394, 658, 722, 786, 850, 856, 1240)
NBIAS = 1245


def build(nc, t, out):
    with ExitStack() as ctx:
        ctx.enter_context(nc.allow_non_contiguous_dma(reason="small weights are laid out on their way in"))
        def sb(name, shape, dt=F32):
            return ctx.enter_context(nc.sbuf_tensor(name, shape, dt))[tuple(slice(None) for _ in shape)]

        psum = ctx.enter_context(nc.psum_tensor("psum", [128, 8, 512], F32))
        bank = [psum[:, i, :] for i in range(8)]
        xbuf = nc.dram_tensor("expert_in", [E0 * ROWS, D], F32, kind="Internal").ap()
        ybuf = nc.dram_tensor("expert_out", [E0 * ROWS, D], F32, kind="Internal").ap()

        H = sb("H", [R, NP, NJ, 2, D])
        XN = sb("XN", [R, NP, NJ, 2, D])
        XT = sb("XT", [128, NP * L])
        ident = sb("ident", [128, 128])
        identb = sb("identb", [128, 128], BF16)
        triu = sb("triu", [128, 128])
        ones = sb("ones", [128, 128])
        mhalf = sb("mhalf", [128, 64])
        zero1 = sb("zero1", [128, 1])
        lnst = sb("lnst", [R, 4, NP, 2 * NJ])
        bias = sb("bias", [128, NBIAS])
        iota8 = sb("iota8", [R, 8])
        trig = sb("trig", [R, 2, NJ * PP + WN])
        halfpi = sb("halfpi", [128, 1])
        big = sb("big", [128, 2])

        WCOLS = [("gw", 16), ("hop1", 128), ("hop2", 264), ("wta", 320), ("ksk1", 128), ("ksm", 128), ("sg1", 64),
                 ("ksk2", 64), ("sg2", 2), ("outw", 128),
                 ("rw1", 64), ("rw2", 12), ("b1", 16), ("b2", 4), ("e1b", 3), ("e2b", 3), ("kb", 1), ("sgb1", 1),
                 ("hopb", 1), ("rb1", 1)]
        wall = sb("wall", [128, sum(n for _, n in WCOLS)])
        W, at = {}, 0
        for name, n in WCOLS:
            W[name] = wall[:, at:at + n]
            at += n
        qkp = sb("qkp", [128, 2, 2, HEADS * QR])
        vox = sb("vox", [128, 4, 130])
        slot_in = sb("slot_in", [R, NG], U32)
        slot_out = sb("slot_out", [R, NG], U32)
        prob = sb("prob", [R, NG])
        pk = sb("pk", [R, NG])

        ASIZE = 37660
        arena = sb("arena", [128, ASIZE])

        def view(at, shape, dt=F32, parts=128):
            n = int(np.prod(shape))
            w = n if dt != BF16 else (n + 1) // 2
            assert at + w <= ASIZE, (at, shape)
            v = arena[0:parts, at:at + w]
            if dt != F32:
                v = v.bitcast(dt)
            if len(shape) > 1:
                dims = [f"d{i}" for i in range(len(shape))]
                v = v.rearrange(f"p ({' '.join(dims)}) -> p {' '.join(dims)}", **dict(zip(dims[1:], shape[1:])))
            return v, at + w

        Fw, at = view(0, [NB * KT, 160], parts=96)
        Wout, at = view(at, [NS * B, D], parts=96)
        P4, at = view(at, [256], parts=4)
        W96, at = view(at, [256], parts=96)
        xc, at = view(at, [SEG], parts=96)
        xs, at = view(at, [SEG], parts=96)
        xr, at = view(at, [SEG], parts=96)
        bmask, at = view(at, [B], parts=96)
        m24, at = view(at, [NS * B], parts=96)
        R4, at = view(at, [96], parts=4)
        bn, at = view(at, [3, NB], parts=96)
        ppt, at = view(at, [NJ * R], parts=PP)
        outb, at = view(at, [D], parts=R)
        phases, at = view(at, [NJ * PP + WN], parts=R)
        ppx, at = view(at, [NJ, PP], parts=R)
        qload, at = view(at, [2, 2, 192])
        voload, at = view(at, [2, 4, D])
        early = [("hop1b", 128), ("kskb", 128), ("kcet", 128), ("kce", 64), ("kb1", 1), ("kceb", 1)]
        wearly, at = view(at, [sum(n for _, n in early)])
        col = 0
        for name, n in early:
            W[name] = wearly[:, col:col + n]
            col += n
        zeros = XN[:, 0].rearrange("r j a d -> r (j a d)")[:, 0:512]
        PAR, OW = NB * CIN * KT, NB * CIN * KT + 5 * NB
        SQ, at_sq = view(ASIZE - 3 * 768, [3, 768], parts=R)
        assert at <= ASIZE - 3 * 768
        PPF = sb("PPF", [128, L])

        QA, at = view(0, [2, HEADS, L], BF16)
        QB, at = view(at, [2, HEADS, L], BF16)
        KA, at = view(at, [2, HEADS, L], BF16)
        KB, at = view(at, [2, HEADS, L], BF16)
        SP, at = view(at, [2, 3, L], BF16)
        RR, at = view(at, [2, HALF])
        CT, at = view(at, [2, 4, L])
        PR, at = view(at, [4, L], parts=R)
        MX, at = view(at, [2, 24], parts=R)
        M1, at = view(at, [2, 12], parts=R)
        MR, at = view(at, [2, 12], parts=R)
        NM, at = view(at, [2, 36], BF16, parts=R)
        MT, at = view(at, [2, 126], BF16, parts=36)
        RD, at = view(at, [2, 4], parts=R)
        OT, at = view(at, [8, D], parts=R)
        OR, at = view(at, [D], parts=R)
        XSQ, at = view(at, [NJ, D], parts=R)
        lnb, at = view(at, [4, NJ], parts=R)
        LG, at = view(at, [NJ, E0], parts=R)
        LD, at = view(at, [NJ, E0], parts=R)
        EQ, at = view(at, [NJ, E0], parts=R)
        OH, at = view(at, [NJ, E0], parts=R)
        SO, at = view(at, [NJ + 1, E0], parts=R)
        PX, at = view(at, [NJ, E0], parts=R)
        r1, at = view(at, [9, NJ], parts=R)

        w1p, at = view(0, [E0, F0])
        w2e, at = view(at, [E0, 2, D])
        XB, at = view(at, [4, 8, 128], parts=R)
        XBT, at = view(at, [4, ROWS])
        HM, at = view(at, [2, 2, 2, CAP])
        YT, at = view(at, [4, ROWS])
        msk = SQ[:, 0, :]
        mski = msk.bitcast(U32)
        assert at <= ASIZE - 3 * 768

        HG, at = view(0, [2 * L])
        KG, at = view(at, [2 * L])
        SG, at = view(at, [2 * L])
        CX, at = view(at, [2 * L])
        CV, at = view(at, [3 * NJ, 2, 2, D], parts=R)
        TC, at = view(at, [6 * NJ, PH, PP], parts=R)
        TK, at = view(at, [3 * NJ, 2, 2, PP], parts=R)
        SC, at = view(at, [6 * NJ, PH, PP], parts=R)
        SK, at = view(at, [3 * NJ, 2, 2, PP], parts=R)
        QQ = TC.rearrange("r g h p -> r g (h p)")
        FF = SC.rearrange("r g h p -> r g (h p)")
        QF, at = view(at, [8, 2 * R])
        PT, at = view(at, [4, 4, PH, PP], parts=R)
        UV, at = view(at, [2, 4, PP], parts=R)
        UT, at = view(at, [2, 4, PP], parts=R)
        SM, at = view(at, [4, 2, 2, R], parts=R)
        ST, at = view(at, [2, NJ, 2, D])
        WS, at = view(at, [NG * PH], parts=R)
        WA, at = view(at, [3, NG * PH], parts=R)
        WE, at = view(at, [2 * NJ * PH, WN], parts=R)
        WX, at = view(at, [2 * NJ * PH, WN], parts=R)
        GA, at = view(at, [6, NG], parts=R)
        hdl, at = view(at, [WN], parts=R)
        pos1, at = view(at, [L])
        assert at <= ASIZE - 3 * 768, at

        e1w, at = view(0, [2, 3, 128])
        e2w, at = view(at, [3, 128])
        e3w, at = view(at, [3, 128])
        RH, at = view(at, [NP * L])
        H1, at = view(at, [4, HALF])
        H2, at = view(at, [3, NP * L])
        GL, at = view(at, [NG, E1], parts=R)
        GE, at = view(at, [NG, E1], parts=R)
        GO, at = view(at, [NG, E1], parts=R)
        GC, at = view(at, [NG, E1], parts=R)
        GW, at = view(at, [NG, E1], parts=R)
        g1, at = view(at, [8, NG], parts=R)
        YO, at = view(at, [2, 6, D], parts=R)
        YR, at = view(at, [2, D], parts=R)
        assert at <= ASIZE - 3 * 768, at

        S = {}

        def sem(*names):
            for n in names:
                S[n] = ctx.enter_context(nc.semaphore(n))

        sem(*[f"bank_full{i}" for i in range(8)], *[f"bank_free{i}" for i in range(8)])
        sem(*[f"{what}{k}" for k in range(4) for what in ("centred", "squared", "variance", "normed")])
        sem("dve_chain", "pool_chain")
        sem("zeroed", "dma_conv", "dma_weights", "consts", "w96", "conv_w", "bn_var", "bn_rstd", 
            "conv_x", "vo_ready", "xbuf_zero",
            "ppt", "ppf", "trig_r", "trig_done")
        sem("ring_full", "ring_free", "split1", "split3", "qk_dma0", "qk_dma1", "kb_ones", "v_ready",
            "mx_neg", "shift_in", "shift_dma", "st_done", "exp_done", "pv_done", "ctx_out",
            "att_h", "lnb_sum", "lnb_x", "lnb_ssq", "lnb_done", "onehot_sum", "pos_ready", "memory", "dma_prep")
        sem("late_zero", "w_late", "big", "route_ld", "route_ex", "onehot", "slots", "scattered", "xb_loaded",
            "y_stored", "gathered0", "gathered1", "gathered2", "gathered3",
            "pos", "cx", "hop_act", "tanh", "width", "gate", "warg", "wexp", "wab", "gc", "sines", "absd",
            "cosines", "prod", "vsum", "uv", "qf_ready", "ff", "state", "h_pre", "lnx",
            "route1", "route1_ex", "h4", "stored")
        gathered = [S["gathered0"], S["gathered1"], S["gathered2"], S["gathered3"]]
        full = [S[f"bank_full{i}"] for i in range(8)]
        free = [S[f"bank_free{i}"] for i in range(8)]

        jobs = {}

        def take(pe, name):
            k = len(jobs)
            jobs[name] = k
            if k >= 8:
                pe.wait_ge(free[k % 8], k // 8)
            return bank[k % 8], full[k % 8]

        def filled(eng, name):
            k = jobs[name]
            eng.wait_ge(full[k % 8], k // 8 + 1)
            return bank[k % 8], free[k % 8]

        def emptied(eng, name):
            k = jobs[name]
            eng.wait_ge(free[k % 8], k // 8 + 1)

        def pairs(buf, p):
            return buf[:, p].rearrange("r j a d -> r (j a) d")

        def held(p):
            return slice(NJ * (p % 3), NJ * (p % 3) + NJ)

        def held2(p):
            return slice(2 * NJ * (p % 3), 2 * NJ * (p % 3) + 2 * NJ)

        def phases_of(p, heads, keys):
            return (heads[:, held2(p)].rearrange("r g h p -> r (g h p)"),
                    keys[:, held(p)].rearrange("r j k a p -> r (j k a p)"))

        def over(ap, n, width):
            return ap.unsqueeze(2).to_broadcast([ap.shape[0], n, width])

        def rows(ap, n):
            return ap.unsqueeze(1).to_broadcast([ap.shape[0], n, ap.shape[1]])

        taps = []
        for i in range(NB):
            mm = [(2, 0, 0, SEG, 0)]
            for tap, shift in ((1, 2 ** i), (0, 2 ** (i + 1))):
                q, r = divmod(shift, SEG)
                if q < NS:
                    mm.append((tap, q, r, SEG, 0))
                if q + 1 < NS and r:
                    mm.append((tap, q + 1, 0, r, SEG - r))
            taps.append(mm)

        NU = 4 * B
        mx, im, pos, sums, kept, sl, sx, tx, sy = (r1[:, i, :] for i in range(9))
        events = [("gathered", 0), ("centre", 1, 0), ("variance", 1, 0), ("gathered", 1), ("centre", 1, 1),
                  ("transpose", 1, 0), ("mean", 0), ("variance", 1, 1), ("hidden", 0), ("tokens", 0, 0),
                  ("tokens", 0, 1), ("transpose", 1, 1), ("widths", 0), ("sines", 0), ("mean", 1), ("weights", 0),
                  ("cosines", 0), ("chunk", 0)]
        for x in range(NT + 14):
            p, k = divmod(x, NJ)
            if x < NT:
                events.append(("features", x))
            if x < NT and k in (0, 2):
                events.append(("chunk", 3 * p + 1 + k // 2))
            if 1 <= x <= NT:
                events.append(("masked", x - 1))
            if 2 <= x < NT + 2:
                events.append(("retrieved", x - 2))
            if p + 1 < NP:
                events += [[("hidden", p + 1)], [("tokens", p + 1, 0)], [("tokens", p + 1, 1)],
                           [("widths", p + 1), ("sines", p + 1)], [("weights", p + 1), ("cosines", p + 1)],
                           [("chunk", 3 * p + 3)]][k]
            if p + 2 < NP:
                events.append([("gathered", p + 2), ("centre", 1, p + 2), ("variance", 1, p + 2),
                               ("normalize", 1, p + 2), ("transpose", 1, p + 2), ("mean", p + 2)][k])
            for p in range(NP):
                k = x - NJ * (p + 1) - 2
                if 0 <= k <= 11 and k not in (3, 9, 10):
                    events.append((("centre", "variance", "normalize", "", "transpose", "product",
                                    "centre", "variance", "normalize", "", "", "transpose")[k], 2 + k // 6, p))
            if x == 3 * NJ:
                events.append(("room", 0))
        ffn_order = [("h1", 0), ("h1", 1), ("y", 0), ("h1", 2), ("y", 1), ("yb", 0), ("h1", 3), ("y", 2), ("yb", 1),
                     ("y", 3), ("yb", 2), ("yb", 3)]
        units1 = [(a, p, th, ep) for a in range(2) for p in range(NP) for th in range(2) for ep in range(3)]

        lns = [(1, 2), (1, 2 + NP)]
        for b in range(B):
            if b == 1:
                lns += [(1, 3), (1, 3 + NP)]
            if b:
                lns.append((2, b - 1))
        lns.append((2, B - 1))
        ln_at = {x: k for k, x in enumerate(lns)}

        def ring_jobs(n, c):
            found = []
            if n + 2 < NU:
                found += [("score", n + 2, 4 * c + i) for i in range(4)]
            if c == 1 and n + 1 < NU:
                found.append(("shift", n + 1))
            b, hp = divmod(n, 4)
            if hp < 2 and b + 1 < B and c >= 2:
                found.append(("proj", b + 1, hp, (c - 2) // 2, c % 2))
            k = 6 * hp + c - 2
            if b > 0 and 0 <= k < 12:
                found.append(("out", b - 1, k // 2, k % 2))
            if b < 2 and hp == 2 and c < 2:
                found.append(("xt", 1, b + 2, c))
            if b > 0 and hp == 3:
                found += {0: [("xt", 2, b - 1, 0)], 1: [("xt", 2, b - 1, 1)], 2: [("logits", b - 1)],
                          4: [("pos", b - 1)]}.get(c, [])
            return found

        def side_jobs(n, c):
            b, hp = divmod(n, 4)
            found = []
            if b < 2 and hp < 2 and c in (2, 4):
                found.append(("ln_mean" if c == 2 else "ln_std", 1, b + 2 + NP * hp))
            if b > 0:
                if hp == 2 and c in (3, 4):
                    found.append(("ln_mean" if c == 3 else "ln_std", 2, b - 1))
                if hp == 3 and c in (2, 3):
                    found.append(("choose" if c == 2 else "weigh", b - 1))
            if b > 1:
                if hp == 0 and c == 2:
                    found.append(("slots", b - 2))
                if hp < 2 and c >= 3:
                    found.append(("scatter", b - 2, 3 * hp + c - 3))
            return found

        before = [("proj", 0, 0, qk, th) for qk in range(2) for th in range(2)]
        before += [("score", 0, i) for i in range(24)] + [("shift", 0)]
        before += [("proj", 0, 1, qk, th) for qk in range(2) for th in range(2)]
        before += [("score", 1, i) for i in range(24)]
        b = B - 1
        after = [("slots", b - 1)] + [("scatter", b - 1, j) for j in range(NJ)]
        after += [("out", b, j, h) for j in range(NJ) for h in range(2)]
        after += [("ln_mean", 2, b), ("ln_std", 2, b), ("xt", 2, b, 0), ("xt", 2, b, 1), ("logits", b), ("choose", b),
                  ("weigh", b), ("pos", b), ("slots", b)] + [("scatter", b, j) for j in range(NJ)]
        order = before + [x for n in range(NU) for c in range(6) for x in ring_jobs(n, c) + side_jobs(n, c)] + after
        on_ring = ("proj", "score", "shift", "out", "xt", "logits", "pos")
        ring_at = {x: k for k, x in enumerate(y for y in order if y[0] in on_ring)}
        nproj = {x: k for k, x in enumerate(y for y in order if y[0] == "proj")}
        ring_bank = [bank[0], bank[1]]
        st_bank = [[bank[2], bank[3]], [bank[4], bank[5]]]
        ctx_bank = [bank[6], bank[7]]

        wd = []
        prep = []
        for qk, name in enumerate(("L0_attn_Q", "L0_attn_K")):
            prep.append((qload[:, qk, :, 64:128], t[name].rearrange("(g h) r d -> (h r) g d", g=2)))
        for h2 in range(2):
            rowsl = slice(64 * h2, 64 * h2 + 64)
            vo = t["L0_attn_VO"].rearrange("(hp h) d e -> h d hp e", h=2)[h2]
            prep.append((voload[rowsl, 0, :, :], vo))
            prep.append((voload[rowsl, 1, :, :], t["L0_attn_VO"].rearrange("(hp h) d e -> h d hp e", h=2)[h2, 63]
                       .partition_broadcast(64)))
        for a in range(2):
            r = slice(64 * a, 64 * a + 64)
            wd += [(W["gw"][r, 8 * a:8 * a + 8], t["L0_ffn_gate_w"]),
                   (W["hop1"][r, 64 * a:64 * a + 64], t["L1_attn_hop_w1"][0:64]),
                   (W["hop2"][r, 132 * a:132 * a + 132], t["L1_attn_hop_w2"]),
                   (W["wta"][r, 128 * a:128 * a + 64], t["L1_attn_mc_w"]),
                   (W["wta"][r, 128 * a + 64:128 * a + 128], t["L1_attn_ve_w"]),
                   (W["wta"][r, 256 + 32 * a:288 + 32 * a], t["L1_attn_cpe_w"]),
                   (W["ksk1"][r, 64 * a:64 * a + 64], t["L1_attn_ksk_w1"][0:64]),
                   (W["sg1"][r, 32 * a:32 * a + 32], t["L1_attn_sg_w1"]),
                   (W["ksk2"][r, 32 * a:32 * a + 32], t["L1_attn_ksk_w2"]),
                   (W["sg2"][32 * a:32 * a + 32, a:a + 1], t["L1_attn_sg_w2"]),
                   (W["outw"][r, 64 * a:64 * a + 64], t["L1_attn_out_w"]),
                   (W["rw1"][r, 32 * a:32 * a + 32], t["L1_ffn_router_w1"]),
                   (W["rw2"][32 * a:32 * a + 32, 6 * a:6 * a + 6], t["L1_ffn_router_w2"]),
                   (W["b2"][r, :], t["L0_ffn_b2"][4 * a:4 * a + 4].rearrange("e d -> d e")),
                   (W["e1b"][r, :], t["L1_ffn_expert_b1"].rearrange("(ep e) h -> e h ep", e=2)[a]),
                   (W["e2b"][r, :], t["L1_ffn_expert_b2"].rearrange("(ep e) h -> e h ep", e=2)[a]),
                   (W["sgb1"][32 * a:32 * a + 32, :], t["L1_attn_sg_b1"].unsqueeze(1)),
                   (W["rb1"][32 * a:32 * a + 32, :], t["L1_ffn_router_b1"].unsqueeze(1))]
            prep += [(W["hop1b"][0:32, 64 * a:64 * a + 64], t["L1_attn_hop_w1"][64:96]),
                     (W["kskb"][0:64, 64 * a:64 * a + 64], t["L1_attn_ksk_w1"][64:128]),
                     (W["kb1"][r, :], t["L1_attn_ksk_b1"].unsqueeze(1)),
                     (W["hopb"][r, :], t["L1_attn_hop_b1"].unsqueeze(1))]
            for at_, name, n in ((CVB + 128 * a, "mc_b", 64), (CVB + 128 * a + 64, "ve_b", 64),
                                 (KSB + 32 * a, "cpe_b", 32), (KSB + 64 + 32 * a, "ksk_b2", 32),
                                 (GTB + a, "sg_b2", 1), (AOB + 132 * a, "hop_b2", 132)):
                wd.append((bias[:, at_:at_ + n], t["L1_attn_" + name].partition_broadcast(128)))
        for at_, name, n in ((GB, "L0_ffn_gate_b", 8), (LNG, "L1_attn_ln_g", 64), (LNB, "L1_attn_ln_b", 64),
                             (OB, "L1_attn_out_b", 64), (RB2, "L1_ffn_router_b2", 6)):
            wd.append((bias[:, at_:at_ + n], t[name].partition_broadcast(128)))
        wd.append((bias[:, EB3:EB3 + 384], t["L1_ffn_expert_b3"].rearrange("e d -> (e d)").partition_broadcast(128)))
        wd.append((W["b1"][:, :], t["L0_ffn_b1"].rearrange("e (h f) -> f (e h)", h=2)))
        prep.append((bias[:, WD:WD + WN], t["L1_attn_window_deltas"].partition_broadcast(128)))
        prep.append((W["kceb"][0:64, :], t["L1_attn_kce_b"].unsqueeze(1)))
        prep.append((W["kce"][0:64, :], t["L1_attn_kce_w"]))
        prep.append((ppx[:, :, :], t["L1_attn_pos_phases"][0:L].rearrange("(j r) p -> r j p", r=R)))

        block = ctx.enter_context(nc.Block())

        @block.tensor
        def _(pe):
            pe.wait_ge(S["dma_conv"], 16 * 11)
            pe.wait_ge(S["consts"], 1)
            ps, done = take(pe, "w96")
            pe.matmul(ps[0:96, 0:OW + D], R4, P4[:, 0:OW + D], start=True, stop=True).then_inc(done, 1)
            pe.wait_ge(S["conv_w"], 1)
            for i in range(NB):
                ps, done = take(pe, ("conv", i))
                if i:
                    pe.wait_ge(S["conv_x"], i)
                for n, (tap, q, lo, hi, src) in enumerate(taps[i]):
                    last = pe.matmul(ps[0:96, lo:hi], Fw[:, i * KT + tap, 64 - 32 * q:160 - 32 * q],
                                     xc[:, src:src + hi - lo], start=(n == 0), stop=(n == len(taps[i]) - 1))
                last.then_inc(done, 1)
                if i == 4:
                    pe.wait_ge(S["dma_prep"], 16 * len(prep))
                    pe.wait_ge(S["consts"], 2)
                    for qk in range(2):
                        for a in range(2):
                            ps, done = take(pe, ("qkp", qk, a))
                            for g in range(2):
                                last = pe.transpose(ps[:, g * 128:(g + 1) * 128],
                                                    qload[:, qk, g, 64 - 64 * a:192 - 64 * a], ident)
                            last.then_inc(done, 1)
                if i == 5:
                    ps, done = take(pe, "kcet")
                    pe.transpose(ps[0:64, 0:64], W["kce"][0:64, :], ident[0:64, 0:64]).then_inc(done, 1)
                    ps, done = take(pe, "kb")
                    pe.matmul(ps[:, 0:1], W["kskb"][0:64, :], W["kceb"][0:64, :], start=True, stop=True).then_inc(done, 1)
                    for h in range(2):
                        ps, done = take(pe, ("ppt", h))
                        for n in range(3):
                            last = pe.transpose(ps[0:PP, n * R:(n + 1) * R], ppx[:, 3 * h + n, :], ident[0:R, 0:R])
                        last.then_inc(done, 1)
                if i == 6:
                    emptied(pe, "kcet")
                    emptied(pe, "kb")
                    ps, done = take(pe, "ksm")
                    pe.matmul(ps[:, 0:64], W["kcet"][0:64, :], W["kskb"][0:64, 0:64], start=True, stop=True)\
                        .then_inc(done, 1)
                    emptied(pe, ("ppt", 0))
                    emptied(pe, ("ppt", 1))
                    for h in range(2):
                        ps, done = take(pe, ("ppf", h))
                        pe.matmul(ps[:, 0:HALF], W["hop1b"][0:PP, :], ppt[:, h * HALF:(h + 1) * HALF],
                                  start=True, stop=True).then_inc(done, 1)
            pe.wait_ge(S["conv_x"], NB)
            for half in range(2):
                for s in range(NS):
                    ps, done = take(pe, ("h0", half, s))
                    pe.matmul(ps[0:R, :], xc[:, half * R:(half + 1) * R], Wout[:, 8 * s:8 * s + 8, :],
                              start=True, stop=True).then_inc(done, 1)

            def transposes(k, src, p, ready):
                pe.wait_ge(ready, p + 1)
                for h in range(2):
                    ps, done = take(pe, ("xt", k, p, h))
                    for n in range(3):
                        last = pe.transpose(ps[:, n * R:(n + 1) * R], src(p, 3 * h + n), ident[0:R, 0:R])
                    last.then_inc(done, 1)

            def xn_tile(p, j):
                return XN[:, p, j].rearrange("r a d -> r (a d)")

            for p in range(2):
                transposes(0, xn_tile, p, S["normed0"])

            for k in range(len(jobs) - 8, len(jobs)):
                pe.wait_ge(free[k % 8], k // 8 + 1)
            
            def ring(job):
                k = ring_at[job]
                if k >= 2:
                    pe.wait_ge(S["ring_free"], k - 1)
                ps = ring_bank[k % 2]
                kind = job[0]
                if kind == "proj":
                    _, b, g, qk, th = job
                    p, a = b % NP, b // NP
                    if ("xt", 1, b, 1) in ring_at:
                        pe.wait_ge(S["ring_free"], ring_at[("xt", 1, b, 1)] + 1)
                    last = pe.matmul(ps[:, 0:HALF], qkp[:, a, qk, g * 128:(g + 1) * 128],
                                     XT[:, p * L + th * HALF:p * L + (th + 1) * HALF], start=True, stop=True)
                elif kind == "score":
                    _, n, i = job
                    b, hp = divmod(n, 4)
                    h2, j, half = i // 12, i // 2 % 6, i % 2
                    if i == 0:
                        pe.wait_ge(S["qk_dma0"] if hp < 2 else S["qk_dma1"], 16 * 12 * (b + 1))
                    h = 2 * hp + h2
                    last = pe.matmul(ps[0:R, 0:HALF], QA[0:96, b % 2, h, j * R:(j + 1) * R],
                                     KA[0:96, b % 2, h, half * HALF:(half + 1) * HALF], start=True, stop=True)
                elif kind == "shift":
                    n = job[1]
                    pe.wait_ge(S["shift_in"], n + 1)
                    last = pe.transpose(ps[0:36, 0:63].bitcast(BF16)[:, 0:R],
                                        NM[:, n % 2, :], identb[0:R, 0:R])
                elif kind == "xt":
                    _, k_, b, h = job
                    p = b % NP
                    pe.wait_ge(S["lnb_done"], ln_at[(k_, b + NP if k_ == 1 else b)] + 1)
                    for i in range(3):
                        last = pe.transpose(ps[:, i * R:(i + 1) * R],
                                            XN[:, p, 3 * h + i].rearrange("r a d -> r (a d)"), ident[0:R, 0:R])
                elif kind == "logits":
                    b = job[1]
                    p, a = b % NP, b // NP
                    pe.wait_ge(S["ring_free"], ring_at[("xt", 2, b, 1)] + 1)
                    for j in range(NJ):
                        c = p * L + j * R
                        last = pe.matmul(ps[0:R, E0 * j:E0 * j + E0], XT[:, c:c + R],
                                         W["gw"][:, E0 * a:E0 * a + E0], start=True, stop=True)
                elif kind == "pos":
                    b = job[1]
                    pe.wait_ge(S["onehot"], b + 1)
                    pe.wait_ge(S["onehot_sum"], b + 1)
                    pe.matmul(ps[0:R, 0:NJ * E0], triu[0:R, 0:R], OH, start=True, stop=False)
                    last = pe.matmul(ps[0:R, 0:NJ * E0], ones[0:R, 0:R], SO[:, 0:NJ, :], start=False, stop=True)
                else:
                    _, b, j, h = job
                    for i in range(2):
                        hp = 2 * h + i
                        if j == 0 and i == 0:
                            pe.wait_ge(S["ctx_out"], 2 * (4 * b + 2 * h + 2))
                        last = pe.matmul(ps[0:R, i * 130:(i + 1) * 130], CT[:, b % 2, hp, j * R:(j + 1) * R],
                                         vox[:, hp, :], start=True, stop=True)
                last.then_inc(S["ring_full"], 1)

            def scores_t(n, c, h2, th):
                b, hp = divmod(n, 4)
                x = 12 * n + 2 * c + h2
                if th == 0:
                    if x >= 2:
                        pe.wait_ge(S["exp_done"], x - 1)
                    if c == 0 and h2 == 0:
                        pe.wait_ge(S["shift_dma"], 48 * (n + 1))
                        if n == 0:
                            pe.wait_ge(S["kb_ones"], 2)
                h = 2 * hp + h2
                cols = slice(th * HALF, (th + 1) * HALF)
                ps = st_bank[h2][th][0:R, 0:HALF]
                pe.matmul(ps, KA[0:96, b % 2, h, c * R:(c + 1) * R], QA[0:96, b % 2, h, cols],
                          start=True, stop=False)
                last = pe.matmul(ps, KB[0:99, b % 2, h, c * R:(c + 1) * R], QB[0:99, b % 2, h, cols],
                                 start=False, stop=True)
                if th == 1:
                    last.then_inc(S["st_done"], 1)

            def values(n, c, th):
                b = n // 4
                p, a = b % NP, b // NP
                if th == 0:
                    pe.wait_ge(S["exp_done"], 12 * n + 2 * c + 2)
                    if c == 0:
                        pe.wait_ge(S["v_ready"], p + 1)
                if c == 0 and n:
                    pe.wait_ge(S["ctx_out"], 2 * n - 1 + th)
                for h2 in range(2):
                    last = pe.matmul(ctx_bank[th][64 * h2:64 * h2 + 64, 0:HALF], XN[:, p, c, a, :],
                                     PR[:, (2 * c + h2) % 4, th * HALF:(th + 1) * HALF],
                                     start=(c == 0), stop=(c == 5), tile_position=(0, 64 * h2))
                if th == 1:
                    last.then_inc(S["pv_done"], 1)

            for job in before:
                ring(job)
            for n in range(NU):
                for c in range(6):
                    js = ring_jobs(n, c)
                    rest = [(scores_t, (n, c, h2, th)) for h2 in range(2) for th in range(2)]
                    u = 6 * n + c - 1
                    if u >= 0:
                        rest += [(values, (u // 6, u % 6, th)) for th in range(2)]
                    m = 0
                    for k, (emit, what) in enumerate(rest):
                        emit(*what)
                        if k in (1, 3, 4) and m < len(js):
                            ring(js[m])
                            m += 1
                    for job in js[m:]:
                        ring(job)
            values(NU - 1, 5, 0)
            values(NU - 1, 5, 1)
            for job in after:
                if job in ring_at:
                    ring(job)

            pe.wait_ge(S["xb_loaded"], 16 * 8)
            for e in range(4):
                for h in range(2):
                    ps, done = take(pe, ("xbt", e, h))
                    for n in range(4):
                        last = pe.transpose(ps[:, n * R:(n + 1) * R], XB[:, e, 4 * h + n, :], ident[0:R, 0:R])
                    last.then_inc(done, 1)
            pe.wait_ge(S["w_late"], 16 * 3)

            def expert_in(e):
                emptied(pe, ("xbt", e, 0))
                emptied(pe, ("xbt", e, 1))
                for a in range(2):
                    for fh in range(2):
                        for nn in range(2):
                            ps, done = take(pe, ("h1", e, a, fh, nn))
                            pe.matmul(ps[:, 0:CH], w1p[:, e + 4 * a, fh * 128:(fh + 1) * 128],
                                      XBT[:, e, nn * CH:(nn + 1) * CH], start=True, stop=True).then_inc(done, 1)

            def expert_out(e):
                for a in range(2):
                    for fh in range(2):
                        for nn in range(2):
                            emptied(pe, ("h1", e, a, fh, nn))
                for nn in range(2):
                    ps, done = take(pe, ("y", e, nn))
                    for fh in range(2):
                        for a in range(2):
                            last = pe.matmul(ps[64 * a:64 * a + 64, 0:CH], w2e[:, e + 4 * a, fh, :],
                                             HM[:, e % 2, a, fh, nn * CH:(nn + 1) * CH],
                                             start=(fh == 0), stop=(fh == 1), tile_position=(0, 64 * a))
                    last.then_inc(done, 1)

            def expert_back(e):
                emptied(pe, ("y", e, 0))
                emptied(pe, ("y", e, 1))
                pe.wait_ge(S["big"], 2)
                for h in range(2):
                    ps, done = take(pe, ("yb", e, h))
                    for n in range(4):
                        last = pe.transpose(ps[0:R, n * 128:(n + 1) * 128],
                                            YT[:, e, (4 * h + n) * R:(4 * h + n + 1) * R], ident)
                    last.then_inc(done, 1)

            expert_in(0)
            for e in range(4):
                if e < 3:
                    expert_in(e + 1)
                expert_out(e)
                if e:
                    expert_back(e - 1)
            expert_back(3)

            def hidden(p):
                for h in range(2):
                    emptied(pe, ("xt", 1, p, h))
                for th in range(2):
                    cols = slice(p * L + th * HALF, p * L + (th + 1) * HALF)
                    own = slice(p % 2 * L + th * HALF, p % 2 * L + (th + 1) * HALF)
                    for name, w in (("hop", W["hop1"]), ("sg", W["sg1"])):
                        ps, done = take(pe, (name, p, th))
                        pe.matmul(ps[0:w.shape[1], 0:HALF], w, XT[:, cols], start=True, stop=True).then_inc(done, 1)
                    if th == 0:
                        pe.wait_ge(S["cx"], p + 1)
                    ps, done = take(pe, ("ksk", p, th))
                    pe.matmul(ps[:, 0:HALF], W["ksk1"], XT[:, cols], start=True, stop=False)
                    pe.matmul(ps[:, 0:HALF], W["ksm"], CX[:, own], start=False, stop=True).then_inc(done, 1)

            def tokens(p, h):
                if h == 0:
                    for th in range(2):
                        emptied(pe, ("ksk", p, th))
                    pe.wait_ge(S["hop_act"], 2 * (p + 1))
                for i in range(NJ * p + 3 * h, NJ * p + 3 * h + 3):
                    cols = slice(i * R, (i + 1) * R)
                    own = slice((i - p // 2 * 2 * NJ) * R, (i - p // 2 * 2 * NJ + 1) * R)
                    ps, done = take(pe, ("tok", i))
                    pe.matmul(ps[0:R, 0:320], XT[:, cols], W["wta"], start=True, stop=True)
                    pe.matmul(ps[0:R, 320:384], KG[:, own], W["ksk2"], start=True, stop=True)
                    pe.matmul(ps[0:R, 384:386], SG[0:64, own], W["sg2"][0:64, :], start=True, stop=True)\
                        .then_inc(done, 1)
                    ps, done = take(pe, ("ao", i))
                    pe.matmul(ps[0:R, 0:264], HG[:, own], W["hop2"], start=True, stop=True).then_inc(done, 1)

            def gate_sums(p):
                pe.wait_ge(S["gate"], p + 1)
                for name, m in (("gcum", triu), ("gtot", ones)):
                    ps, done = take(pe, (name, p))
                    pe.matmul(ps[0:R, 0:2 * NJ], m[0:R, 0:R], GA[:, 0, 2 * NJ * p:2 * NJ * (p + 1)],
                              start=True, stop=True).then_inc(done, 1)

            def features(x):
                p, j = divmod(x, NJ)
                g = 2 * NJ * (p % 3) + 2 * j
                pe.wait_ge(S["qf_ready"], x // 2 + 1)
                pe.wait_ge(S["ff"], x // 2 + 1)
                pe.wait_ge(S["memory"], x // 2 + 1)
                for a in range(2):
                    ps, done = take(pe, ("qf", x, a))
                    pe.transpose(ps[:, 0:R], QQ[:, g + a, :], ident[0:R, 0:R])
                    pe.transpose(ps[:, R:2 * R], FF[:, g + a, :], ident[0:R, 0:R]).then_inc(done, 1)

            def masked(x):
                p, j = divmod(x, NJ)
                g = 2 * NJ * (p % 3) + 2 * j
                for k in range(2):
                    ps, done = take(pe, ("sm", x, k))
                    for a in range(2):
                        if k == 0:
                            emptied(pe, ("qf", x, a))
                        q = QF[64 * k:64 * k + 64, (2 * x + a) % 8, :]
                        last = pe.matmul(ps[0:R, a * R:(a + 1) * R], q[:, R:2 * R], q[:, 0:R], start=True, stop=True)
                    last.then_inc(done, 1)
                if j < NJ - 1:
                    ps, done = take(pe, ("state", x))
                    for a in range(2):
                        last = pe.matmul(ps[:, a * 128:(a + 1) * 128], FF[:, g + a, :],
                                         CV[:, g // 2, a].rearrange("r c d -> r (c d)"), start=True, stop=True)
                    last.then_inc(done, 1)

            def retrieved(x):
                p, j = divmod(x, NJ)
                g = 2 * NJ * (p % 3) + 2 * j
                emptied(pe, ("sm", x, 0))
                emptied(pe, ("sm", x, 1))
                if j:
                    pe.wait_ge(S["state"], 2 * (p * (NJ - 1) + j))
                ps, done = take(pe, ("ret", x))
                for a in range(2):
                    o = ps[0:R, a * D:(a + 1) * D]
                    pe.matmul(o, SM[:, x % 4, 0, a, :], CV[:, g // 2, a, 0, :], start=True, stop=False)
                    last = pe.matmul(o, SM[:, x % 4, 1, a, :], CV[:, g // 2, a, 1, :], start=False, stop=(j == 0))
                    if j:
                        last = pe.matmul(o, QF[:, (2 * x + a) % 8, 0:R], ST[:, p % 2, j, a, :],
                                         start=False, stop=True)
                last.then_inc(done, 1)

            def product(p):
                for h in range(2):
                    emptied(pe, ("xt", 2, p, h))
                for h in range(2):
                    ps, done = take(pe, ("product", p, h))
                    for n in range(3):
                        c = p * L + (3 * h + n) * R
                        last = pe.matmul(ps[0:R, n * 128:(n + 1) * 128], XT[:, c:c + R], W["outw"],
                                         start=True, stop=True)
                    last.then_inc(done, 1)

            for event in events:
                kind, x = event[0:2]
                if kind == "transpose":
                    transposes(x, xn_tile, event[2], S["lnx"] if x == 2 else S[f"normed{x}"])
                elif kind == "hidden":
                    hidden(x)
                elif kind == "tokens":
                    tokens(x, event[2])
                elif kind == "weights":
                    gate_sums(x)
                elif kind == "features":
                    features(x)
                elif kind == "masked":
                    masked(x)
                elif kind == "retrieved":
                    retrieved(x)
                elif kind == "product":
                    product(event[2])

            pe.wait_ge(S["w_late"], 16 * 9)
            for p in range(NP):
                emptied(pe, ("xt", 3, p, 0))
                emptied(pe, ("xt", 3, p, 1))
                for th in range(2):
                    cols = slice(p * L + th * HALF, p * L + (th + 1) * HALF)
                    ps, done = take(pe, ("rh", p, th))
                    pe.matmul(ps[0:64, 0:HALF], W["rw1"], XT[:, cols], start=True, stop=True).then_inc(done, 1)
            for p in range(NP):
                emptied(pe, ("rh", p, 0))
                emptied(pe, ("rh", p, 1))
            ps, done = take(pe, "logits1")
            for i in range(NT):
                last = pe.matmul(ps[0:R, 12 * i:12 * i + 12], RH[0:64, i * R:(i + 1) * R], W["rw2"][0:64, :],
                                 start=True, stop=True)
            last.then_inc(done, 1)
            units = units1

            def layer1(x):
                a, p, th, ep = units[x]
                ps, done = take(pe, ("l1", x))
                pe.matmul(ps[:, 0:HALF], e1w[:, a, ep, :], XT[:, p * L + th * HALF:p * L + (th + 1) * HALF],
                          start=True, stop=True).then_inc(done, 1)

            def layer2(x):
                a, p, th, ep = units[x]
                emptied(pe, ("l1", x))
                ps, done = take(pe, ("l2", x))
                pe.matmul(ps[:, 0:HALF], e2w[:, ep, :], H1[:, x % 4, :], start=True, stop=True).then_inc(done, 1)

            def layer3(a, p, th):
                x0 = 3 * ((a * NP + p) * 2 + th)
                for ep in range(3):
                    emptied(pe, ("l2", x0 + ep))
                for n in range(3):
                    j = 3 * th + n
                    ps, done = take(pe, ("l3", a, p, j))
                    for ep in range(3):
                        last = pe.matmul(ps[0:R, ep * 128:(ep + 1) * 128],
                                         H2[:, ep, p * L + j * R:p * L + (j + 1) * R], e3w[:, ep, :],
                                         start=True, stop=True)
                    last.then_inc(done, 1)

            NX = len(units)
            for x in range(NX + 1):
                if x < NX:
                    layer1(x)
                if x:
                    layer2(x - 1)
                    if x >= 6 and x % 3 == 0:
                        layer3(*units[x - 6][0:3])
            layer3(*units[NX - 3][0:3])

        @block.sync
        def _(sp):
            for s in range(NS):
                sp.dma_start(xc[32 * s:32 * s + 32, :],
                             t["x"].rearrange("b c (s l) -> s (b c) l", s=NS)[s]).then_inc(S["dma_conv"], 16)
            sp.dma_start(P4[:, 0:PAR].rearrange("c (i o k) -> c i o k", i=NB, o=CIN),
                         t["L0_tok_conv_w"].rearrange("i o c k -> c i o k")).then_inc(S["dma_conv"], 16)
            for n, name in enumerate(("conv_b", "bn_gamma", "bn_beta", "bn_mean", "bn_var")):
                sp.dma_start(P4[:, PAR + n * NB:PAR + (n + 1) * NB],
                             t["L0_tok_" + name].rearrange("i c -> c i")).then_inc(S["dma_conv"], 16)
            sp.dma_start(P4[:, OW:OW + D], t["L0_tok_out_w"].rearrange("v c o -> c (v o)")).then_inc(S["dma_conv"], 16)
            sp.dma_start(outb[:, :], t["L0_tok_out_b"].partition_broadcast(R)).then_inc(S["dma_conv"], 16)
            sp.wait_ge(S["zeroed"], 1)
            for e in range(E0):
                sp.dma_start(xbuf[e * ROWS:(e + 1) * ROWS].rearrange("(r c) d -> r (c d)", r=R), zeros)\
                    .then_inc(S["xbuf_zero"], 16)
            sp.wait_ge(S["zeroed"], 2)
            for dst, src in prep:
                sp.dma_start(dst, src).then_inc(S["dma_prep"], 16)
            for dst, src in wd:
                sp.dma_start(dst, src).then_inc(S["dma_weights"], 16)

            for job in order:
                if job[0] == "proj" and job[4] == 1:
                    _, b, g, qk, th = job
                    dma = S["qk_dma0"] if g == 0 else S["qk_dma1"]
                    sp.wait_ge(S["split3"], nproj[job] + 1)
                    if b >= 2:
                        sp.wait_ge(S["st_done"], 48 * (b - 1))
                    for arr, terms in (((QA, (0, 0, 1)), (QB, (0, 2, 1))), ((KA, (0, 1, 0)), (KB, (2, 0, 1))))[qk]:
                        for s, term in enumerate(terms):
                            sp.dma_start(arr[32 * s:32 * s + 32, b % 2, 4 * g:4 * g + 4, :],
                                         SP[:, qk, term, :]).then_inc(dma, 16)
                if job[0] == "shift":
                    n = job[1]
                    b, hp = divmod(n, 4)
                    sp.wait_ge(S["ring_free"], ring_at[job] + 1)
                    for term in range(3):
                        dst = QB[96 + term:97 + term, b % 2, 2 * hp:2 * hp + 2, :]
                        sp.dma_start(dst.rearrange("o h (j r) -> o (h j) r", r=R), MT[12 * term:12 * term + 12, n % 2, 0:R])\
                            .then_inc(S["shift_dma"], 16)

            sp.wait_ge(S["late_zero"], 1)
            sp.dma_start(w1p[0:64, 0:4, :], t["L0_ffn_w1"][0:4].rearrange("e d f -> d e f")).then_inc(S["w_late"], 16)
            sp.dma_start(w1p[64:128, 4:8, :], t["L0_ffn_w1"][4:8].rearrange("e d f -> d e f")).then_inc(S["w_late"], 16)
            sp.dma_start(w2e.rearrange("f e h d -> f (e h) d"),
                         t["L0_ffn_w2"].rearrange("e (h f) d -> f (e h) d", h=2)).then_inc(S["w_late"], 16)
            sp.wait_ge(S["scattered"], 16 * NG)
            for e in range(4):
                for a in range(2):
                    r0 = (e + 4 * a) * ROWS
                    sp.dma_start(XB[:, e, :, a * D:(a + 1) * D],
                                 xbuf[r0:r0 + ROWS].rearrange("(c r) d -> r c d", r=R)).then_inc(S["xb_loaded"], 16)
            for e in range(4):
                emptied(sp, ("yb", e, 0))
                emptied(sp, ("yb", e, 1))
                for a in range(2):
                    r0 = (e + 4 * a) * ROWS
                    sp.dma_start(ybuf[r0:r0 + ROWS].rearrange("(c r) d -> r c d", r=R),
                                 XB[:, e, :, a * D:(a + 1) * D]).then_inc(S["y_stored"], 16)
            sp.wait_ge(S["late_zero"], 2)
            for a in range(2):
                r = slice(64 * a, 64 * a + 64)
                w1, w2, w3 = (t["L1_ffn_expert_w" + str(n)].rearrange("(ep e) d h -> e d ep h", e=2)
                              for n in (1, 2, 3))
                sp.dma_start(e1w[r, a].rearrange("d ep (e h) -> d (ep e) h", e=2),
                             t["L1_ffn_expert_w1"].rearrange("e d h -> d e h")).then_inc(S["w_late"], 16)
                sp.dma_start(e2w[r, :, 64 * a:64 * a + 64], w2[a]).then_inc(S["w_late"], 16)
                sp.dma_start(e3w[r, :, 64 * a:64 * a + 64], w3[a]).then_inc(S["w_late"], 16)
            for a in range(2):
                for p in range(NP):
                    sp.wait_ge(S["h4"], NJ * (a * NP + p + 1))
                    sp.dma_start(out[p + 4 * a].rearrange("(j r) d -> r j d", r=R), H[:, p, :, a, :])\
                        .then_inc(S["stored"], 16)
            sp.wait_ge(S["stored"], 16 * B)

        @block.gpsimd
        def _(pool):
            n_ = [0]

            def link(ins):
                n_[0] += 1
                ins.then_inc(S["pool_chain"], 1)
                pool.wait_ge(S["pool_chain"], n_[0])

            pool.memset(R4, 0.0)
            pool.memset(bmask, 1.0)
            link(pool.memset(m24, 1.0))
            v = R4.rearrange("c (g k) -> c g k", k=CIN)
            pool.affine_select(out=v, in_=v, compare_op=ALU.not_equal, fill=1.0, base=0,
                               pattern=[[0, NS * B], [-1, CIN]], channel_multiplier=1).then_inc(S["consts"], 1)
            masks = [bmask[32 * s:32 * s + 32, :] for s in range(NS)] + [m24]
            for v in masks:
                link(pool.affine_select(out=v, in_=v, compare_op=ALU.is_ge, fill=0.0, base=0,
                                        pattern=[[-CIN, v.shape[1]]], channel_multiplier=1))
                link(pool.affine_select(out=v, in_=v, compare_op=ALU.is_ge, fill=0.0, base=CIN - 1,
                                        pattern=[[CIN, v.shape[1]]], channel_multiplier=-1))
            pool.memset(Fw, 0.0)
            pool.memset(ident[:, :], 0.0)
            pool.memset(triu[:, :], 1.0)
            pool.memset(ones[:, :], 1.0)
            pool.memset(mhalf[:, :], -0.5)
            link(pool.memset(halfpi[:, :], PI / 2))
            pool.affine_select(out=ident[:, :], in_=ident[:, :], compare_op=ALU.not_equal, fill=1.0, base=0,
                               pattern=[[-1, 128]], channel_multiplier=1).then_inc(S["consts"], 1)
            pool.affine_select(out=triu[:, :], in_=triu[:, :], compare_op=ALU.is_ge, fill=0.0, base=0,
                               pattern=[[1, 128]], channel_multiplier=-1)
            pool.memset(zero1[:, :], 0.0)
            pool.memset(wearly, 0.0)
            pool.memset(zeros, 0.0).then_inc(S["zeroed"], 1)
            pool.memset(qload, 0.0)
            pool.memset(wall[:, :], 0.0)
            pool.memset(vox[:, :, :], 0.0).then_inc(S["zeroed"], 1)
            pool.wait_ge(S["consts"], 2)
            pool.tensor_copy(identb[:, :], ident[:, :]).then_inc(S["consts"], 1)
            pool.iota(out=iota8[:, :], pattern=[[1, E0]], base=-E0, channel_multiplier=0,
                      allow_small_or_imprecise_dtypes=True).then_inc(S["consts"], 1)
            pool.wait_ge(S["bn_var"], 1)
            pool.tensor_tensor(bn[:, 1, :], bn[:, 0, :], mhalf[0:96, 0:NB], ALU.pow).then_inc(S["bn_rstd"], 1)
            pool.wait_ge(S["vo_ready"], 1)
            for h2 in range(2):
                v = vox[:, :, 65 * h2 + 64:65 * h2 + 65]
                ins = pool.affine_select(out=v, in_=v, compare_op=ALU.not_equal, fill=1.0, base=-(63 + 64 * h2),
                                         pattern=[[0, 4], [0, 1]], channel_multiplier=1)
            ins.then_inc(S["vo_ready"], 1)

            def scale(k, p):
                pool.wait_ge(S[f"variance{k}"], p + 1)
                link(pool.tensor_tensor(lnst[:, 3, p, :], lnst[:, 2, p, :], mhalf[0:R, 0:2 * NJ], ALU.pow))
                pool.tensor_tensor(pairs(XN, p), pairs(XN, p), over(lnst[:, 3, p, :], 2 * NJ, D), ALU.mult)\
                    .then_inc(S[f"normed{k}"], 1)

            pool.wait_ge(S["vo_ready"], 2)
            for a in range(2):
                pool.memset(KB[96:99, a], 1.0).then_inc(S["kb_ones"], 1)
                pool.wait_ge(S["kb_ones"], a + 1)
            scale(0, 0)
            scale(0, 1)


            def values_ready(p):
                pool.memset(XN[:, p, :, :, D - 1:D], 1.0).then_inc(S["v_ready"], 1)

            link(pool.memset(SO[:, NJ, :], 0.0))
            for p in range(2):
                for h in range(2):
                    pool.wait_ge(full[jobs[("xt", 0, p, h)] % 8], jobs[("xt", 0, p, h)] // 8 + 1)
                values_ready(p)
            for job in order:
                kind = job[0]
                if kind == "proj":
                    _, b, g, qk, th = job
                    q = nproj[job]
                    cols = slice(th * HALF, (th + 1) * HALF)
                    pool.wait_ge(S["ring_free"], ring_at[job] + 1)
                    link(pool.tensor_copy(SP[:, qk, 1, cols], RR[:, q % 2, :]))
                    pool.tensor_tensor(SP[:, qk, 2, cols], RR[:, q % 2, :], SP[:, qk, 1, cols], ALU.subtract)\
                        .then_inc(S["split3"], 1)
                elif kind == "score" and job[2] == 23:
                    n = job[1]
                    pool.wait_ge(S["mx_neg"], n + 1)
                    if n >= 2:
                        pool.wait_ge(S["ring_full"], ring_at[("shift", n - 2)] + 1)
                    m, nm = M1[:, n % 2, :], NM[:, n % 2, :]
                    link(pool.tensor_scalar(nm[:, 0:12], m, -1.0, None, ALU.mult))
                    link(pool.tensor_tensor(MR[:, 0, :], m, nm[:, 0:12], ALU.add))
                    link(pool.tensor_scalar(nm[:, 12:24], MR[:, 0, :], -1.0, None, ALU.mult))
                    link(pool.tensor_tensor(MR[:, 1, :], MR[:, 0, :], nm[:, 12:24], ALU.add))
                    pool.tensor_scalar(nm[:, 24:36], MR[:, 1, :], -1.0, None, ALU.mult).then_inc(S["shift_in"], 1)
                elif kind == "xt" and job[1] == 1 and job[3] == 1:
                    pool.wait_ge(S["ring_full"], ring_at[job] + 1)
                    values_ready(job[2])
                elif kind == "ln_mean":
                    k, b = ln_at[job[1:3]], job[2]
                    p, a = b % NP, b // NP
                    pool.wait_ge(S["lnb_sum"], k + 1)
                    x = XN[:, p, :, a, :]
                    link(pool.tensor_scalar(lnb[:, 1, :], lnb[:, 0, :], -1.0 / D, None, ALU.mult))
                    link(pool.tensor_tensor(x, H[:, p, :, a, :], over(lnb[:, 1, :], NJ, D), ALU.add))
                    pool.tensor_tensor(XSQ, x, x, ALU.mult).then_inc(S["lnb_x"], 1)
                elif kind == "ln_std":
                    k, b = ln_at[job[1:3]], job[2]
                    p, a = b % NP, b // NP
                    pool.wait_ge(S["lnb_ssq"], k + 1)
                    x = XN[:, p, :, a, :]
                    link(pool.tensor_scalar(lnb[:, 3, :], lnb[:, 2, :], 1.0 / D, EPS, ALU.mult, ALU.add))
                    link(pool.tensor_tensor(lnb[:, 3, :], lnb[:, 3, :], mhalf[0:R, 0:NJ], ALU.pow))
                    pool.tensor_tensor(x, x, over(lnb[:, 3, :], NJ, D), ALU.mult).then_inc(S["lnb_done"], 1)
                elif kind == "choose":
                    b = job[1]
                    pool.wait_ge(S["onehot"], b + 1)
                    link(pool.tensor_copy(SO[:, 0, :], SO[:, NJ, :]))
                    for j in range(NJ):
                        ins = pool.tensor_tensor(SO[:, j + 1, :], SO[:, j, :], OH[:, j, :], ALU.add)
                        if j < NJ - 1:
                            link(ins)
                    ins.then_inc(S["onehot_sum"], 1)
                elif kind == "slots":
                    b = job[1]
                    tiles = slice(NJ * b, NJ * b + NJ)
                    pool.wait_ge(S["pos_ready"], b + 1)
                    link(pool.tensor_scalar(kept, pos, float(CAP), None, ALU.is_le))
                    link(pool.tensor_tensor(pk[:, tiles], prob[:, tiles], kept, ALU.mult))
                    link(pool.tensor_scalar(sl, im, float(ROWS), float(E0 * ROWS), ALU.mult, ALU.add))
                    link(pool.tensor_scalar(tx, kept, -65536.0, 65535.0, ALU.mult, ALU.add))
                    link(pool.tensor_tensor(sx, sl, pos, ALU.add))
                    link(pool.tensor_tensor(sx, sx, tx, ALU.add))
                    link(pool.tensor_copy(slot_in[:, tiles], sx))
                    link(pool.tensor_scalar(sy, pos, float(CAP), -1.0, ALU.min, ALU.add))
                    link(pool.tensor_tensor(sy, sy, sl, ALU.add))
                    link(pool.tensor_copy(slot_out[:, tiles], sy))
                    if b == 0:
                        pool.wait_ge(S["xbuf_zero"], 16 * E0)
                elif kind == "scatter":
                    _, b, j = job
                    p, a = b % NP, b // NP
                    g = b * NJ + j
                    pool.indirect_dma_start(out=xbuf, out_offset=bass.IndirectOffsetOnAxis(ap=slot_in[:, g:g + 1],
                                                                                           axis=0),
                                            in_=XN[:, p, j, a, :], in_offset=None, bounds_check=E0 * ROWS - 1,
                                            oob_is_err=False).then_inc(S["scattered"], 16)
                if job == after[NJ]:
                    pool.wait_ge(S["st_done"], 12 * NU)
                    pool.memset(w1p, 0.0).then_inc(S["late_zero"], 1)
                    pool.wait_ge(S["late_zero"], 1)

            pool.memset(big[:, 0:1], 1.0e4)
            pool.memset(big[:, 1:2], -1.0e4).then_inc(S["big"], 1)
            pool.memset(YT[:, :, CAP:ROWS], 0.0).then_inc(S["big"], 1)
            pool.wait_ge(S["y_stored"], 16 * 8)

            def gather(p, js=range(NJ)):
                for j in js:
                    for a in range(2):
                        g = a * NT + p * NJ + j
                        pool.indirect_dma_start(
                            out=XN[:, p, j, a, :], out_offset=None, in_=ybuf,
                            in_offset=bass.IndirectOffsetOnAxis(ap=slot_out[:, g:g + 1], axis=0),
                            bounds_check=E0 * ROWS - 1, oob_is_err=False).then_inc(gathered[p], 16)

            def residual(p):
                pool.wait_ge(S["normed1"], p + 1)
                link(pool.tensor_tensor(pairs(H, p), pairs(H, p), pairs(XN, p), ALU.add))
                pool.tensor_tensor(pairs(H, p), pairs(H, p), rows(bias[0:R, OB:OB + D], 2 * NJ), ALU.add)\
                    .then_inc(S["h_pre"], 1)

            gather(0)
            pool.iota(out=pos1, pattern=[[1, L]], base=1, channel_multiplier=0,
                      allow_small_or_imprecise_dtypes=True).then_inc(S["pos"], 1)
            gather(1, range(3))
            scale(1, 0)
            gather(1, range(3, NJ))
            gather(2)
            gather(3, range(3))
            scale(1, 1)
            gather(3, range(3, NJ))

            def chunk(q):
                p, c = divmod(q, 3)
                g = slice(2 * NJ * (p % 3) + 4 * c, 2 * NJ * (p % 3) + 4 * c + 4)
                tiles = slice(NJ * (p % 3) + 2 * c, NJ * (p % 3) + 2 * c + 2)
                pool.wait_ge(S["cosines"], 2 * (p + 1))
                pool.wait_ge(S["wab"], p + 1)
                if q:
                    pool.wait_ge(S["uv"], q)
                cc, sc = (x[:, g].rearrange("r g h p -> r (g h) p") for x in (TC, SC))
                wa, wb = (over(WA[:, i, 16 * q:16 * q + 16], 16, PP) for i in range(2))
                p2, p3 = (PT[:, i].rearrange("r g h p -> r (g h) p") for i in (2, 3))
                pool.tensor_tensor(p2, sc, wa, ALU.mult)
                link(pool.tensor_tensor(p3, cc, wb, ALU.mult))
                pool.tensor_tensor(p2, p2, p3, ALU.add).then_inc(S["vsum"], 1)
                pool.wait_ge(S["prod"], q + 1)
                pool.wait_ge(S["vsum"], q + 1)
                for i, x in ((0, TK), (1, SK)):
                    fq = QQ[:, g, 64 + 32 * i:96 + 32 * i].rearrange("r (j a) p -> r j a p", a=2)
                    pool.tensor_tensor(fq, x[:, tiles, 0],
                                       over(GA[:, 5, 4 * q:4 * q + 4], 4, PP).rearrange("r (j a) p -> r j a p", a=2),
                                       ALU.mult)
                v = CV[:, tiles, :, 1, :].rearrange("r j a d -> r (j a) d")
                pool.tensor_tensor(v, v, over(GA[:, 0, 4 * q:4 * q + 4], 4, D), ALU.mult).then_inc(S["ff"], 1)

            for event in events:
                kind, x = event[0:2]
                if kind == "mean":
                    residual(x)
                elif kind == "weights":
                    g = slice(2 * NJ * x, 2 * NJ * (x + 1))
                    pool.wait_ge(S["gc"], x + 1)
                    link(pool.tensor_tensor(GA[:, 5, g], GA[:, 4, g], mhalf[0:R, 0:2 * NJ], ALU.pow))
                    link(pool.tensor_scalar(GA[:, 5, g], GA[:, 5, g], RS, None, ALU.mult))
                elif kind == "chunk":
                    chunk(x)
                elif kind == "variance" and not (x == 1 and event[2] < 2):
                    scale(x, event[2])
                elif kind == "normalize" and x == 2:
                    p = event[2]
                    pool.wait_ge(S["normed2"], p + 1)
                    link(pool.tensor_tensor(pairs(XN, p), pairs(XN, p), rows(bias[0:R, LNG:LNG + D], 12), ALU.mult))
                    pool.tensor_tensor(pairs(XN, p), pairs(XN, p), rows(bias[0:R, LNB:LNB + D], 12), ALU.add)\
                        .then_inc(S["lnx"], 1)
                elif kind == "room":
                    k = jobs[("ao", NT - 1)]
                    pool.wait_ge(full[k % 8], k // 8 + 1)
                    pool.memset(e1w, 0.0)
                    pool.memset(e2w, 0.0)
                    pool.memset(e3w, 0.0).then_inc(S["late_zero"], 1)

        @block.scalar
        def _(act):
            for i in range(NB):
                ps, done = filled(act, ("conv", i))
                if i == 0:
                    act.wait_ge(S["w96"], 1)
                act.activation(xr, ps[0:96, 0:SEG], ACT.Relu, bias=W96[:, PAR + i:PAR + i + 1]).then_inc(done, 1)
                if i == 4:
                    for qk in range(2):
                        for a in range(2):
                            ps, done = filled(act, ("qkp", qk, a))
                            act.wait_ge(S["zeroed"], 2)
                            act.activation(qkp[:, a, qk, :].rearrange("p (g r h) -> p g h r", g=2, h=4),
                                           ps[:, 0:256].rearrange("p (g h r) -> p g h r", g=2, h=4), ACT.Copy)\
                               .then_inc(done, 1)
                if i == 5:
                    ps, done = filled(act, "kcet")
                    act.activation(W["kcet"][0:64, 0:64], ps[0:64, 0:64], ACT.Copy)
                    act.activation(W["kcet"][0:64, 64:128], ps[0:64, 0:64], ACT.Copy).then_inc(done, 1)
                    ps2, done2 = filled(act, "kb")
                    act.activation(W["kb"], ps2[:, 0:1], ACT.Identity, bias=W["kb1"]).then_inc(done2, 1)
                    for h in range(2):
                        ps, done = filled(act, ("ppt", h))
                        act.activation(ppt[:, h * HALF:(h + 1) * HALF], ps[0:PP, 0:HALF], ACT.Copy)\
                           .then_inc(done, 1)
                if i == 6:
                    ps, done = filled(act, "ksm")
                    for a in range(2):
                        r = slice(64 * a, 64 * a + 64)
                        last = act.activation(W["ksm"][r, 64 * a:64 * a + 64], ps[r, 0:64], ACT.Copy)
                    last.then_inc(done, 1)
                    for h in range(2):
                        ps, done = filled(act, ("ppf", h))
                        act.activation(PPF[:, h * HALF:(h + 1) * HALF], ps[:, 0:HALF], ACT.Identity, bias=W["hopb"])\
                           .then_inc(done, 1)
            act.wait_ge(S["trig_r"], 1)
            act.activation(trig[:, 1, :], phases, ACT.Sin).then_inc(S["trig_done"], 1)
            act.activation(trig[:, 0, :], trig[:, 0, :], ACT.Sin, bias=halfpi[0:R, :], scale=-1.0)\
               .then_inc(S["trig_done"], 1)

            def squares(k, p, src):
                act.wait_ge(S[f"centred{k}"], p + 1)
                i = p % 2 if k == 0 else k - 1
                if k and p:
                    act.wait_ge(S[f"variance{k}"], p)
                act.activation(SQ[:, i, :], src, ACT.Square).then_inc(S[f"squared{k}"], 1)

            def xn_flat(p):
                return XN[:, p].rearrange("r j a d -> r (j a d)")

            def to_xt(k, p):
                for h in range(2):
                    ps, done = filled(act, ("xt", k, p, h))
                    act.activation(XT[:, p * L + h * HALF:p * L + (h + 1) * HALF], ps[:, 0:HALF], ACT.Copy)\
                       .then_inc(done, 1)

            squares(0, 0, xn_flat(0))
            squares(0, 1, xn_flat(1))
            to_xt(0, 0)
            to_xt(0, 1)

            def split1(job):
                _, b, g, qk, th = job
                k = ring_at[job]
                act.wait_ge(S["ring_full"], k + 1)
                group = 2 * b + g
                if group and qk == 0 and th == 0:
                    prev = group - 1
                    act.wait_ge((S["qk_dma0"], S["qk_dma1"])[prev % 2], 16 * 12 * (prev // 2 + 1))
                act.activation(SP[:, qk, 0, th * HALF:(th + 1) * HALF], ring_bank[k % 2][:, 0:HALF], ACT.Copy,
                               scale=(0.125 if qk == 0 else 1.0)).then_inc(S["split1"], 1)

            def exp_(n, c, h2):
                x = 12 * n + 2 * c + h2
                act.wait_ge(S["st_done"], x + 1)
                if x >= 4:
                    act.wait_ge(S["pv_done"], x // 2 - 1)
                act.activation(PR[:, x % 4, :].rearrange("r (h c) -> r h c", h=2),
                               psum[0:R, 2 + 2 * h2:4 + 2 * h2, 0:HALF], ACT.Exp).then_inc(S["exp_done"], 1)

            def ctx_out(n):
                b, hp = divmod(n, 4)
                act.wait_ge(S["pv_done"], 6 * (n + 1))
                if b >= 2:
                    act.wait_ge(S["ring_full"], ring_at[("out", b - 2, NJ - 1, 1)] + 1)
                for th in range(2):
                    act.activation(CT[:, b % 2, hp, th * HALF:(th + 1) * HALF], ctx_bank[th][:, 0:HALF], ACT.Copy)\
                       .then_inc(S["ctx_out"], 1)

            def weigh(b):
                act.wait_ge(S["route_ld"], b + 1)
                act.activation(LD, LD, ACT.Exp).then_inc(S["route_ex"], 1)

            for job in before:
                if job[0] == "proj":
                    split1(job)
            for n in range(NU):
                for c in range(6):
                    exp_(n, c, 0)
                    exp_(n, c, 1)
                    if c == 0 and n:
                        ctx_out(n - 1)
                    for job in ring_jobs(n, c) + side_jobs(n, c):
                        if job[0] == "proj":
                            split1(job)
                        elif job[0] == "weigh":
                            weigh(job[1])
            ctx_out(NU - 1)
            weigh(B - 1)

            def copy_out(name, dst):
                ps, done = filled(act, name)
                act.activation(dst, ps[0:dst.shape[0], 0:dst.shape[1]], ACT.Copy).then_inc(done, 1)

            for e in range(4):
                copy_out(("xbt", e, 0), XBT[:, e, 0:4 * R])
            for kind, e in ffn_order:
                if kind == "h1":
                    for a in range(2):
                        for nn in range(2):
                            name = ("h1", e, a, 0, nn)
                            ps, done = filled(act, name)
                            act.activation(HM[:, e % 2, a, 0, nn * CH:(nn + 1) * CH], ps[:, 0:CH], ACT.Relu,
                                           bias=W["b1"][:, 2 * (e + 4 * a):2 * (e + 4 * a) + 1]).then_inc(done, 1)
                elif kind == "y":
                    for nn in range(2):
                        ps, done = filled(act, ("y", e, nn))
                        act.activation(YT[:, e, nn * CH:(nn + 1) * CH], ps[:, 0:CH], ACT.Identity,
                                       bias=W["b2"][:, e:e + 1]).then_inc(done, 1)
                else:
                    copy_out(("yb", e, 0), XB[:, e, 0:4, :].rearrange("r c d -> r (c d)"))

            def hidden(p):
                for th in range(2):
                    own = slice(p % 2 * L + th * HALF, p % 2 * L + (th + 1) * HALF)
                    emptied(act, ("hop", p, th))
                    act.activation(HG[:, own], HG[:, own], ACT.Gelu).then_inc(S["hop_act"], 1)
                    for name, dst, b_, w in (("sg", SG, W["sgb1"], 64), ("ksk", KG, W["kb"], 128)):
                        ps, done = filled(act, (name, p, th))
                        act.activation(dst[0:w, own], ps[0:w, 0:HALF], ACT.Gelu, bias=b_[0:w, :]).then_inc(done, 1)

            def squash(p):
                for i in range(NJ * p, NJ * p + NJ):
                    emptied(act, ("ao", i))
                for x in phases_of(p, TC, TK):
                    act.activation(x, x, ACT.Tanh).then_inc(S["tanh"], 1)
                ws = WS[:, 48 * p:48 * p + 48]
                act.activation(ws, ws, ACT.Sigmoid).then_inc(S["width"], 1)
                g = slice(2 * NJ * p, 2 * NJ * (p + 1))
                act.activation(GA[:, 0, g], GA[:, 1, g], ACT.Sigmoid).then_inc(S["gate"], 1)

            def window(p):
                act.wait_ge(S["warg"], p + 1)
                act.activation(WE, WE, ACT.Exp).then_inc(S["wexp"], 1)

            def sines(p):
                act.wait_ge(S["tanh"], 2 * (p + 1))
                for x, y in zip(phases_of(p, TC, TK), phases_of(p, SC, SK)):
                    act.activation(y, x, ACT.Sin, scale=PI_IN).then_inc(S["sines"], 1)

            def cosines(p):
                act.wait_ge(S["sines"], 2 * (p + 1))
                for x in phases_of(p, TC, TK):
                    act.activation(x, x, ACT.Abs).then_inc(S["absd"], 1)
                for i, x in enumerate(phases_of(p, TC, TK)):
                    act.wait_ge(S["absd"], 2 * p + i + 1)
                    act.activation(x, x, ACT.Sin, bias=halfpi[0:R, :], scale=-PI).then_inc(S["cosines"], 1)

            def memory_features(q):
                p, c = divmod(q, 3)
                g = slice(2 * NJ * (p % 3) + 4 * c, 2 * NJ * (p % 3) + 4 * c + 4)
                tiles = slice(NJ * (p % 3) + 2 * c, NJ * (p % 3) + 2 * c + 2)
                act.wait_ge(S["prod"], q + 1)
                act.wait_ge(S["vsum"], q + 1)
                for i, x in ((0, TK), (1, SK)):
                    act.activation(FF[:, g, 64 + 32 * i:96 + 32 * i].rearrange("r (j a) p -> r j a p", a=2),
                                   x[:, tiles, 1], ACT.Copy)
                    last = act.activation(FF[:, g, 32 * i:32 * i + 32].rearrange("r (j a) p -> r j a p", a=2),
                                          trig[:, i, 2 * c * PP:(2 * c + 2) * PP]
                                          .rearrange("r (j p) -> r j p", p=PP)
                                          .unsqueeze(2).to_broadcast([R, 2, 2, PP]), ACT.Copy)
                last.then_inc(S["memory"], 1)

            def feature_tiles(x):
                for a in range(2):
                    ps, done = filled(act, ("qf", x, a))
                    if x >= 4:
                        k = jobs[("ret", x - 4)]
                        act.wait_ge(full[k % 8], k // 8 + 1)
                    act.activation(QF[:, (2 * x + a) % 8, :], ps[:, 0:2 * R], ACT.Copy).then_inc(done, 1)

            def retrieved_out(x):
                p, j = divmod(x, NJ)
                ps, done = filled(act, ("ret", x))
                act.wait_ge(S["h_pre"], p + 1)
                act.activation(XN[:, p, j].rearrange("r a d -> r (a d)"), ps[0:R, 0:128], ACT.Copy)\
                   .then_inc(done, 1)

            for event in events:
                kind, x = event[0:2]
                if kind == "centre":
                    squares(x, event[2], xn_flat(event[2]))
                elif kind == "transpose":
                    to_xt(x, event[2])
                elif kind == "hidden":
                    hidden(x)
                elif kind == "tokens" and event[2] == 1:
                    squash(x)
                elif kind == "widths":
                    window(x)
                elif kind == "sines":
                    sines(x)
                elif kind == "cosines":
                    cosines(x)
                elif kind == "chunk":
                    memory_features(x)
                elif kind == "features":
                    feature_tiles(x)
                elif kind == "retrieved":
                    retrieved_out(x)

            for p in range(NP):
                for th in range(2):
                    name = ("rh", p, th)
                    ps, done = filled(act, name)
                    act.activation(RH[0:64, p * L + th * HALF:p * L + (th + 1) * HALF], ps[0:64, 0:HALF], ACT.Relu,
                                   bias=W["rb1"][0:64, :]).then_inc(done, 1)
            act.wait_ge(S["route1"], 1)
            act.activation(GE, GE, ACT.Exp).then_inc(S["route1_ex"], 1)
            act.wait_ge(S["route1"], 2)
            act.activation(g1[:, 3, :], g1[:, 2, :], ACT.Exp).then_inc(S["route1_ex"], 1)
            act.wait_ge(S["route1"], 3)
            act.activation(g1[:, 5, :], g1[:, 4, :], ACT.Exp).then_inc(S["route1_ex"], 1)

            def hidden_out(layer, x):
                a, p, th, ep = units1[x]
                name = (f"l{layer}", x)
                dst = H1[:, x % 4, :] if layer == 1 else H2[:, ep, p * L + th * HALF:p * L + (th + 1) * HALF]
                b_ = (W["e1b"] if layer == 1 else W["e2b"])[:, ep:ep + 1]
                ps, done = filled(act, name)
                act.activation(dst, ps[:, 0:HALF], ACT.Relu, bias=b_).then_inc(done, 1)

            for x in range(len(units1) + 1):
                if x < len(units1):
                    hidden_out(1, x)
                if x:
                    hidden_out(2, x - 1)

        @block.vector
        def _(dve):
            n_ = [0]

            def link(ins):
                n_[0] += 1
                ins.then_inc(S["dve_chain"], 1)
                dve.wait_ge(S["dve_chain"], n_[0])

            ps, done96 = filled(dve, "w96")
            link(dve.tensor_copy(W96[:, 0:OW + D], ps[0:96, 0:OW + D]))
            dve.tensor_scalar(bn[:, 0, :], W96[:, PAR + 4 * NB:PAR + 5 * NB], EPS, None, ALU.add)\
               .then_inc(S["bn_var"], 1)
            dve.wait_ge(S["consts"], 2)
            wk = W96[:, 0:PAR].rearrange("p (i o k) -> p i o k", i=NB, o=CIN)
            fk = Fw.rearrange("p (i k) c -> p i k c", k=KT)
            for s in range(NS):
                r = slice(32 * s, 32 * s + 32)
                for tap in range(KT):
                    last = dve.tensor_tensor(
                        fk[r, :, tap, 64 + 32 * s:96 + 32 * s].rearrange("p i (b o) -> p i b o", b=B),
                        wk[r, :, :, tap].unsqueeze(2).to_broadcast([32, NB, B, CIN]),
                        bmask[r].unsqueeze(1).unsqueeze(3).to_broadcast([32, NB, B, CIN]), ALU.mult)
            last.then_inc(S["conv_w"], 1)
            dve.wait_ge(S["bn_rstd"], 1)
            link(dve.tensor_tensor(bn[:, 1, :], bn[:, 1, :], W96[:, PAR + NB:PAR + 2 * NB], ALU.mult))
            link(dve.tensor_tensor(bn[:, 0, :], bn[:, 1, :], W96[:, PAR + 3 * NB:PAR + 4 * NB], ALU.mult))
            link(dve.tensor_tensor(bn[:, 2, :], W96[:, PAR + 2 * NB:PAR + 3 * NB], bn[:, 0, :], ALU.subtract))
            dve.sem_inc(S["w96"], 1)
            dve.sem_inc(done96, 1)
            for i in range(NB):
                link(dve.tensor_scalar(xs, xc, bn[:, 2, i:i + 1], None, ALU.add))
                if i == 1:
                    dve.tensor_tensor(Wout, rows(W96[:, OW:OW + D], NS * B), over(m24, NS * B, D), ALU.mult)
                if i == 5:
                    dve.wait_ge(S["dma_prep"], 16 * len(prep))
                    for h2 in range(2):
                        r = slice(64 * h2, 64 * h2 + 64)
                        last = dve.tensor_tensor(vox[r, :, 65 * h2:65 * h2 + D], voload[r, 0], voload[r, 1],
                                                 ALU.subtract)
                    last.then_inc(S["vo_ready"], 1)
                emptied(dve, ("conv", i))
                ins = dve.scalar_tensor_tensor(xc, xr, bn[:, 1, i:i + 1], xs, ALU.mult, ALU.add)
                ins.then_inc(S["conv_x"], 1)
                dve.wait_ge(S["conv_x"], i + 1)
                if i == 6:
                    x0, x1 = phases, trig[:, 0, :]
                    dve.tensor_scalar(x0[:, NJ * PP:], bias[0:R, WD:WD + WN], 0.1, None, ALU.mult)
                    link(dve.tensor_copy(x0[:, 0:NJ * PP], ppx.rearrange("r j p -> r (j p)")))
                    link(dve.tensor_scalar(x1, x0, 1.0 / (2 * np.pi), MAGIC, ALU.mult, ALU.add))
                    link(dve.tensor_scalar(x1, x1, MAGIC, None, ALU.subtract))
                    for c in (C1, C2, C3):
                        link(dve.scalar_tensor_tensor(x0, x1, -c, x0, ALU.mult, ALU.add))
                    link(dve.tensor_scalar(x0, x0, PI_IN, -PI_IN, ALU.min, ALU.max))
                    dve.scalar_tensor_tensor(x1, x0, -1.0, x0, ALU.mult, ALU.max).then_inc(S["trig_r"], 1)
            for half in range(2):
                for s in range(NS):
                    ps, done = filled(dve, ("h0", half, s))
                    for a in range(2):
                        last = dve.tensor_tensor(H[:, :, 2 * s + half, a, :],
                                                 ps[0:R, 256 * a:256 * a + 256].rearrange("r (p d) -> r p d", p=NP),
                                                 rows(outb[:, :], NP), ALU.add)
                    last.then_inc(done, 1)
            k = jobs[("h0", 1, NS - 1)]
            dve.wait_ge(free[k % 8], k // 8 + 1)

            def centre(k, p, src, dst):
                link(dve.reduce_sum(lnst[:, 0, p, :], src, AX))
                link(dve.tensor_scalar(lnst[:, 1, p, :], lnst[:, 0, p, :], -1.0 / D, None, ALU.mult))
                dve.tensor_tensor(dst, src, over(lnst[:, 1, p, :], 2 * NJ, D), ALU.add)\
                   .then_inc(S[f"centred{k}"], 1)

            def variance(k, p):
                dve.wait_ge(S[f"squared{k}"], p + 1)
                i = p % 2 if k == 0 else k - 1
                link(dve.reduce_sum(lnst[:, 0, p, :], SQ[:, i, :].rearrange("r (g d) -> r g d", d=D), AX))
                dve.tensor_scalar(lnst[:, 2, p, :], lnst[:, 0, p, :], 1.0 / D, EPS, ALU.mult, ALU.add)\
                   .then_inc(S[f"variance{k}"], 1)

            dve.wait_ge(S["xbuf_zero"], 16 * E0)
            for p in range(2):
                centre(0, p, pairs(H, p), pairs(XN, p))
            for p in range(2):
                variance(0, p)

            for job in order:
                if job in ring_at:
                    k = ring_at[job]
                    ps = ring_bank[k % 2]
                    dve.wait_ge(S["ring_full"], k + 1)
                if job[0] == "score":
                    _, n, i = job
                    dve.reduce_max(MX[:, n % 2, i:i + 1], ps[0:R, 0:HALF], AX).then_inc(S["ring_free"], 1)
                    if i == 23:
                        dve.wait_ge(S["ring_free"], k + 1)
                        if n >= 2:
                            dve.wait_ge(S["shift_in"], n - 1)
                        dve.reduce_max(M1[:, n % 2, :], MX[:, n % 2, :].rearrange("r (t h) -> r t h", h=2), AX)\
                           .then_inc(S["mx_neg"], 1)
                elif job[0] == "proj":
                    _, b, g, qk, th = job
                    q = nproj[job]
                    dve.wait_ge(S["split1"], q + 1)
                    if q >= 2:
                        dve.wait_ge(S["split3"], q - 1)
                    dve.scalar_tensor_tensor(RR[:, q % 2, :], ps[:, 0:HALF], 0.125 if qk == 0 else 1.0,
                                             SP[:, qk, 0, th * HALF:(th + 1) * HALF], ALU.mult, ALU.subtract)\
                       .then_inc(S["ring_free"], 1)
                elif job[0] == "shift":
                    n = job[1]
                    if n >= 2:
                        dve.wait_ge(S["shift_dma"], 48 * (n - 1))
                    dve.tensor_copy(MT[:, n % 2, 0:R], ps[0:36, 0:63].bitcast(BF16)[:, 0:R]).then_inc(S["ring_free"], 1)
                elif job[0] == "xt":
                    _, which, b, h = job
                    p, a = b % NP, b // NP
                    r = slice(0, 128) if which == 1 else slice(64 * a, 64 * a + 64)
                    dve.tensor_copy(XT[r, p * L + h * HALF:p * L + (h + 1) * HALF], ps[r, 0:HALF])\
                       .then_inc(S["ring_free"], 1)
                elif job[0] == "logits":
                    dve.tensor_tensor(LG, ps[0:R, 0:NJ * E0].rearrange("r (g e) -> r g e", e=E0),
                                      rows(bias[0:R, GB:GB + E0], NJ), ALU.add).then_inc(S["ring_free"], 1)
                    dve.wait_ge(S["ring_free"], k + 1)
                elif job[0] == "choose":
                    link(dve.reduce_max(mx, LG, AX))
                    dve.tensor_tensor(LD, LG, over(mx, NJ, E0), ALU.subtract).then_inc(S["route_ld"], 1)
                    link(dve.tensor_tensor(EQ, LG, over(mx, NJ, E0), ALU.is_equal))
                    link(dve.tensor_tensor(EQ, EQ, rows(iota8, NJ), ALU.mult))
                    link(dve.tensor_reduce(im, EQ, AX, ALU.min))
                    dve.tensor_tensor(OH, rows(iota8, NJ), over(im, NJ, E0), ALU.is_equal).then_inc(S["onehot"], 1)
                elif job[0] == "pos":
                    b = job[1]
                    link(dve.tensor_tensor(PX, ps[0:R, 0:NJ * E0].rearrange("r (g e) -> r g e", e=E0), OH, ALU.mult))
                    dve.sem_inc(S["ring_free"], 1)
                    dve.wait_ge(S["route_ex"], b + 1)
                    dve.reduce_sum(pos, PX, AX)
                    link(dve.reduce_sum(sums, LD, AX))
                    dve.reciprocal(prob[:, NJ * b:NJ * b + NJ], sums).then_inc(S["pos_ready"], 1)
                elif job[0] == "ln_mean":
                    b = job[2]
                    if job[1] == 2:
                        dve.wait_ge(S["att_h"], NJ * (b + 1))
                    dve.reduce_sum(lnb[:, 0, :], H[:, b % NP, :, b // NP, :], AX).then_inc(S["lnb_sum"], 1)
                elif job[0] == "ln_std":
                    dve.wait_ge(S["lnb_x"], ln_at[job[1:3]] + 1)
                    dve.reduce_sum(lnb[:, 2, :], XSQ, AX).then_inc(S["lnb_ssq"], 1)
                elif job[0] == "out":
                    _, b, j, h = job
                    p, a = b % NP, b // NP
                    v = ps[0:R, 0:260].rearrange("r (h c) -> r h c", c=D + 1)
                    link(dve.reciprocal(RD[:, h, :].unsqueeze(2), v[:, :, D:D + 1]))
                    dve.tensor_tensor(OT[:, 4 * h:4 * h + 4, :], v[:, :, 0:D], over(RD[:, h, :], 4, D), ALU.mult)\
                       .then_inc(S["ring_free"], 1)
                    if h == 1:
                        dve.wait_ge(S["ring_free"], k + 1)
                        link(dve.reduce_sum(OR, OT.rearrange("r h d -> r d h"), AX))
                        dve.tensor_tensor(H[:, p, j, a, :], H[:, p, j, a, :], OR, ALU.add).then_inc(S["att_h"], 1)
            dve.wait_ge(S["att_h"], NJ * B)

            def copy_out(name, dst):
                ps, done = filled(dve, name)
                dve.tensor_copy(dst, ps[0:dst.shape[0], 0:dst.shape[1]]).then_inc(done, 1)

            for e in range(4):
                copy_out(("xbt", e, 1), XBT[:, e, 4 * R:8 * R])
            for kind, e in ffn_order:
                if kind == "h1":
                    for a in range(2):
                        for nn in range(2):
                            name = ("h1", e, a, 1, nn)
                            ps, done = filled(dve, name)
                            i = 2 * (e + 4 * a) + 1
                            dve.tensor_scalar(HM[:, e % 2, a, 1, nn * CH:(nn + 1) * CH], ps[:, 0:CH],
                                              W["b1"][:, i:i + 1], 0.0, ALU.add, ALU.max).then_inc(done, 1)
                elif kind == "yb":
                    copy_out(("yb", e, 1), XB[:, e, 4:8, :].rearrange("r c d -> r (c d)"))
            dve.wait_ge(S["big"], 2)

            def routed(p):
                dve.wait_ge(gathered[p], 16 * 12)
                y = pairs(XN, p)
                yf = y.rearrange("r g d -> r (g d)")
                w = pk.rearrange("r (a n j) -> r a n j", a=2, n=NP)[:, :, p, :].rearrange("r a j -> r j a")
                link(dve.tensor_tensor(XN[:, p], XN[:, p], w.unsqueeze(3).to_broadcast([R, NJ, 2, D]), ALU.mult))
                link(dve.tensor_scalar(msk, yf, 3.4028235e38, None, ALU.is_gt))
                link(dve.copy_predicated(yf, mski, big[0:R, 0:1].to_broadcast([R, 768])))
                link(dve.tensor_scalar(msk, yf, -3.4028235e38, None, ALU.is_lt))
                link(dve.copy_predicated(yf, mski, big[0:R, 1:2].to_broadcast([R, 768])))
                link(dve.tensor_tensor(msk, yf, yf, ALU.not_equal))
                link(dve.copy_predicated(yf, mski, zero1[0:R, 0:1].to_broadcast([R, 768])))
                link(dve.tensor_tensor(pairs(H, p), pairs(H, p), y, ALU.add))

            def running_mean(p):
                for h in range(2):
                    emptied(dve, ("xt", 1, p, h))
                cols, own = slice(p * L, (p + 1) * L), slice(p % 2 * L, p % 2 * L + L)
                link(dve.tensor_tensor_scan(CX[:, own], ones[:, 0:1].to_broadcast([128, L]), XT[:, cols], 0.0,
                                            ALU.mult, ALU.add))
                dve.tensor_tensor(CX[:, own], CX[:, own], pos1, ALU.mult).then_inc(S["cx"], 1)

            def hop_hidden(p):
                for th in range(2):
                    ps, done = filled(dve, ("hop", p, th))
                    own = slice(p % 2 * L + th * HALF, p % 2 * L + (th + 1) * HALF)
                    dve.tensor_tensor(HG[:, own], ps[:, 0:HALF], PPF[:, th * HALF:(th + 1) * HALF], ALU.add)\
                       .then_inc(done, 1)

            def tokens_out(p, h):
                for i in range(NJ * p + 3 * h, NJ * p + 3 * h + 3):
                    n = NJ * (p % 3) + i - NJ * p
                    ps, done = filled(dve, ("tok", i))
                    dve.tensor_tensor(CV[:, n].rearrange("r a c d -> r (a c d)"), ps[0:R, 0:256],
                                      bias[0:R, CVB:CVB + 256], ALU.add)
                    dve.tensor_tensor(TK[:, n].rearrange("r k a p -> r (k a p)"), ps[0:R, 256:384],
                                      bias[0:R, KSB:KSB + 128], ALU.add)
                    dve.tensor_tensor(GA[:, 1, 2 * i:2 * i + 2], ps[0:R, 384:386], bias[0:R, GTB:GTB + 2], ALU.add)\
                       .then_inc(done, 1)
                    ps, done = filled(dve, ("ao", i))
                    v = ps[0:R, 0:264].rearrange("r (g c) -> r g c", c=PP + 1)
                    bv = bias[0:R, AOB:AOB + 264].rearrange("r (g c) -> r g c", c=PP + 1)
                    dve.tensor_tensor(TC[:, 2 * n:2 * n + 2].rearrange("r g h p -> r (g h) p"), v[:, :, 0:PP],
                                      bv[:, :, 0:PP], ALU.add)
                    dve.tensor_tensor(WS[:, 8 * i:8 * i + 8].unsqueeze(2), v[:, :, PP:], bv[:, :, PP:], ALU.add)\
                       .then_inc(done, 1)

            def widths(p):
                if p == 0:
                    link(dve.tensor_tensor(hdl, bias[0:R, WD:WD + WN], bias[0:R, WD:WD + WN], ALU.mult))
                    link(dve.tensor_scalar(hdl, hdl, -0.5, None, ALU.mult))
                w = WS[:, 48 * p:48 * p + 48]
                dve.wait_ge(S["width"], p + 1)
                link(dve.tensor_scalar(w, w, 2.0, 0.1, ALU.mult, ALU.add))
                link(dve.tensor_tensor(w, w, w, ALU.mult))
                link(dve.tensor_scalar(w, w, 1e-6, None, ALU.add))
                link(dve.reciprocal(w, w))
                dve.tensor_tensor(WE, over(w, 48, WN), rows(hdl, 48), ALU.mult).then_inc(S["warg"], 1)

            def weights(p):
                wa = [WA[:, i, 48 * p:48 * p + 48] for i in range(3)]
                dve.wait_ge(S["wexp"], p + 1)
                for i in range(2):
                    link(dve.tensor_tensor(WX, WE, rows(trig[:, i, NJ * PP:], 48), ALU.mult))
                    link(dve.reduce_sum(wa[i], WX, AX))
                link(dve.reduce_sum(wa[2], WE, AX))
                link(dve.tensor_scalar(wa[2], wa[2], 1e-6, None, ALU.add))
                link(dve.reciprocal(wa[2], wa[2]))
                link(dve.tensor_scalar(wa[2], wa[2], RS / PH, None, ALU.mult))
                dve.tensor_tensor(wa[0], wa[0], wa[2], ALU.mult)
                dve.tensor_tensor(wa[1], wa[1], wa[2], ALU.mult).then_inc(S["wab"], 1)
                ps, done = filled(dve, ("gcum", p))
                ps2, done2 = filled(dve, ("gtot", p))
                g = slice(2 * NJ * p, 2 * NJ * (p + 1))
                dve.tensor_copy(GA[:, 2, g], ps2[0:R, 0:2 * NJ]).then_inc(done2, 1)
                emptied(dve, ("gtot", p))
                tot, run = (GA[:, i, g].rearrange("r (j a) -> r a j", a=2) for i in (2, 3))
                for a in range(2):
                    last = dve.tensor_tensor_scan(run[:, a], ones[0:R, 0:NJ], tot[:, a], 0.0, ALU.mult, ALU.add)
                link(last)
                link(dve.tensor_tensor(GA[:, 3, g], GA[:, 3, g], GA[:, 2, g], ALU.subtract))
                dve.tensor_tensor(GA[:, 4, g], ps[0:R, 0:2 * NJ], GA[:, 3, g], ALU.add).then_inc(done, 1)
                emptied(dve, ("gcum", p))
                dve.tensor_scalar(GA[:, 4, g], GA[:, 4, g], 1.0, None, ALU.max).then_inc(S["gc"], 1)

            def chunk(q):
                p, c = divmod(q, 3)
                g = slice(2 * NJ * (p % 3) + 4 * c, 2 * NJ * (p % 3) + 4 * c + 4)
                dve.wait_ge(S["cosines"], 2 * (p + 1))
                cc, sc = (x[:, g].rearrange("r g h p -> r (g h) p") for x in (TC, SC))
                wa, wb = (over(WA[:, i, 16 * q:16 * q + 16], 16, PP) for i in range(2))
                p0, p1 = (PT[:, i].rearrange("r g h p -> r (g h) p") for i in (0, 1))
                dve.tensor_tensor(p0, cc, wa, ALU.mult)
                dve.tensor_tensor(p1, sc, wb, ALU.mult).then_inc(S["prod"], 1)
                dve.wait_ge(S["prod"], q + 1)
                link(dve.tensor_tensor(p0, p0, p1, ALU.subtract))
                dve.reduce_sum(UV[:, 0], PT[:, 0].rearrange("r g h p -> r g p h"), AX)
                dve.wait_ge(S["vsum"], q + 1)
                dve.reduce_sum(UV[:, 1], PT[:, 2].rearrange("r g h p -> r g p h"), AX).then_inc(S["uv"], 1)
                dve.wait_ge(S["uv"], q + 1)
                u, w = (UV[:, i].rearrange("r (j a) p -> r j a p", a=2) for i in (0, 1))
                t0, t1 = (UT[:, i].rearrange("r (j a) p -> r j a p", a=2) for i in (0, 1))
                j = 2 * (q % 3)
                cp, sp_ = (trig[:, i, j * PP:(j + 2) * PP].rearrange("r (j p) -> r j p", p=PP).unsqueeze(2)
                           .to_broadcast([R, 2, 2, PP]) for i in (0, 1))
                qc, qs = (QQ[:, g, 32 * i:32 * i + 32].rearrange("r (j a) p -> r j a p", a=2) for i in (0, 1))
                dve.tensor_tensor(t0, u, cp, ALU.mult)
                link(dve.tensor_tensor(t1, w, sp_, ALU.mult))
                link(dve.tensor_tensor(qc, t0, t1, ALU.subtract))
                dve.tensor_tensor(t0, u, sp_, ALU.mult)
                link(dve.tensor_tensor(t1, w, cp, ALU.mult))
                dve.tensor_tensor(qs, t0, t1, ALU.add).then_inc(S["qf_ready"], 1)

            mask = triu[0:R, 0:R].unsqueeze(1).to_broadcast([R, 2, R])

            def masked(x):
                p, j = divmod(x, NJ)
                for k2 in range(2):
                    ps, done = filled(dve, ("sm", x, k2))
                    if x >= 4 and k2 == 0:
                        k = jobs[("ret", x - 4)]
                        dve.wait_ge(full[k % 8], k // 8 + 1)
                    dve.tensor_tensor(SM[:, x % 4, k2], ps[0:R, 0:2 * R].rearrange("r (a c) -> r a c", a=2), mask,
                                      ALU.mult).then_inc(done, 1)
                if j < NJ - 1:
                    ps, done = filled(dve, ("state", x))
                    for c in range(2):
                        r = slice(64 * c, 64 * c + 64)
                        delta = ps[r, 0:256].rearrange("r (a c d) -> r a c d", a=2, c=2)[:, :, c, :]
                        if j == 0:
                            ins = dve.tensor_copy(ST[r, p % 2, 1], delta)
                        else:
                            ins = dve.tensor_tensor(ST[r, p % 2, j + 1], ST[r, p % 2, j], delta, ALU.add)
                        ins.then_inc(S["state"], 1)
                    dve.wait_ge(S["state"], 2 * (p * (NJ - 1) + j + 1))
                    dve.sem_inc(done, 1)

            for event in events:
                kind, x = event[0:2]
                if kind == "gathered":
                    routed(x)
                elif kind == "mean":
                    if x == 0:
                        dve.wait_ge(S["pos"], 1)
                        link(dve.reciprocal(pos1, pos1))
                    running_mean(x)
                elif kind == "hidden":
                    hop_hidden(x)
                elif kind == "tokens":
                    tokens_out(x, event[2])
                elif kind == "widths":
                    widths(x)
                elif kind == "weights":
                    weights(x)
                elif kind == "chunk":
                    chunk(x)
                elif kind == "masked":
                    masked(x)
                elif kind == "product":
                    p = event[2]
                    for h in range(2):
                        ps, done = filled(dve, ("product", p, h))
                        dve.wait_ge(S["h_pre"], p + 1)
                        v = H[:, p, 3 * h:3 * h + 3].rearrange("r j a d -> r (j a d)")
                        dve.tensor_tensor(v, v, ps[0:R, 0:3 * 128], ALU.add).then_inc(done, 1)
                elif kind == "centre":
                    p = event[2]
                    for i in range(NJ if x == 2 else 0):
                        emptied(dve, ("ret", NJ * p + i))
                    for h in range(2 if x == 3 else 0):
                        emptied(dve, ("product", p, h))
                    centre(x, p, pairs(XN if x == 2 else H, p), pairs(XN, p))
                elif kind == "variance":
                    variance(x, event[2])

            ps, done = filled(dve, "logits1")
            link(dve.tensor_tensor(GL, ps[0:R, 0:NG * E1].rearrange("r (g e) -> r g e", e=E1),
                                   rows(bias[0:R, RB2:RB2 + E1], NG), ALU.add))
            dve.sem_inc(done, 1)
            m1, i1, d2, x2, ww, w1_, m2, t2 = (g1[:, i, :] for i in range(8))
            i6 = rows(iota8[:, 0:E1], NG)
            link(dve.reduce_max(m1, GL, AX))
            dve.tensor_tensor(GE, GL, over(m1, NG, E1), ALU.subtract).then_inc(S["route1"], 1)
            link(dve.tensor_tensor(GC, GL, over(m1, NG, E1), ALU.is_equal))
            link(dve.tensor_tensor(GC, GC, i6, ALU.mult))
            link(dve.tensor_reduce(i1, GC, AX, ALU.min))
            link(dve.tensor_tensor(GO, i6, over(i1, NG, E1), ALU.is_equal))
            link(dve.scalar_tensor_tensor(GC, GO, -3.0e38, GL, ALU.mult, ALU.add))
            link(dve.reduce_max(m2, GC, AX))
            dve.tensor_tensor(d2, m2, m1, ALU.subtract).then_inc(S["route1"], 1)
            link(dve.tensor_tensor(GC, GC, over(m2, NG, E1), ALU.is_equal))
            link(dve.tensor_tensor(GC, GC, i6, ALU.mult))
            link(dve.tensor_reduce(i1, GC, AX, ALU.min))
            link(dve.tensor_tensor(GW, i6, over(i1, NG, E1), ALU.is_equal))
            dve.wait_ge(S["route1_ex"], 2)
            link(dve.reduce_sum(t2, GE, AX))
            link(dve.reciprocal(t2, t2))
            link(dve.tensor_scalar(x2, x2, 1.0, None, ALU.subtract))
            dve.tensor_tensor(ww, x2, t2, ALU.mult).then_inc(S["route1"], 1)
            dve.wait_ge(S["route1_ex"], 3)
            link(dve.tensor_scalar(t2, w1_, 1.0, None, ALU.add))
            link(dve.reciprocal(t2, t2))
            link(dve.tensor_tensor(w1_, w1_, t2, ALU.mult))
            dve.tensor_tensor(GO, GO, over(t2, NG, E1), ALU.mult)
            link(dve.tensor_tensor(GW, GW, over(w1_, NG, E1), ALU.mult))
            link(dve.tensor_tensor(GW, GW, GO, ALU.add))
            x = 0
            for a in range(2):
                for p in range(NP):
                    for j in range(NJ):
                        ps, done = filled(dve, ("l3", a, p, j))
                        k = jobs[("l3", a, p, j)]
                        yo = YO[:, x % 2]
                        dve.tensor_tensor(yo, ps[0:R, 0:384].rearrange("r (e d) -> r e d", e=E1),
                                          bias[0:R, EB3:EB3 + 384].rearrange("r (e d) -> r e d", e=E1), ALU.add)\
                           .then_inc(done, 1)
                        dve.wait_ge(free[k % 8], k // 8 + 1)
                        g = (p * NJ + j) * 2 + a
                        link(dve.tensor_tensor(yo, yo, over(GW[:, g, :], E1, D), ALU.mult))
                        link(dve.reduce_sum(YR[:, x % 2, :], yo.rearrange("r e d -> r d e"), AX))
                        dve.tensor_tensor(H[:, p, j, a, :], H[:, p, j, a, :], YR[:, x % 2, :], ALU.add)\
                           .then_inc(S["h4"], 1)
                        x += 1


_INS = ['x', 'L0_tok_conv_w', 'L0_tok_conv_b', 'L0_tok_bn_gamma', 'L0_tok_bn_beta', 'L0_tok_bn_mean',
        'L0_tok_bn_var', 'L0_tok_out_w', 'L0_tok_out_b', 'L0_attn_Q', 'L0_attn_K', 'L0_attn_VO',
        'L0_ffn_gate_w', 'L0_ffn_gate_b', 'L0_ffn_w1', 'L0_ffn_b1', 'L0_ffn_w2', 'L0_ffn_b2',
        'L1_attn_pos_phases', 'L1_attn_window_deltas', 'L1_attn_mc_w', 'L1_attn_mc_b', 'L1_attn_hop_w1',
        'L1_attn_hop_b1', 'L1_attn_hop_w2', 'L1_attn_hop_b2', 'L1_attn_cpe_w', 'L1_attn_cpe_b', 'L1_attn_ve_w',
        'L1_attn_ve_b', 'L1_attn_kce_w', 'L1_attn_kce_b', 'L1_attn_ksk_w1', 'L1_attn_ksk_b1', 'L1_attn_ksk_w2',
        'L1_attn_ksk_b2', 'L1_attn_sg_w1', 'L1_attn_sg_b1', 'L1_attn_sg_w2', 'L1_attn_sg_b2', 'L1_attn_ln_g',
        'L1_attn_ln_b', 'L1_attn_out_w', 'L1_attn_out_b', 'L1_ffn_router_w1', 'L1_ffn_router_b1',
        'L1_ffn_router_w2', 'L1_ffn_router_b2', 'L1_ffn_expert_w1', 'L1_ffn_expert_b1', 'L1_ffn_expert_w2',
        'L1_ffn_expert_b2', 'L1_ffn_expert_w3', 'L1_ffn_expert_b3']


def kernel(**inputs):
    import concourse.bacc as bacc
    from concourse.bass_utils import run_bass_kernel_spmd

    nc = bacc.Bacc("TRN2", target_bir_lowering=False, num_devices=1)
    arrays, args = {}, {}
    for name in _INS:
        a = np.ascontiguousarray(inputs[name])
        arrays[f"in_{name}"] = a
        args[name] = nc.dram_tensor(f"in_{name}", a.shape, mybir.dt.from_np(a.dtype), kind="ExternalInput").ap()
    out = nc.dram_tensor("out_0", (B, L, D), F32, kind="ExternalOutput").ap()
    build(nc, args, out)
    r = run_bass_kernel_spmd(nc, [arrays], core_ids=[0])
    return r.results[0]["out_0"]
```
